# Optimizing a Trainium2 kernel written in Bass

```python
import numpy as np
import jax
import jax.numpy as jnp

def _softmax(x, axis=-1):
    return jax.nn.softmax(x, axis=axis)

def _gelu(x):
    return jax.nn.gelu(x, approximate=True)

def _silu(x):
    return jax.nn.silu(x)

def _sigmoid(x):
    return jax.nn.sigmoid(x)

def _layernorm(x, axis=-1, eps=1e-05):
    m = jnp.mean(x, axis=axis, keepdims=True)
    v = jnp.var(x, axis=axis, keepdims=True)
    return (x - m) / jnp.sqrt(v + eps)

def _scatter_add(tgt, idx, src, axis=0):
    return tgt.at[idx].add(src)

def _segment_sum(src, seg, n):
    return jax.ops.segment_sum(src, seg, n)
kernel_name = 'mk_adj_preln_d4_adj_r2_b0f031'

def setup_inputs(seed: int=0):
    np.random.seed(seed)
    _w = jnp.asarray

    def _rec_inputs():
        import jax
        import jax.numpy as jnp
        _gk = jax.random.key(seed)
        x = -0.0002928 + 1 * jax.random.normal(jax.random.fold_in(_gk, 1), (2048, 512), jnp.float32)
        _a = jax.random.bernoulli(jax.random.fold_in(_gk, 2), 0.00195312, (2048, 2048))
        _a = jnp.logical_or(_a, jnp.swapaxes(_a, -1, -2))
        _a = jnp.logical_or(_a, jnp.eye(2048, dtype=bool))
        _af = _a.astype(jnp.float32)
        adj = _af
        return (x, adj)
    x, adj = _rec_inputs()

    def _L0_gnn_setup():
        import jax, jax.numpy as jnp
        import numpy as np
        ALPHA = 0.2
        NEG = -9000000000000000.0
        N, NFEAT, NHID, NHEADS = (2048, 512, 64, 8)
        EMB = NHID * NHEADS
        key = jax.random.key(seed)
        ks = jax.random.split(key, 16)
        x = jax.random.normal(ks[0], (N, NFEAT), dtype=jnp.float32)
        adj = (jax.random.uniform(ks[1], (N, N)) < 0.01).astype(jnp.float32)
        adj = jnp.maximum(adj, jnp.eye(N, dtype=jnp.float32))
        s = 0.05
        W = jax.random.normal(ks[2], (NHEADS, NFEAT, NHID), dtype=jnp.float32) * s
        a1 = jax.random.normal(ks[3], (NHEADS, NHID), dtype=jnp.float32) * s
        a2 = jax.random.normal(ks[4], (NHEADS, NHID), dtype=jnp.float32) * s
        W1 = jax.random.normal(ks[5], (EMB // 2, EMB), dtype=jnp.float32) * s
        b1 = jnp.zeros((EMB // 2,), dtype=jnp.float32)
        W2 = jax.random.normal(ks[6], (NFEAT // 4, EMB // 2), dtype=jnp.float32) * s
        b2 = jnp.zeros((NFEAT // 4,), dtype=jnp.float32)
        W3 = jax.random.normal(ks[7], (NFEAT // 2, NFEAT // 4), dtype=jnp.float32) * s
        b3 = jnp.zeros((NFEAT // 2,), dtype=jnp.float32)
        W4 = jax.random.normal(ks[8], (NFEAT, NFEAT // 2), dtype=jnp.float32) * s
        b4 = jnp.zeros((NFEAT,), dtype=jnp.float32)
        return {'x': x, 'adj': adj, 'W': W, 'a1': a1, 'a2': a2, 'W1': W1, 'b1': b1, 'W2': W2, 'b2': b2, 'W3': W3, 'b3': b3, 'W4': W4, 'b4': b4}
    _L0_gnn_all = _L0_gnn_setup()
    _L0_gnn_in = {k: v for k, v in _L0_gnn_all.items() if k in ('W', 'a1', 'a2', 'W1', 'b1', 'W2', 'b2', 'W3', 'b3', 'W4', 'b4')}
    del _L0_gnn_all

    def _L1_gnn_setup():
        import jax, jax.numpy as jnp
        import numpy as np
        D_IN, D_ATTN, STEPS = (512, 64, 2)
        P_TOP, TAU, LN_EPS = (0.9, 1.0, 1e-05)
        N = 2048

        def _xavier(key, shape):
            fan_in, fan_out = (shape[0], shape[1])
            lim = jnp.sqrt(6.0 / (fan_in + fan_out))
            return jax.random.uniform(key, shape, jnp.float32, -lim, lim)

        def _adj_from_feats(Xa, W1, W2, W3):
            Q = Xa @ W1
            K = Xa @ W3
            logits = Q @ W2 @ K.T / TAU
            n = logits.shape[1]
            order = jnp.argsort(-logits, axis=1)
            vals = jnp.take_along_axis(logits, order, axis=1)
            probs = jax.nn.softmax(vals, axis=1)
            csum = jnp.cumsum(probs, axis=1)
            k_i = jnp.sum(csum < P_TOP, axis=1) + 1
            keep = jnp.arange(n)[None, :] < k_i[:, None]
            masked_sorted = jnp.where(keep, vals, -jnp.inf)
            rows = jnp.arange(n)[:, None]
            masked = jnp.full_like(logits, -jnp.inf).at[rows, order].set(masked_sorted)
            return jax.nn.softmax(masked, axis=1)
        key = jax.random.key(seed)
        ks = jax.random.split(key, 12)
        X = jax.random.normal(ks[0], (N, D_IN), jnp.float32)
        S = jax.random.uniform(ks[1], (N, N), jnp.float32)
        W1 = _xavier(ks[2], (D_IN, D_ATTN))
        W3 = _xavier(ks[3], (D_IN, D_ATTN))
        W2 = _xavier(ks[4], (D_ATTN, D_ATTN))
        U1_0 = _xavier(ks[5], (D_IN, D_IN))
        U1_1 = _xavier(ks[6], (D_IN, D_IN))
        U2_0 = _xavier(ks[7], (D_IN, D_IN))
        U2_1 = _xavier(ks[8], (D_IN, D_IN))
        gamma = jnp.ones((D_IN,), jnp.float32)
        beta = jnp.zeros((D_IN,), jnp.float32)
        return {'X': X, 'S': S, 'W1': W1, 'W2': W2, 'W3': W3, 'U1_0': U1_0, 'U1_1': U1_1, 'U2_0': U2_0, 'U2_1': U2_1, 'gamma': gamma, 'beta': beta}
    _L1_gnn_all = _L1_gnn_setup()
    _L1_gnn_in = {k: v for k, v in _L1_gnn_all.items() if k in ('W1', 'W2', 'W3', 'U1_0', 'U1_1', 'U2_0', 'U2_1', 'gamma', 'beta')}
    del _L1_gnn_all

    def _L2_gnn_setup():
        import jax, jax.numpy as jnp
        import numpy as np
        N = 4096
        D = 512

        def adjacent_mat(adj):
            adj = adj + jnp.eye(adj.shape[0], dtype=adj.dtype)
            deg = jnp.sum(adj, axis=1)
            dinv = jnp.where(deg > 0, deg ** (-0.5), 0.0).astype(adj.dtype)
            return dinv[:, None] * adj * dinv[None, :]
        key = jax.random.key(seed)
        k1, k2 = jax.random.split(key)
        x = jax.random.normal(k1, (N, D), dtype=jnp.float32)
        Coefficient2 = 1e-08 * jnp.ones((N, N), dtype=jnp.float32)
        A = jax.random.uniform(k2, (N, N), dtype=jnp.float32)
        return {'x': x, 'Coefficient2': Coefficient2, 'A': A}
    _L2_gnn_all = _L2_gnn_setup()
    _L2_gnn_in = {k: v for k, v in _L2_gnn_all.items() if k in ()}
    del _L2_gnn_all

    def _L3_gnn_setup():
        import jax, jax.numpy as jnp
        import numpy as np
        N = 4096
        IN_FEATURES = 512
        OUT_FEATURES = 512
        key = jax.random.key(seed)
        k_x, k_adj, k_w, k_b = jax.random.split(key, 4)
        x = jax.random.normal(k_x, (N, IN_FEATURES), dtype=jnp.float32)
        adj = jax.random.uniform(k_adj, (N, N), dtype=jnp.float32)
        stdv = 1.0 / np.sqrt(OUT_FEATURES)
        weight = jax.random.uniform(k_w, (IN_FEATURES, OUT_FEATURES), dtype=jnp.float32, minval=-stdv, maxval=stdv)
        bias = jax.random.uniform(k_b, (OUT_FEATURES,), dtype=jnp.float32, minval=-stdv, maxval=stdv)
        return {'x': x, 'adj': adj, 'weight': weight, 'bias': bias}
    _L3_gnn_all = _L3_gnn_setup()
    _L3_gnn_in = {k: v for k, v in _L3_gnn_all.items() if k in ('weight', 'bias')}
    del _L3_gnn_all
    return {'x': x, 'adj': adj, 'L0_gnn_W': _L0_gnn_in['W'], 'L0_gnn_a1': _L0_gnn_in['a1'], 'L0_gnn_a2': _L0_gnn_in['a2'], 'L0_gnn_W1': _L0_gnn_in['W1'], 'L0_gnn_b1': _L0_gnn_in['b1'], 'L0_gnn_W2': _L0_gnn_in['W2'], 'L0_gnn_b2': _L0_gnn_in['b2'], 'L0_gnn_W3': _L0_gnn_in['W3'], 'L0_gnn_b3': _L0_gnn_in['b3'], 'L0_gnn_W4': _L0_gnn_in['W4'], 'L0_gnn_b4': _L0_gnn_in['b4'], 'L1_gnn_W1': _L1_gnn_in['W1'], 'L1_gnn_W2': _L1_gnn_in['W2'], 'L1_gnn_W3': _L1_gnn_in['W3'], 'L1_gnn_U1_0': _L1_gnn_in['U1_0'], 'L1_gnn_U1_1': _L1_gnn_in['U1_1'], 'L1_gnn_U2_0': _L1_gnn_in['U2_0'], 'L1_gnn_U2_1': _L1_gnn_in['U2_1'], 'L1_gnn_gamma': _L1_gnn_in['gamma'], 'L1_gnn_beta': _L1_gnn_in['beta'], 'L3_gnn_weight': _L3_gnn_in['weight'], 'L3_gnn_bias': _L3_gnn_in['bias']}

def reference(x, adj, L0_gnn_W, L0_gnn_a1, L0_gnn_a2, L0_gnn_W1, L0_gnn_b1, L0_gnn_W2, L0_gnn_b2, L0_gnn_W3, L0_gnn_b3, L0_gnn_W4, L0_gnn_b4, L1_gnn_W1, L1_gnn_W2, L1_gnn_W3, L1_gnn_U1_0, L1_gnn_U1_1, L1_gnn_U2_0, L1_gnn_U2_1, L1_gnn_gamma, L1_gnn_beta, L3_gnn_weight, L3_gnn_bias):
    import jax
    import jax.numpy as jnp

    def _L0_gnn_ref(x, adj, W, a1, a2, W1, b1, W2, b2, W3, b3, W4, b4):
        import jax, jax.numpy as jnp
        import numpy as np
        ALPHA = 0.2
        NEG = -9000000000000000.0
        N, NFEAT, NHID, NHEADS = (2048, 512, 64, 8)
        EMB = NHID * NHEADS
        Wh = jnp.einsum('nf,hfd->hnd', x, W)
        e_src = jnp.einsum('hnd,hd->hn', Wh, a1)
        e_dst = jnp.einsum('hnd,hd->hn', Wh, a2)
        e = jax.nn.leaky_relu(e_src[:, :, None] + e_dst[:, None, :], ALPHA)
        e = jnp.where(adj[None] > 0, e, NEG)
        att = jax.nn.softmax(e, axis=-1)
        h = jnp.einsum('hnm,hmd->hnd', att, Wh)
        h = jax.nn.elu(h)
        enc = jnp.transpose(h, (1, 0, 2)).reshape(x.shape[0], -1)
        out = jax.nn.relu(enc @ W1.T + b1)
        out = jax.nn.relu(out @ W2.T + b2)
        out = jax.nn.relu(out @ W3.T + b3)
        out = out @ W4.T + b4
        return out

    def _L1_gnn_ref(X, S, W1, W2, W3, U1_0, U1_1, U2_0, U2_1, gamma, beta):
        import jax, jax.numpy as jnp
        import numpy as np
        D_IN, D_ATTN, STEPS = (512, 64, 2)
        P_TOP, TAU, LN_EPS = (0.9, 1.0, 1e-05)
        N = 2048

        def _xavier(key, shape):
            fan_in, fan_out = (shape[0], shape[1])
            lim = jnp.sqrt(6.0 / (fan_in + fan_out))
            return jax.random.uniform(key, shape, jnp.float32, -lim, lim)

        def _adj_from_feats(Xa, W1, W2, W3):
            Q = Xa @ W1
            K = Xa @ W3
            logits = Q @ W2 @ K.T / TAU
            n = logits.shape[1]
            order = jnp.argsort(-logits, axis=1)
            vals = jnp.take_along_axis(logits, order, axis=1)
            probs = jax.nn.softmax(vals, axis=1)
            csum = jnp.cumsum(probs, axis=1)
            k_i = jnp.sum(csum < P_TOP, axis=1) + 1
            keep = jnp.arange(n)[None, :] < k_i[:, None]
            masked_sorted = jnp.where(keep, vals, -jnp.inf)
            rows = jnp.arange(n)[:, None]
            masked = jnp.full_like(logits, -jnp.inf).at[rows, order].set(masked_sorted)
            return jax.nn.softmax(masked, axis=1)
        n = X.shape[0]
        S = S + jnp.eye(n, dtype=X.dtype)
        R = S / jnp.clip(S.sum(axis=1, keepdims=True), 1e-12)
        Z = jnp.zeros_like(X)
        Xf, Xa = (X, X)
        U1s, U2s = ((U1_0, U1_1), (U2_0, U2_1))
        for s in range(STEPS):
            A = _adj_from_feats(Xa, W1, W2, W3)
            Xf = R @ Xf
            Xa = A @ Xa
            Z = Z + (Xf @ U1s[s] + Xa @ U2s[s])
        Y = X + Z
        mu = Y.mean(axis=-1, keepdims=True)
        var = Y.var(axis=-1, keepdims=True)
        return (Y - mu) * jax.lax.rsqrt(var + LN_EPS) * gamma + beta

    def _L2_gnn_ref(x, Coefficient2, A):
        import jax, jax.numpy as jnp
        import numpy as np
        N = 4096
        D = 512

        def adjacent_mat(adj):
            adj = adj + jnp.eye(adj.shape[0], dtype=adj.dtype)
            deg = jnp.sum(adj, axis=1)
            dinv = jnp.where(deg > 0, deg ** (-0.5), 0.0).astype(adj.dtype)
            return dinv[:, None] * adj * dinv[None, :]
        A_c = jax.lax.stop_gradient(A)
        adj = adjacent_mat((A_c + A_c.T) * 0.5)
        y = Coefficient2 @ adj
        y = y @ x
        return y

    def _L3_gnn_ref(x, adj, weight, bias):
        import jax, jax.numpy as jnp
        import numpy as np
        N = 4096
        IN_FEATURES = 512
        OUT_FEATURES = 512
        support = jnp.matmul(x, weight)
        output = jnp.matmul(adj, support)
        return output + bias
    h = jnp.maximum(_layernorm(x, axis=-1), 0.0)
    x = x + _L0_gnn_ref(h, adj, L0_gnn_W, L0_gnn_a1, L0_gnn_a2, L0_gnn_W1, L0_gnn_b1, L0_gnn_W2, L0_gnn_b2, L0_gnn_W3, L0_gnn_b3, L0_gnn_W4, L0_gnn_b4)
    h = jnp.maximum(_layernorm(x, axis=-1), 0.0)
    x = x + _L1_gnn_ref(h, adj, L1_gnn_W1, L1_gnn_W2, L1_gnn_W3, L1_gnn_U1_0, L1_gnn_U1_1, L1_gnn_U2_0, L1_gnn_U2_1, L1_gnn_gamma, L1_gnn_beta)
    h = jnp.maximum(_layernorm(x, axis=-1), 0.0)
    x = x + _L2_gnn_ref(h, adj, adj)
    h = jnp.maximum(_layernorm(x, axis=-1), 0.0)
    x = x + _L3_gnn_ref(h, adj, L3_gnn_weight, L3_gnn_bias)
    return x

_drawn_inputs = setup_inputs


def setup_inputs(seed=0):
    import zlib

    import numpy as np

    out = dict(_drawn_inputs(seed))
    spreads = {'L0_gnn_b1': (0.0, 0.348),
     'L0_gnn_b2': (0.0, 0.1),
     'L0_gnn_b3': (0.0, 0.1),
     'L0_gnn_b4': (0.0, 0.1),
     'L1_gnn_gamma': (1.0, 0.2),
     'L1_gnn_beta': (0.0, 0.1)}
    factors = {'L0_gnn_a1': 8.0, 'L0_gnn_a2': 8.0, 'L3_gnn_bias': 8.0}
    for name, (base, spread) in spreads.items():
        noise = np.random.default_rng([zlib.crc32(name.encode()), seed]).standard_normal(out[name].shape)
        drawn = base * np.exp(spread * noise) if base else spread * noise
        out[name] = jnp.asarray(drawn.astype(out[name].dtype))
    for name, factor in factors.items():
        out[name] = (out[name] * factor).astype(out[name].dtype)
    return out
```

```python
import math
from contextlib import ExitStack

import numpy as np

import concourse.bass as bass
from concourse import mybir

F32 = mybir.dt.float32
F16 = mybir.dt.float16
BF16 = mybir.dt.bfloat16
ALU = mybir.AluOpType
ACT = mybir.ActivationFunctionType
AXIS = mybir.AxisListType

P = 128
N = 2048
NT = N // P
D = 512
KT = D // P
H, HD = 8, 64
BANK = 512
HALF = N // 2
SLOPE = 0.2
LN_EPS = 1e-5
EXP_CAP = 80.0
P_TOP = 0.9
SEARCH = math.log(N / (1.0 - P_TOP)) + 0.05
STEPS = 22
KB = 1024
ARENA = 200 * KB


class Chain:

    def __init__(self, eng, sem, base=0):
        self.eng, self.sem, self.base, self.n = eng, sem, base, 0

    def link(self, ins):
        self.count(ins)
        self.wait()

    def count(self, ins):
        self.n += 1
        ins.then_inc(self.sem, 1)

    def wait(self):
        self.eng.wait_ge(self.sem, self.base + self.n)


class Memory:

    def __init__(self, nc, ctx):
        self.nc, self.ctx = nc, ctx
        self.arena = ctx.enter_context(nc.sbuf_tensor("arena", [P, ARENA // 4], F32))
        self.psum = ctx.enter_context(nc.psum_tensor("banks", [P, 8, BANK], F32))
        self.eye = self.small("eye", [P, P], F32)
        self.eye16 = self.small("eye16", [P, P], F16)
        self.minus_half = self.small("minus_half", [P, 1], F32)
        self.ones = self.small("ones", [P, 32], F32)
        self.ones16 = self.small("ones16", [P, 1], F16)
        self.stats = self.small("stats", [P, NT, 6], F32)
        self.norm = self.small("norm", [P, 6, NT], F32)
        self.inv_degree = self.small("inv_degree", [P, NT], F32)
        self.inv_sqrt_degree = self.small("inv_sqrt_degree", [P, NT], F32)
        self.qk_weight = self.small("qk_weight", [P, KT, P], F32)
        self.scratch = self.small("scratch", [P, 4 * KB // 4], F32)
        self.own_feats = shaped(self.scratch[:, 0:512], (2, 256))
        self.pick = shaped(self.scratch[:, 512:768], (2, P))
        self.dst_part = shaped(self.scratch[:, 768:896], (NT, H))
        self.dst_floor = shaped(self.scratch[:, 896:1024], (NT, H))
        self.adj_t = self.f16(0, NT, N)

    def small(self, name, shape, dt):
        return self.ctx.enter_context(self.nc.sbuf_tensor(name, shape, dt))

    def f32(self, kb, *shape, parts=P):
        start, size = int(kb * KB) // 4, int(np.prod(shape))
        assert kb * KB + size * 4 <= ARENA
        view = self.arena[0:parts, start:start + size]
        return shaped(view, shape)

    def f16(self, kb, *shape, dt=F16):
        start, size = kb * KB // 4, int(np.prod(shape)) // 2
        assert kb * KB + size * 4 <= ARENA
        return shaped(self.arena[:, start:start + size].bitcast(dt), shape)

    def bank(self, b, count=1):
        return self.psum[:, b:b + count, :].rearrange("p b n -> p (b n)")


def shaped(view, shape):
    if len(shape) == 2:
        return view.rearrange("p (a b) -> p a b", a=shape[0])
    if len(shape) == 3:
        return view.rearrange("p (a b c) -> p a b c", a=shape[0], b=shape[1])
    return view


def columns(dram):
    return dram.rearrange("(k p) -> p k", p=P)


def rows(dram):
    return dram.rearrange("(t p) f -> p t f", p=P)


def on_all(dram):
    return dram.partition_broadcast(P)


def wait(eng, sem, value):
    if not isinstance(value, int) or value > 0:
        eng.wait_ge(sem, value)


def column(table, t):
    return table[:, bass.ds(t, 1)]


def repeat(eng, count, body):
    body(0)
    with eng.Fori(1, count) as i:
        body(i)


def walk(eng, body, lanes):
    groups = NT // lanes
    for lane in range(lanes):
        body(lane, lane, 0)
    with eng.Fori(1, groups - 1) as g:
        for lane in range(lanes):
            body(g * lanes + lane, lane, g)
    for lane in range(lanes):
        body(NT - lanes + lane, lane, groups - 1)


def row_constants(dve, chain, stats, norm):
    sq, diff, var, mean2 = (norm[:, k, :] for k in range(4))
    half = [stats[:, :, k] for k in range(6)]
    dve.tensor_tensor(sq, half[2], half[5], ALU.add)
    chain.link(dve.tensor_tensor(diff, half[1], half[4], ALU.subtract))
    chain.link(dve.scalar_tensor_tensor(mean2, diff, 0.25, diff, ALU.mult, ALU.mult))
    chain.link(dve.scalar_tensor_tensor(var, sq, 1.0 / D, mean2, ALU.mult, ALU.add))
    chain.link(dve.tensor_scalar(var, var, LN_EPS, None, ALU.add))
    chain.link(dve.tensor_tensor(mean2, half[1], half[4], ALU.add))


def constants(nc, m):
    with ExitStack() as ctx:
        zeroed = ctx.enter_context(nc.semaphore("zeroed"))
        made = ctx.enter_context(nc.semaphore("made"))
        block = ctx.enter_context(nc.Block())

        @block.gpsimd
        def _(pool):
            for eye in (m.eye, m.eye16):
                pool.memset(eye[:, :], 0.0).then_inc(zeroed, 1)
            pool.wait_ge(zeroed, 2)
            for eye in (m.eye, m.eye16):
                pool.affine_select(out=eye[:, :], in_=eye[:, :], compare_op=ALU.not_equal, fill=1.0, base=0,
                                   pattern=[[-1, P]], channel_multiplier=1).then_inc(made, 1)

        @block.vector
        def _(dve):
            dve.memset(m.minus_half[:, :], -0.5).then_inc(made, 1)
            dve.memset(m.ones[:, :], 1.0).then_inc(made, 1)
            dve.memset(m.ones16[:, :], 1.0).then_inc(made, 1)


def project(nc, m, x, adj_t, weight, a1, a2, u_rows):
    x_sb = m.f32(64, NT, D)
    feats = m.f32(96, NT, D)
    w_sb = m.f32(128, KT, D)
    h = m.f32(136, 2, D)
    h_t = m.f32(140, KT, P)
    a_sb = m.f32(144, 2, D)
    product = m.f32(148, D)
    w_a = m.f32(150, 2, KT * H)
    top_wide = m.f32(151, P, parts=H)
    row_sum = m.f32(152, N, parts=1)
    u_t = m.f32(160, N, parts=H)
    adj_in = m.f32(168, 4, N)
    top = m.f32(151.5, 3, H)
    top_head = m.f32(151.625, 1, parts=H)
    degrees = m.f32(151.65625, 4, NT)
    d_col = m.dst_part
    step = m.norm
    with ExitStack() as ctx:
        def sem(name):
            return ctx.enter_context(nc.semaphore("A_" + name))

        x_in, w_in, a_in = sem("x_in"), sem("w_in"), sem("a_in")
        adj_landed = [sem(f"adj_landed{k}") for k in range(4)]
        adj_cast, sum_row, sum_cols = sem("adj_cast"), sem("sum_row"), sem("sum_cols")
        stats_done, dve_chain, variance, rstd, shift = (sem("stats_done"), sem("dve_chain"), sem("variance"),
                                                        sem("rstd"), sem("shift"))
        w_a_done, h_done, transposed, h_t_done = sem("w_a_done"), sem("h_done"), sem("transposed"), sem("h_t_done")
        feats_done, feats_kept, parts_done, parts_kept = (sem("feats_done"), sem("feats_kept"), sem("parts_done"),
                                                          sem("parts_kept"))
        top_t, top_row, top_bc, top_all, cols_kept = sem("top_t"), sem("top_row"), sem("top_bc"), sem("top_all"), sem("cols_kept")
        deg_base, deg_pow, base_done, u_done, u_stored = sem("deg_base"), sem("deg_pow"), sem("base_done"), sem("u_done"), sem("u_stored")
        block = ctx.enter_context(nc.Block())
        degree_row = m.bank(0, 4)[0:1, :]
        ps_t, ps_w, ps_s = m.bank(4), m.bank(5), m.bank(6)
        ps_small = m.bank(7)

        @block.sync
        def _(sp):
            sp.dma_start(x_sb, rows(x)).then_inc(x_in, 16)
            sp.dma_start(w_sb, weight.rearrange("(k p) n -> p k n", p=P)).then_inc(w_in, 16)
            def load(t, lane, group):
                wait(sp, adj_cast, t - 3)
                sp.dma_start(adj_in[:, lane, :], adj_t[bass.ts(t, P), :]).then_inc(adj_landed[lane], 16)
            walk(sp, load, 4)
            sp.wait_ge(u_done, 1)
            sp.dma_start(u_rows, u_t).then_inc(u_stored, 16)
            sp.wait_ge(u_stored, 16)

        @block.gpsimd
        def _(pool):
            pool.dma_start(a_sb[:, 0, :], on_all(a1)).then_inc(a_in, 16)
            pool.dma_start(a_sb[:, 1, :], on_all(a2)).then_inc(a_in, 16)
            pool.wait_ge(variance, 1)
            pool.tensor_tensor(step[:, 4, :], step[:, 2, :], m.minus_half[:, :].broadcast_to([P, NT]), ALU.pow).then_inc(rstd, 1)
            pool.wait_ge(deg_base, 1)
            pool.tensor_tensor(m.inv_sqrt_degree[:, :], degrees[:, 2, :], m.minus_half[:, :].broadcast_to([P, NT]), ALU.pow).then_inc(deg_pow, 1)

        @block.vector
        def _(dve):
            chain = Chain(dve, dve_chain)
            dve.wait_ge(x_in, 16)
            def turn(t):
                dve.bn_stats(m.stats[:, t, :], x_sb[:, t, :]).then_inc(stats_done, 1)
            repeat(dve, NT, turn)
            dve.wait_ge(stats_done, NT)
            row_constants(dve, chain, m.stats, step)
            dve.sem_inc(variance, 1)
            dve.wait_ge(w_in, 16)
            dve.wait_ge(a_in, 32)
            for which in range(2):
                for k in range(KT):
                    chain.link(dve.tensor_tensor(product, w_sb[:, k, :], a_sb[:, which, :], ALU.mult))
                    chain.link(dve.tensor_reduce(w_a[:, which, k * H:(k + 1) * H],
                                                 product.rearrange("p (h d) -> p h d", h=H), AXIS.X, ALU.add))
            dve.sem_inc(w_a_done, 1)
            dve.wait_ge(rstd, 1)
            dve.scalar_tensor_tensor(step[:, 5, :], step[:, 3, :], -0.5, step[:, 4, :], ALU.mult, ALU.mult).then_inc(shift, 1)
            def turn(t):
                dve.wait_ge(transposed, t + 1)
                wait(dve, parts_done, t)
                dve.tensor_scalar(h_t.rearrange("p k n -> p (k n)"), ps_t, 0.0, None, ALU.add).then_inc(h_t_done, 1)
                dve.wait_ge(parts_done, t + 1)
                dve.tensor_scalar(d_col[:, t, :], ps_s[:, 0:H], 0.0, None, ALU.add).then_inc(parts_kept, 1)
                dve.tensor_scalar(u_t[:, bass.ts(t, P)], ps_s[0:H, 256:256 + P], 0.0, None, ALU.add).then_inc(parts_kept, 1)
            repeat(dve, NT, turn)
            dve.wait_ge(parts_kept, 2 * NT)
            dve.tensor_reduce(top[:, 0, :], d_col.rearrange("p t h -> p h t"), AXIS.X, ALU.max).then_inc(top_t, 1)
            dve.wait_ge(top_row, 1)
            chain.link(dve.tensor_reduce(top_head, ps_small[0:H, 0:P], AXIS.X, ALU.max))
            chain.link(dve.tensor_scalar(top_wide, m.eye[0:H, 0:1].broadcast_to([H, P]), 0.0, top_head,
                                         ALU.mult, ALU.add))
            dve.sem_inc(top_bc, 1)
            chain.link(dve.tensor_scalar(u_t, u_t, top_head, 1.0 - SLOPE, ALU.add, ALU.mult))
            chain.link(dve.tensor_scalar(u_t, u_t, EXP_CAP, None, ALU.min))
            dve.sem_inc(u_done, 1)
            dve.wait_ge(top_all, 1)
            chain.link(dve.tensor_scalar(top[:, 1, :], ps_small[:, P:P + H], 0.0, None, ALU.add))
            dve.tensor_tensor(d_col, d_col, top[:, 1, :].rearrange("p (a h) -> p a h", a=1).broadcast_to([P, NT, H]),
                              ALU.subtract).then_inc(base_done, 1)
            dve.wait_ge(sum_row, NT)
            dve.tensor_scalar(row_sum, degree_row, 0.0, None, ALU.add).then_inc(cols_kept, 1)
            dve.wait_ge(sum_cols, 1)
            deg = degrees
            chain.link(dve.tensor_scalar(deg[:, 0, :], ps_small[:, 256:256 + NT], 0.0, None, ALU.add))
            dve.wait_ge(adj_cast, NT)
            chain.link(dve.tensor_tensor(deg[:, 2, :], deg[:, 0, :], deg[:, 1, :], ALU.add))
            chain.link(dve.tensor_scalar(deg[:, 2, :], deg[:, 2, :], 0.5, 1.0, ALU.mult, ALU.add))
            chain.link(dve.tensor_scalar(deg[:, 3, :], deg[:, 2, :], 0.0, None, ALU.is_gt))
            chain.link(dve.tensor_scalar(deg[:, 2, :], deg[:, 2, :], 1e-37, None, ALU.max))
            dve.sem_inc(deg_base, 1)
            chain.link(dve.tensor_scalar(deg[:, 0, :], deg[:, 0, :], 1.0, 1e-12, ALU.add, ALU.max))
            dve.reciprocal(m.inv_degree[:, :], deg[:, 0, :])
            dve.wait_ge(deg_pow, 1)
            chain.link(dve.tensor_tensor(m.inv_sqrt_degree[:, :], m.inv_sqrt_degree[:, :], deg[:, 3, :], ALU.mult))

        @block.scalar
        def _(act):
            act.activation(top[:, 2, 0:1], m.minus_half[:, :], ACT.Exp)
            act.wait_ge(shift, 1)

            def tile(t, lane, group):
                wait(act, transposed, t - 1)
                act.activation(h[:, lane % 2, :], x_sb[:, t, :], ACT.Relu, scale=column(step[:, 4, :], t),
                               bias=column(step[:, 5, :], t)).then_inc(h_done, 1)
                act.wait_ge(adj_landed[lane], (group + 1) * 16)
                act.activation(m.adj_t[:, t, :], adj_in[:, lane, :], ACT.Copy,
                               accum_out=column(degrees[:, 1, :], t)).then_inc(adj_cast, 1)
                act.wait_ge(feats_done, t + 1)
                act.activation(feats[:, t, :], ps_w, ACT.Copy).then_inc(feats_kept, 1)
            walk(act, tile, 4)
            act.wait_ge(base_done, 1)
            act.activation(m.dst_floor, d_col, ACT.Exp, scale=SLOPE)

        @block.tensor
        def _(pe):
            pe.wait_ge(w_a_done, 1)

            def tile(t, lane, group):
                pe.wait_ge(h_done, t + 1)
                wait(pe, h_t_done, t)
                for k in range(KT):
                    last = pe.transpose(ps_t[:, k * P:(k + 1) * P], h[:, lane % 2, k * P:(k + 1) * P], m.eye[:, :])
                last.then_inc(transposed, 1)
                pe.wait_ge(h_t_done, t + 1)
                wait(pe, feats_kept, t)
                wait(pe, parts_kept, t * 2)
                for k in range(KT):
                    last = pe.matmul(ps_w, h_t[:, k, :], w_sb[:, k, :], start=k == 0, stop=k == KT - 1)
                last.then_inc(feats_done, 1)
                for k in range(KT):
                    pe.matmul(ps_s[:, 0:H], h_t[:, k, :], w_a[:, 1, k * H:(k + 1) * H], start=k == 0, stop=k == KT - 1)
                for k in range(KT):
                    last = pe.matmul(ps_s[0:H, 256:256 + P], w_a[:, 0, k * H:(k + 1) * H], h_t[:, k, :],
                                     start=k == 0, stop=k == KT - 1)
                last.then_inc(parts_done, 1)
                pe.wait_ge(adj_cast, t + 1)
                first, final = isinstance(t, int) and t == 0, isinstance(t, int) and t == NT - 1
                for c in range(4):
                    last = pe.matmul(degree_row[:, c * BANK:(c + 1) * BANK], m.ones16[:, :],
                                     m.adj_t[:, t, c * BANK:(c + 1) * BANK], start=first, stop=final)
                last.then_inc(sum_row, 1)
            walk(pe, tile, 4)
            pe.wait_ge(top_t, 1)
            pe.transpose(ps_small[0:H, 0:P], top[:, 0, :], m.eye[:, :]).then_inc(top_row, 1)
            pe.wait_ge(top_bc, 1)
            pe.matmul(ps_small[:, P:P + H], top_wide, m.eye[0:H, 0:H], start=True, stop=True).then_inc(top_all, 1)
            pe.wait_ge(cols_kept, 1)
            for t in range(NT):
                last = pe.matmul(ps_small[:, 256 + t:257 + t], row_sum[:, t * P:(t + 1) * P], m.ones[0:1, 0:1],
                                 start=True, stop=True)
            last.then_inc(sum_cols, 1)


def attend(nc, m, u_rows):
    feats = m.f32(96, NT, D)
    enc = m.f32(128, KT, N)
    u_all = [m.f32(168, 4, HALF), m.f32(184, 4, HALF)]
    weights = m.f32(64, 8, HALF)
    own = m.own_feats
    pick = m.pick

    def elu_part(r, pair):
        return u_all[r % 2][:, pair, :]

    def inv_den(r):
        return u_all[r % 2][:, 2, :]

    rounds = [(quad, half) for quad in range(2) for half in range(2)]
    with ExitStack() as ctx:
        def sem(name):
            return ctx.enter_context(nc.semaphore("B_" + name))

        pick_zero, pick_done, own_ready = sem("pick_zero"), sem("pick_done"), sem("own_ready")
        u_landed = [sem(f"u_landed{k}") for k in range(2)]
        exp_done, masked, summed, round_done = sem("exp_done"), sem("masked"), sem("summed"), sem("round_done")
        sums_kept, den_kept, den_spread, scaled = sem("sums_kept"), sem("den_kept"), sem("den_spread"), sem("scaled")
        floored, elu_exp, elu_done = sem("floored"), sem("elu_exp"), sem("elu_done")
        block = ctx.enter_context(nc.Block())
        ps_sum = [m.bank(0, 2), m.bank(2, 2)]
        ps_den = m.bank(4, 2)
        ps_misc = m.bank(6, 2)

        @block.sync
        def _(sp):
            for r, (quad, half) in enumerate(rounds):
                if r >= 2:
                    sp.wait_ge(elu_done, 2 * (r - 1))
                sp.dma_start(u_all[r % 2], u_rows[quad * 4:quad * 4 + 4, half * HALF:(half + 1) * HALF]
                             .partition_broadcast(P)).then_inc(u_landed[r % 2], 16)

        @block.gpsimd
        def _(pool):
            pool.memset(pick, 0.0).then_inc(pick_zero, 1)
            pool.wait_ge(pick_zero, 1)
            pool.affine_select(out=pick.rearrange("p a (b c) -> p a b c", b=2), in_=pick.rearrange("p a (b c) -> p a b c", b=2),
                               compare_op=ALU.not_equal, fill=1.0, base=0,
                               pattern=[[-64, 2], [-32, 2], [0, 64]], channel_multiplier=1).then_inc(pick_done, 1)
            for r, (quad, half) in enumerate(rounds):
                def body(t, slot, group):
                    wait(pool, summed, t + (r * NT - 1))
                    pool.tensor_copy(own[:, slot, :], feats[:, t, quad * 256:(quad + 1) * 256]).then_inc(own_ready, 1)
                walk(pool, body, 2)

        @block.scalar
        def _(act):
            act.activation(m.norm[:, 0, 0:1], m.minus_half[:, :], ACT.Exp)

            for r, (quad, half) in enumerate(rounds):
                def body(t, slot, group):
                    wait(act, summed, t + (r * NT - 1))
                    for q in range(4):
                        bias = d_at(m.dst_part, t, quad * 4 + q)
                        act.activation(weights[:, slot * 4 + q, :], u_all[r % 2][:, q, :], ACT.Exp,
                                       bias=bias).then_inc(exp_done, 1)
                act.wait_ge(u_landed[r % 2], 16 * (r // 2 + 1))
                walk(act, body, 2)
                act.wait_ge(round_done, r + 1)
                for pair in range(2):
                    act.activation(enc[:, quad * 2 + pair, half * HALF:(half + 1) * HALF], ps_sum[pair],
                                   ACT.Copy).then_inc(sums_kept, 1)
                for pair in range(2):
                    act.wait_ge(floored, 2 * r + pair + 1)
                    act.activation(elu_part(r, pair), elu_part(r, pair), ACT.Exp).then_inc(elu_exp, 1)

        @block.vector
        def _(dve):
            for r, (quad, half) in enumerate(rounds):
                def body(t, slot, group):
                    for q in range(4):
                        w = weights[:, slot * 4 + q, :]
                        dve.wait_ge(exp_done, (t + r * NT) * 4 + q + 1)
                        dve.scalar_tensor_tensor(w, w, d_at(m.dst_floor, t, quad * 4 + q),
                                                 m.adj_t[:, t, half * HALF:(half + 1) * HALF],
                                                 ALU.max, ALU.mult).then_inc(masked, 1)
                walk(dve, body, 2)
                dve.wait_ge(round_done, r + 1)
                if r:
                    dve.wait_ge(den_spread, 2 * r)
                dve.reciprocal(inv_den(r), ps_den).then_inc(den_kept, 1)
                for pair in range(2):
                    part = enc[:, quad * 2 + pair, half * HALF:(half + 1) * HALF]
                    dve.wait_ge(den_spread, 2 * r + pair + 1)
                    dve.wait_ge(sums_kept, 2 * r + pair + 1)
                    dve.tensor_tensor(part, part, ps_misc, ALU.mult).then_inc(scaled, 1)
                    dve.wait_ge(scaled, 2 * r + pair + 1)
                    dve.tensor_scalar(elu_part(r, pair), part, 0.0, None, ALU.min).then_inc(floored, 1)
                for pair in range(2):
                    part = enc[:, quad * 2 + pair, half * HALF:(half + 1) * HALF]
                    dve.wait_ge(elu_exp, 2 * r + pair + 1)
                    dve.scalar_tensor_tensor(part, elu_part(r, pair), -1.0, part, ALU.add, ALU.max).then_inc(elu_done, 1)

        @block.tensor
        def _(pe):
            pe.wait_ge(pick_done, 1)
            for r, (quad, half) in enumerate(rounds):
                def body(t, slot, group):
                    first, final = isinstance(t, int) and t == 0, isinstance(t, int) and t == NT - 1
                    if first and r:
                        pe.wait_ge(sums_kept, 2 * r)
                        pe.wait_ge(den_kept, r)
                    pe.wait_ge(own_ready, t + (r * NT + 1))
                    for pair in range(2):
                        pe.wait_ge(masked, (t + r * NT) * 4 + 2 * pair + 2)
                        for c in range(2):
                            for q in range(2):
                                pe.matmul(ps_sum[pair][64 * q:64 * q + 64, c * BANK:(c + 1) * BANK],
                                          own[:, slot, (2 * pair + q) * HD:(2 * pair + q + 1) * HD],
                                          weights[:, slot * 4 + 2 * pair + q, c * BANK:(c + 1) * BANK],
                                          start=first, stop=final, tile_position=(0, 64 * q))
                    for c in range(2):
                        for q in range(4):
                            last = pe.matmul(ps_den[32 * q:32 * q + 32, c * BANK:(c + 1) * BANK], m.ones[:, :],
                                             weights[:, slot * 4 + q, c * BANK:(c + 1) * BANK],
                                             start=first, stop=final, tile_position=(0, 32 * q))
                    last.then_inc(summed, 1)
                walk(pe, body, 2)
                pe.wait_ge(summed, (r + 1) * NT)
                pe.sem_inc(round_done, 1)
                pe.wait_ge(den_kept, r + 1)
                for pair in range(2):
                    wait(pe, scaled, 2 * r + pair)
                    for c in range(2):
                        last = pe.matmul(ps_misc[:, c * BANK:(c + 1) * BANK], pick[:, pair, :],
                                         inv_den(r)[:, c * BANK:(c + 1) * BANK], start=True, stop=True)
                    last.then_inc(den_spread, 1)


def dense(nc, m, x, w1, b1, w2, b2, w3, b3, w4, b4, x1_rows):
    x_sb = m.f32(64, NT, D)
    enc = m.f32(128, KT, N)
    w1_sb, w2_sb, w3_sb, w4_sb = m.f32(96, 4, 256), m.f32(100, 2, P), m.f32(101, 1, 256), m.f32(102, 2, D)
    y1, y2, y3 = m.f32(106, 2, BANK), m.f32(110, BANK), m.f32(112, 2, BANK)
    b1_sb, b2_sb, b3_sb, b4_sb = m.f32(116, 2), m.f32(116.125, 1), m.f32(116.25, 2), m.f32(117, D)
    with ExitStack() as ctx:
        def sem(name):
            return ctx.enter_context(nc.semaphore("C_" + name))

        x_in, w_in, b_in, biased = sem("x_in"), sem("w_in"), sem("b_in"), sem("biased")
        l1_done, l2_done, l3_done, l4_done = sem("l1_done"), sem("l2_done"), sem("l3_done"), sem("l4_done")
        y1_kept, y2_kept, y3_kept, x1_done = sem("y1_kept"), sem("y2_kept"), sem("y3_kept"), sem("x1_done")
        stats_done, stored = sem("stats_done"), sem("stored")
        block = ctx.enter_context(nc.Block())

        @block.sync
        def _(sp):
            sp.dma_start(w1_sb, w1.rearrange("(k p) n -> p k n", p=P)).then_inc(w_in, 16)
            sp.dma_start(w2_sb, w2.rearrange("(k p) n -> p k n", p=P)).then_inc(w_in, 16)
            sp.dma_start(w3_sb, w3.rearrange("(k p) n -> p k n", p=P)).then_inc(w_in, 16)
            sp.dma_start(w4_sb, w4.rearrange("(k p) n -> p k n", p=P)).then_inc(w_in, 16)
            sp.dma_start(x_sb, rows(x)).then_inc(x_in, 16)
            def turn(c):
                sp.wait_ge(x1_done, c * 4 + 4)
                sp.dma_start(rows(x1_rows)[:, bass.ts(c, 4), :], x_sb[:, bass.ts(c, 4), :]).then_inc(stored, 16)
            repeat(sp, 4, turn)
            sp.wait_ge(stored, 64)

        @block.gpsimd
        def _(pool):
            with nc.allow_non_contiguous_dma(reason="bias columns"):
                pool.dma_start(b1_sb, columns(b1)).then_inc(b_in, 16)
                pool.dma_start(b2_sb, columns(b2)).then_inc(b_in, 16)
                pool.dma_start(b3_sb, columns(b3)).then_inc(b_in, 16)
            pool.dma_start(b4_sb, on_all(b4)).then_inc(b_in, 16)
            pool.wait_ge(b_in, 64)
            pool.wait_ge(x_in, 16)
            def turn(t):
                pool.tensor_tensor(x_sb[:, t, :], x_sb[:, t, :], b4_sb, ALU.add).then_inc(biased, 1)
            repeat(pool, NT, turn)

        @block.scalar
        def _(act):
            act.wait_ge(b_in, 64)
            act.activation(m.scratch[:, 0:1], m.minus_half[:, :], ACT.Copy)
            def turn(c):
                for half in range(2):
                    wait(act, l2_done, c)
                    act.wait_ge(l1_done, c * 2 + half + 1)
                    act.activation(y1[:, half, :], m.bank(half), ACT.Relu, bias=b1_sb[:, half:half + 1]).then_inc(y1_kept, 1)
                wait(act, l3_done, c * 2)
                act.wait_ge(l2_done, c + 1)
                act.activation(y2, m.bank(2), ACT.Relu, bias=b2_sb).then_inc(y2_kept, 1)
                for half in range(2):
                    wait(act, l4_done, c * 4)
                    act.wait_ge(l3_done, c * 2 + half + 1)
                    act.activation(y3[:, half, :], m.bank(half), ACT.Relu, bias=b3_sb[:, half:half + 1]).then_inc(y3_kept, 1)
            repeat(act, 4, turn)

        @block.vector
        def _(dve):
            dve.wait_ge(biased, NT)
            def turn(c):
                for i in range(4):
                    dve.wait_ge(l4_done, c * 4 + i + 1)
                    dve.tensor_tensor(x_sb[:, c * 4 + i, :], x_sb[:, c * 4 + i, :], m.bank(3 + i), ALU.add).then_inc(x1_done, 1)
                    dve.wait_ge(x1_done, c * 4 + i + 1)
                    dve.bn_stats(m.stats[:, c * 4 + i, :], x_sb[:, c * 4 + i, :]).then_inc(stats_done, 1)
            repeat(dve, 4, turn)

        @block.tensor
        def _(pe):
            pe.wait_ge(w_in, 64)
            def turn(c):
                wait(pe, y3_kept, c * 2)
                for half in range(2):
                    for k in range(KT):
                        last = pe.matmul(m.bank(half), w1_sb[:, k, half * P:(half + 1) * P], enc[:, k, bass.ts(c, BANK)],
                                         start=k == 0, stop=k == KT - 1)
                    last.then_inc(l1_done, 1)
                pe.wait_ge(y1_kept, c * 2 + 2)
                wait(pe, y2_kept, c)
                for k in range(2):
                    last = pe.matmul(m.bank(2), w2_sb[:, k, :], y1[:, k, :], start=k == 0, stop=k == 1)
                last.then_inc(l2_done, 1)
                pe.wait_ge(y2_kept, c + 1)
                for half in range(2):
                    pe.matmul(m.bank(half), w3_sb[:, 0, half * P:(half + 1) * P], y2, start=True, stop=True).then_inc(l3_done, 1)
                pe.wait_ge(y3_kept, c * 2 + 2)
                wait(pe, x1_done, c * 4)
                for i in range(4):
                    for k in range(2):
                        last = pe.matmul(m.bank(3 + i), y3[:, k, i * P:(i + 1) * P], w4_sb[:, k, :], start=k == 0, stop=k == 1)
                    last.then_inc(l4_done, 1)
            repeat(pe, 4, turn)


def norm_constants(nc, m, name, extra_scale=None):
    step = m.norm
    with ExitStack() as ctx:
        variance = ctx.enter_context(nc.semaphore(name + "_variance"))
        power = ctx.enter_context(nc.semaphore(name + "_power"))
        dve_chain = ctx.enter_context(nc.semaphore(name + "_chain"))
        block = ctx.enter_context(nc.Block())

        @block.gpsimd
        def _(pool):
            pool.wait_ge(variance, 1)
            pool.tensor_tensor(step[:, 4, :], step[:, 2, :], m.minus_half[:, :].broadcast_to([P, NT]), ALU.pow).then_inc(power, 1)

        @block.vector
        def _(dve):
            chain = Chain(dve, dve_chain)
            row_constants(dve, chain, m.stats, step)
            dve.sem_inc(variance, 1)
            dve.wait_ge(power, 1)
            if extra_scale is not None:
                chain.link(dve.tensor_tensor(step[:, 4, :], step[:, 4, :], extra_scale, ALU.mult))
            chain.link(dve.scalar_tensor_tensor(step[:, 5, :], step[:, 3, :], -0.5, step[:, 4, :], ALU.mult, ALU.mult))


def queries(nc, m, t_w1, t_w2, t_w3):
    h = m.f32(64, NT, D)
    parts = m.f16(96, NT, 2, D)
    keys, query = m.f32(128, N, parts=64), m.f32(136, N, parts=64)
    h_t, w1_t, w2_sb, ring = m.f32(144, KT, P), m.f32(146, D, parts=64), m.f32(148, 64, parts=64), m.f32(150, 2, D)
    step = m.norm
    with ExitStack() as ctx:
        def sem(name):
            return ctx.enter_context(nc.semaphore("D_" + name))

        w_in, merged, merged_kept = sem("w_in"), sem("merged"), sem("merged_kept")
        ring_done, h_done, high_done, low_done = sem("ring_done"), sem("h_done"), sem("high_done"), sem("low_done")
        transposed, h_t_kept, qk_done, qk_kept = sem("transposed"), sem("h_t_kept"), sem("qk_done"), sem("qk_kept")
        block = ctx.enter_context(nc.Block())
        ps_t, ps_qk = m.bank(0), m.bank(1)

        @block.sync
        def _(sp):
            sp.dma_start(w1_t, t_w1).then_inc(w_in, 16)
            sp.dma_start(w2_sb, t_w2).then_inc(w_in, 16)
            sp.dma_start(m.qk_weight[:, :, 64:P], t_w3.rearrange("(k p) n -> p k n", p=P)).then_inc(w_in, 16)

        @block.scalar
        def _(act):
            act.activation(m.scratch[:, 0:1], m.minus_half[:, :], ACT.Copy)

            def tile(t, lane, group):
                wait(act, transposed, t - 1)
                wait(act, h_done, t - 1)
                scale, shift = column(step[:, 4, :], t), column(step[:, 5, :], t)
                act.activation(ring[:, lane, :], h[:, t, :], ACT.Relu, scale=scale, bias=shift).then_inc(ring_done, 1)
                act.activation(parts[:, t, 0, :], h[:, t, :], ACT.Relu, scale=scale, bias=shift).then_inc(high_done, 1)
            walk(act, tile, 2)

        @block.gpsimd
        def _(pool):
            def tile(t, lane, group):
                pool.wait_ge(ring_done, t + 1)
                pool.wait_ge(high_done, t + 1)
                pool.tensor_copy(h[:, t, :], ring[:, lane, :]).then_inc(h_done, 1)
            walk(pool, tile, 2)

        @block.vector
        def _(dve):
            dve.wait_ge(merged, 1)
            dve.tensor_scalar(m.qk_weight[:, :, 0:64], ps_t[:, 0:256].rearrange("p (k n) -> p k n", k=KT), 0.0, None,
                              ALU.add).then_inc(merged_kept, 1)

            def tile(t, lane, group):
                dve.wait_ge(transposed, t + 1)
                wait(dve, qk_done, t)
                dve.tensor_scalar(h_t.rearrange("p k n -> p (k n)"), ps_t, 0.0, None, ALU.add).then_inc(h_t_kept, 1)
                dve.wait_ge(h_done, t + 1)
                dve.tensor_tensor(parts[:, t, 1, :], h[:, t, :], parts[:, t, 0, :], ALU.subtract).then_inc(low_done, 1)
                dve.wait_ge(qk_done, t + 1)
                dve.tensor_scalar(query[:, bass.ts(t, P)], ps_qk[0:64, 0:P], 0.0, None, ALU.add).then_inc(qk_kept, 1)
                dve.tensor_scalar(keys[:, bass.ts(t, P)], ps_qk[64:P, 0:P], 0.0, None, ALU.add).then_inc(qk_kept, 1)
            walk(dve, tile, 2)

        @block.tensor
        def _(pe):
            pe.wait_ge(w_in, 48)
            for k in range(KT):
                last = pe.matmul(ps_t[:, k * 64:(k + 1) * 64], w1_t[:, k * P:(k + 1) * P], w2_sb, start=True, stop=True)
            last.then_inc(merged, 1)
            pe.wait_ge(merged_kept, 1)

            def tile(t, lane, group):
                pe.wait_ge(ring_done, t + 1)
                wait(pe, h_t_kept, t)
                for k in range(KT):
                    last = pe.transpose(ps_t[:, k * P:(k + 1) * P], ring[:, lane, k * P:(k + 1) * P], m.eye[:, :])
                last.then_inc(transposed, 1)
                pe.wait_ge(h_t_kept, t + 1)
                wait(pe, qk_kept, t * 2)
                for k in range(KT):
                    last = pe.matmul(ps_qk[:, 0:P], m.qk_weight[:, k, :], h_t[:, k, :], start=k == 0, stop=k == KT - 1)
                last.then_inc(qk_done, 1)
            walk(pe, tile, 2)


def diffuse(nc, m, s, u1, u2, xa_rows, xf_rows, y_in, y_out):
    xa = m.f32(64, NT, D)
    xf = m.f16(96, NT, 2, D)
    lo, hi_part = 64 * s, 64 * s + 64
    keys, query = m.f32(128, N)[lo:hi_part, :], m.f32(136, N)[lo:hi_part, :]
    next_keys, next_query = m.f32(128, N)[64:P, :], m.f32(136, N)[64:P, :]
    probs = [m.f32(144, N), m.f32(152, N)]
    above = m.f32(160, N)
    at = m.f32(168, 2, 4 * P)
    q_ring = m.f32(172, 2, P)
    share = m.f32(173, 2, P)
    cols, ratio = m.f32(174, 16), m.f32(174.5, STEPS + 1)
    u1_sb, u2_sb = m.f32(176, KT, D), m.f32(184, KT, D)
    x_t, xt, zt = m.f32(192, KT, P), m.f32(194, D), m.f32(196, D)
    halves, y_old = m.f16(198, 2, D), m.f32(198, D)
    junk = m.scratch[:, :].bitcast(BF16)
    neg_max, total, target, hi, cut, mass, keep, sh, sl, w_inv, count, kept, frac, norm = (cols[:, k:k + 1] for k in range(14))
    first_step = s == 0
    with ExitStack() as ctx:
        def sem(name):
            return ctx.enter_context(nc.semaphore(f"E{s}_" + name))

        u_in, xa_in, xf_in, ratios = sem("u_in"), sem("xa_in"), sem("xf_in"), sem("ratios")
        q_ready, logits, maxed, exp_done, cut_done, dve_chain = (sem("q_ready"), sem("logits"), sem("maxed"),
                                                                 sem("exp_done"), sem("cut_done"), sem("dve_chain"))
        mixed, at_kept, product, xa_kept, xa_stored = sem("mixed"), sem("at_kept"), sem("product"), sem("xa_kept"), sem("xa_stored")
        xt_turned, xt_kept, u_used, qk_done, qk_kept = (sem("xt_turned"), sem("xt_kept"), sem("u_used"), sem("qk_done"),
                                                        sem("qk_kept"))
        spread, xf_kept, high_done, low_done, xf_stored = (sem("spread"), sem("xf_kept"), sem("high_done"), sem("low_done"),
                                                           sem("xf_stored"))
        z_kept, y_landed, y_done, y_stored = sem("z_kept"), sem("y_landed"), sem("y_done"), sem("y_stored")
        block = ctx.enter_context(nc.Block())
        ps_logits = m.bank(0, 4)
        ps_t, ps_x, ps_z = [m.bank(4), m.bank(5)], m.bank(6), m.bank(7)

        def pipeline(head, tail):
            def run(eng):
                if head:
                    head(0, 0)
                    head(1, 1)
                tail(0, 0)
                with eng.Fori(0, NT // 2 - 1) as i:
                    if head:
                        head(i * 2 + 2, 0)
                    tail(i * 2 + 1, 1)
                    if head:
                        head(i * 2 + 3, 1)
                    tail(i * 2 + 2, 0)
                tail(NT - 1, 1)
            return run

        @block.sync
        def _(sp):
            sp.dma_start(u2_sb, u2.rearrange("(k p) n -> p k n", p=P)).then_inc(u_in, 16)
            sp.dma_start(u1_sb, u1.rearrange("(k p) n -> p k n", p=P)).then_inc(u_in, 16)
            if not first_step:
                sp.dma_start(xa, rows(xa_rows)).then_inc(xa_in, 16)
                sp.dma_start(xf, xf_rows.rearrange("(t p) a f -> p t a f", p=P)).then_inc(xf_in, 16)

            def tail(t, lane):
                if first_step:
                    sp.wait_ge(xa_kept, t + 1)
                    sp.dma_start(xa_rows[bass.ts(t, P), :], xt).then_inc(xa_stored, 16)
                    sp.wait_ge(low_done, t + 1)
                    sp.dma_start(xf_rows[bass.ts(t, P), :, :], halves).then_inc(xf_stored, 16)
                else:
                    wait(sp, y_done, t)
                    sp.dma_start(y_old, y_in[bass.ts(t, P), :]).then_inc(y_landed, 16)
                sp.wait_ge(y_done, t + 1)
                sp.dma_start(y_out[bass.ts(t, P), :], zt).then_inc(y_stored, 16)
            pipeline(None, tail)(sp)
            sp.wait_ge(y_stored, 16 * NT)
            if first_step:
                sp.wait_ge(xa_stored, 16 * NT)
                sp.wait_ge(xf_stored, 16 * NT)

        @block.gpsimd
        def _(pool):
            def head(t, lane):
                wait(pool, logits, t - 1)
                pool.tensor_copy(q_ring[0:hi_part, lane, :], m.f32(136, N)[0:hi_part, bass.ts(t, P)]).then_inc(q_ready, 1)

            def tail(t, lane):
                if first_step:
                    pool.wait_ge(high_done, t + 1)
                    pool.tensor_tensor(halves[:, 1, :], xt, halves[:, 0, :], ALU.subtract).then_inc(low_done, 1)
                pool.wait_ge(z_kept, t + 1)
                if first_step:
                    pool.tensor_tensor(zt, zt, xa[:, t, :], ALU.add).then_inc(y_done, 1)
                else:
                    pool.wait_ge(y_landed, t * 16 + 16)
                    pool.tensor_tensor(zt, zt, y_old, ALU.add).then_inc(y_done, 1)
            pipeline(head, tail)(pool)

        @block.vector
        def _(dve):
            links = [0]

            def head(t, lane):
                e = probs[lane]
                per_tile = links[0] if links[0] else 0
                base = t * per_tile
                chain = Chain(dve, dve_chain, base)
                dve.wait_ge(logits, t + 1)
                chain.link(dve.tensor_reduce(neg_max, ps_logits, AXIS.X, ALU.max))
                dve.tensor_scalar(neg_max, neg_max, -1.0, None, ALU.mult).then_inc(maxed, 1)
                dve.wait_ge(exp_done, t + 1)
                chain.link(dve.tensor_scalar(target, total, P_TOP, None, ALU.mult))
                chain.link(dve.tensor_scalar(hi, total, 0.0, 1.0, ALU.mult, ALU.add))
                chain.count(dve.tensor_scalar(cut, hi, ratio[:, 0:1], None, ALU.mult))
                before = chain.n
                per_halving = 4
                with dve.Fori(0, STEPS) as k:
                    inner = Chain(dve, dve_chain, base + (k * per_halving + before))
                    inner.wait()
                    inner.link(dve.scalar_tensor_tensor(junk, e, cut, e, ALU.is_gt, ALU.mult, accum_out=mass))
                    inner.link(dve.tensor_scalar(keep, mass, target, hi, ALU.is_ge, ALU.mult))
                    inner.link(dve.tensor_scalar(hi, keep, cut, None, ALU.max))
                    inner.count(dve.tensor_scalar(cut, hi, column(ratio, k + 1), None, ALU.mult))
                    assert inner.n == per_halving
                chain.n = before + STEPS * per_halving
                chain.wait()
                wait(dve, mixed, t * 4)
                chain.link(dve.scalar_tensor_tensor(above, e, hi, e, ALU.is_gt, ALU.mult, accum_out=sh))
                chain.link(dve.scalar_tensor_tensor(e, e, cut, e, ALU.is_gt, ALU.mult, accum_out=sl))
                chain.link(dve.reciprocal(w_inv, cut))
                chain.link(dve.tensor_tensor(mass, sl, sh, ALU.subtract))
                chain.link(dve.tensor_tensor(keep, target, sh, ALU.subtract))
                round_up = 1.5 * 2 ** 23
                chain.link(dve.tensor_scalar(count, mass, w_inv, round_up, ALU.mult, ALU.add))
                chain.link(dve.tensor_scalar(count, count, -round_up, 1.0, ALU.add, ALU.max))
                chain.link(dve.tensor_scalar(kept, keep, w_inv, 0.4999, ALU.mult, ALU.add))
                chain.link(dve.tensor_scalar(kept, kept, round_up, None, ALU.add))
                chain.link(dve.tensor_scalar(kept, kept, -round_up, 1.0, ALU.add, ALU.max))
                chain.link(dve.tensor_tensor(kept, kept, count, ALU.min))
                chain.link(dve.reciprocal(count, count))
                chain.link(dve.tensor_tensor(frac, kept, count, ALU.mult))
                chain.link(dve.tensor_scalar(norm, mass, frac, sh, ALU.mult, ALU.add))
                chain.link(dve.reciprocal(norm, norm))
                chain.link(dve.tensor_scalar(kept, frac, -1.0, 1.0, ALU.mult, ALU.add))
                chain.link(dve.tensor_scalar(share[:, 0, :], m.eye[:, :], kept, norm, ALU.mult, ALU.mult))
                dve.tensor_scalar(share[:, 1, :], m.eye[:, :], frac, norm, ALU.mult, ALU.mult).then_inc(cut_done, 1)
                if not links[0]:
                    links[0] = chain.n
                assert links[0] == chain.n

            for k in range(STEPS + 1):
                wide = SEARCH / 2 ** (k + 1) if k < STEPS else SEARCH / 2 ** STEPS + 6e-7
                last = dve.memset(ratio[:, k:k + 1], math.exp(-wide))
            last.then_inc(ratios, 1)
            dve.wait_ge(ratios, 1)
            head(0, 0)
            head(1, 1)
            with dve.Fori(1, NT // 2) as i:
                head(i * 2, 0)
                head(i * 2 + 1, 1)

        @block.scalar
        def _(act):
            act.activation(xt[:, 0:1], m.minus_half[:, :], ACT.Exp)

            def head(t, lane):
                act.wait_ge(maxed, t + 1)
                wait(act, mixed, t * 4 - 4)
                act.activation(probs[lane], ps_logits, ACT.Exp, bias=neg_max, accum_out=total).then_inc(exp_done, 1)

            def tail(t, lane):
                for g in range(4):
                    act.wait_ge(mixed, t * 4 + g + 1)
                    wait(act, product, t * 4 + g - 1)
                    act.activation(at[:, g % 2, :], ps_t[g % 2], ACT.Copy).then_inc(at_kept, 1)
                act.wait_ge(product, t * 4 + 4)
                wait(act, xt_turned, t * 2)
                if first_step:
                    wait(act, low_done, t)
                act.activation(xt, ps_x, ACT.Copy).then_inc(xa_kept, 1)
                act.wait_ge(xt_turned, t * 2 + 1)
                wait(act, u_used, t * 2)
                act.activation(x_t.rearrange("p k n -> p (k n)"), ps_t[0], ACT.Copy).then_inc(xt_kept, 1)
                if first_step:
                    act.wait_ge(qk_done, t + 1)
                    act.activation(next_query[:, bass.ts(t, P)], ps_t[1][0:64, 0:P], ACT.Copy).then_inc(qk_kept, 1)
                    act.activation(next_keys[:, bass.ts(t, P)], ps_t[1][64:P, 0:P], ACT.Copy).then_inc(qk_kept, 1)
                act.wait_ge(spread, t + 1)
                if first_step:
                    act.wait_ge(xa_stored, t * 16 + 16)
                act.activation(xt, ps_x, ACT.Copy, scale=column(m.inv_degree[:, :], t)).then_inc(xf_kept, 1)
                if first_step:
                    act.wait_ge(xf_kept, t + 1)
                    wait(act, xf_stored, t * 16)
                    act.activation(halves[:, 0, :], xt, ACT.Copy).then_inc(high_done, 1)
                act.wait_ge(xt_turned, t * 2 + 2)
                act.wait_ge(u_used, t * 2 + 1)
                act.activation(x_t.rearrange("p k n -> p (k n)"), ps_t[0], ACT.Copy).then_inc(xt_kept, 1)
                act.wait_ge(u_used, t * 2 + 2)
                wait(act, y_stored, t * 16)
                act.activation(zt, ps_z, ACT.Copy).then_inc(z_kept, 1)
            pipeline(head, tail)(act)

        @block.tensor
        def _(pe):
            pe.wait_ge(u_in, 32)

            def head(t, lane):
                pe.wait_ge(q_ready, t + 1)
                wait(pe, exp_done, t)
                for c in range(4):
                    last = pe.matmul(ps_logits[:, c * BANK:(c + 1) * BANK], q_ring[lo:hi_part, lane, :],
                                     keys[:, c * BANK:(c + 1) * BANK], start=True, stop=True)
                last.then_inc(logits, 1)

            def tail(t, lane):
                if not first_step and isinstance(t, int) and t == 0:
                    pe.wait_ge(xa_in, 16)
                    pe.wait_ge(xf_in, 16)
                pe.wait_ge(cut_done, t + 1)
                wait(pe, xf_kept, t)
                wait(pe, xt_kept, t * 2)

                def mix(g):
                    wait(pe, at_kept, t * 4 + max(g - 1, 0))
                    for j in range(4):
                        block_of = slice((4 * g + j) * P, (4 * g + j + 1) * P)
                        pe.matmul(ps_t[g % 2][:, j * P:(j + 1) * P], above[:, block_of], share[:, 0, :], start=True, stop=False)
                        last = pe.matmul(ps_t[g % 2][:, j * P:(j + 1) * P], probs[lane][:, block_of], share[:, 1, :],
                                         start=False, stop=True)
                    last.then_inc(mixed, 1)

                def multiply(g):
                    pe.wait_ge(at_kept, t * 4 + g + 1)
                    for j in range(4):
                        last = pe.matmul(ps_x, at[:, g % 2, j * P:(j + 1) * P], xa[:, 4 * g + j, :],
                                         start=g == 0 and j == 0, stop=g == 3 and j == 3)
                    last.then_inc(product, 1)

                if first_step:
                    wait(pe, qk_kept, t * 2)
                mix(0)
                for g in range(1, 4):
                    mix(g)
                    multiply(g - 1)
                multiply(3)
                pe.wait_ge(xa_kept, t + 1)
                for k in range(KT):
                    last = pe.transpose(ps_t[0][:, k * P:(k + 1) * P], xt[:, k * P:(k + 1) * P], m.eye[:, :])
                last.then_inc(xt_turned, 1)
                for k in range(2):
                    pe.matmul(ps_x, m.eye16[:, :], xf[:, t, k, :], start=k == 0, stop=False)
                for j in range(NT):
                    for k in range(2):
                        last = pe.matmul(ps_x, m.adj_t[:, j, bass.ts(t, P)], xf[:, j, k, :], start=False,
                                         stop=j == NT - 1 and k == 1)
                last.then_inc(spread, 1)
                pe.wait_ge(xt_kept, t * 2 + 1)
                wait(pe, z_kept, t)
                if first_step:
                    for k in range(KT):
                        last = pe.matmul(ps_t[1][:, 0:P], m.qk_weight[:, k, :], x_t[:, k, :], start=k == 0, stop=k == KT - 1)
                    last.then_inc(qk_done, 1)
                for k in range(KT):
                    last = pe.matmul(ps_z, x_t[:, k, :], u2_sb[:, k, :], start=k == 0, stop=False)
                last.then_inc(u_used, 1)
                pe.wait_ge(xf_kept, t + 1)
                for k in range(KT):
                    last = pe.transpose(ps_t[0][:, k * P:(k + 1) * P], xt[:, k * P:(k + 1) * P], m.eye[:, :])
                last.then_inc(xt_turned, 1)
                pe.wait_ge(xt_kept, t * 2 + 2)
                for k in range(KT):
                    last = pe.matmul(ps_z, x_t[:, k, :], u1_sb[:, k, :], start=False, stop=k == KT - 1)
                last.then_inc(u_used, 1)
            pipeline(head, tail)(pe)


def close_diffusion(nc, m, y_rows, x1_rows, x2_rows, gamma, beta):
    y, x = m.f32(64, NT, D), m.f32(96, NT, D)
    gamma_sb, beta_sb = m.f32(192, D), m.f32(194, D)
    step = m.norm
    with ExitStack() as ctx:
        def sem(name):
            return ctx.enter_context(nc.semaphore("F_" + name))

        y_in, x_in, g_in, stats_done = sem("y_in"), sem("x_in"), sem("g_in"), sem("stats_done")
        block = ctx.enter_context(nc.Block())

        @block.sync
        def _(sp):
            sp.dma_start(y, rows(y_rows)).then_inc(y_in, 16)
            sp.dma_start(x, rows(x1_rows)).then_inc(x_in, 16)
            sp.dma_start(gamma_sb, on_all(gamma)).then_inc(g_in, 16)
            sp.dma_start(beta_sb, on_all(beta)).then_inc(g_in, 16)
            sp.wait_ge(x_in, 16)
            sp.wait_ge(g_in, 32)

        @block.vector
        def _(dve):
            dve.wait_ge(y_in, 16)
            def turn(t):
                dve.bn_stats(m.stats[:, t, :], y[:, t, :]).then_inc(stats_done, 1)
            repeat(dve, NT, turn)
    norm_constants(nc, m, "F1")
    with ExitStack() as ctx:
        def sem(name):
            return ctx.enter_context(nc.semaphore("G_" + name))

        centred, scaled, shifted, x_done, stats_done, x_stored = (sem("centred"), sem("scaled"), sem("shifted"), sem("x_done"),
                                                                  sem("stats_done"), sem("x_stored"))
        block = ctx.enter_context(nc.Block())

        @block.scalar
        def _(act):
            act.activation(m.scratch[:, 0:1], m.minus_half[:, :], ACT.Identity)
            def turn(t):
                act.activation(y[:, t, :], y[:, t, :], ACT.Identity, scale=column(step[:, 4, :], t),
                               bias=column(step[:, 5, :], t)).then_inc(centred, 1)
            repeat(act, NT, turn)

        @block.gpsimd
        def _(pool):
            def turn(t):
                pool.tensor_tensor(x[:, t, :], x[:, t, :], beta_sb, ALU.add).then_inc(shifted, 1)
            repeat(pool, NT, turn)

        @block.vector
        def _(dve):
            def turn(t):
                dve.wait_ge(centred, t + 1)
                dve.tensor_tensor(y[:, t, :], y[:, t, :], gamma_sb, ALU.mult).then_inc(scaled, 1)
                dve.wait_ge(scaled, t + 1)
                dve.wait_ge(shifted, t + 1)
                dve.tensor_tensor(x[:, t, :], x[:, t, :], y[:, t, :], ALU.add).then_inc(x_done, 1)
                dve.wait_ge(x_done, t + 1)
                dve.bn_stats(m.stats[:, t, :], x[:, t, :]).then_inc(stats_done, 1)
            repeat(dve, NT, turn)

        @block.sync
        def _(sp):
            def turn(c):
                sp.wait_ge(x_done, c * 4 + 4)
                sp.dma_start(rows(x2_rows)[:, bass.ts(c, 4), :], x[:, bass.ts(c, 4), :]).then_inc(x_stored, 16)
            repeat(sp, 4, turn)
            sp.wait_ge(x_stored, 64)
    norm_constants(nc, m, "F2", m.inv_sqrt_degree[:, :])
    normed_halves(nc, m, "F3", x)


def normed_halves(nc, m, name, x):
    halves, ring = m.f16(128, NT, 2, D), m.f32(192, 2, D)
    step = m.norm
    with ExitStack() as ctx:
        full, high, low = (ctx.enter_context(nc.semaphore(name + s)) for s in ("_full", "_high", "_low"))
        block = ctx.enter_context(nc.Block())

        @block.scalar
        def _(act):
            act.activation(m.scratch[:, 0:1], m.minus_half[:, :], ACT.Relu)

            def tile(t, lane, group):
                scale, shift = column(step[:, 4, :], t), column(step[:, 5, :], t)
                wait(act, low, t - 1)
                act.activation(ring[:, lane, :], x[:, t, :], ACT.Relu, scale=scale, bias=shift).then_inc(full, 1)
                act.activation(halves[:, t, 0, :], x[:, t, :], ACT.Relu, scale=scale, bias=shift).then_inc(high, 1)
            walk(act, tile, 2)

        @block.vector
        def _(dve):
            def tile(t, lane, group):
                dve.wait_ge(full, t + 1)
                dve.wait_ge(high, t + 1)
                dve.tensor_tensor(halves[:, t, 1, :], ring[:, lane, :], halves[:, t, 0, :], ALU.subtract).then_inc(low, 1)
            walk(dve, tile, 2)


def symmetrise(nc, m, adj):
    mean, adj_in = m.f16(64, NT, N), m.f32(160, 4, N)
    with ExitStack() as ctx:
        landed = [ctx.enter_context(nc.semaphore(f"H_landed{k}")) for k in range(4)]
        added, halved = ctx.enter_context(nc.semaphore("H_added")), ctx.enter_context(nc.semaphore("H_halved"))
        block = ctx.enter_context(nc.Block())

        @block.sync
        def _(sp):
            def tile(t, lane, group):
                wait(sp, added, t - 3)
                sp.dma_start(adj_in[:, lane, :], adj[bass.ts(t, P), :]).then_inc(landed[lane], 16)
            walk(sp, tile, 4)

        @block.vector
        def _(dve):
            def tile(t, lane, group):
                dve.wait_ge(landed[lane], (group + 1) * 16)
                dve.tensor_tensor(mean[:, t, :], adj_in[:, lane, :], m.adj_t[:, t, :], ALU.add).then_inc(added, 1)
            walk(dve, tile, 4)

        @block.scalar
        def _(act):
            act.activation(m.scratch[:, 0:1], m.minus_half[:, :], ACT.Copy)
            def turn(t):
                act.wait_ge(added, t + 1)
                act.activation(mean[:, t, :], mean[:, t, :], ACT.Copy, scale=0.5).then_inc(halved, 1)
            repeat(act, NT, turn)


def propagate(nc, m, x2_rows):
    mean, source = m.f16(64, NT, N), m.f16(128, NT, 2, D)
    spread, ring = m.f16(160, NT, 2, D), m.f32(192, 2, D)
    with ExitStack() as ctx:
        summed, kept, high, low = (ctx.enter_context(nc.semaphore("I_" + s)) for s in ("summed", "kept", "high", "low"))
        block = ctx.enter_context(nc.Block())

        @block.tensor
        def _(pe):
            def tile(t, lane, group):
                wait(pe, kept, t - 1)
                for k in range(2):
                    pe.matmul(m.bank(lane), m.eye16[:, :], source[:, t, k, :], start=k == 0, stop=False)
                for j in range(NT):
                    for k in range(2):
                        last = pe.matmul(m.bank(lane), mean[:, j, bass.ts(t, P)], source[:, j, k, :], start=False,
                                         stop=j == NT - 1 and k == 1)
                last.then_inc(summed, 1)
            walk(pe, tile, 2)

        @block.scalar
        def _(act):
            act.activation(m.scratch[:, 0:1], m.minus_half[:, :], ACT.Copy)

            def tile(t, lane, group):
                wait(act, low, t - 1)
                act.wait_ge(summed, t + 1)
                act.activation(ring[:, lane, :], m.bank(lane), ACT.Copy, scale=column(m.inv_sqrt_degree[:, :], t)).then_inc(kept, 1)
                act.wait_ge(kept, t + 1)
                act.activation(spread[:, t, 0, :], ring[:, lane, :], ACT.Copy).then_inc(high, 1)
            walk(act, tile, 2)

        @block.vector
        def _(dve):
            def tile(t, lane, group):
                dve.wait_ge(high, t + 1)
                dve.tensor_tensor(spread[:, t, 1, :], ring[:, lane, :], spread[:, t, 0, :], ALU.subtract).then_inc(low, 1)
            walk(dve, tile, 2)
    x = m.f32(64, NT, D)
    with ExitStack() as ctx:
        x_in, summed, x_done, stats_done = (ctx.enter_context(nc.semaphore("J_" + s)) for s in ("x_in", "summed", "x_done", "stats_done"))
        block = ctx.enter_context(nc.Block())

        @block.sync
        def _(sp):
            sp.dma_start(x, rows(x2_rows)).then_inc(x_in, 16)

        @block.tensor
        def _(pe):
            def tile(t, lane, group):
                wait(pe, x_done, t - 1)
                for j in range(NT):
                    for k in range(2):
                        last = pe.matmul(m.bank(lane), m.adj_t[:, j, bass.ts(t, P)], spread[:, j, k, :],
                                         start=j == 0 and k == 0, stop=j == NT - 1 and k == 1)
                last.then_inc(summed, 1)
            walk(pe, tile, 2)

        @block.vector
        def _(dve):
            dve.wait_ge(x_in, 16)

            def tile(t, lane, group):
                dve.wait_ge(summed, t + 1)
                dve.tensor_tensor(x[:, t, :], x[:, t, :], m.bank(lane), ALU.add).then_inc(x_done, 1)
                dve.wait_ge(x_done, t + 1)
                dve.bn_stats(m.stats[:, t, :], x[:, t, :]).then_inc(stats_done, 1)
            walk(dve, tile, 2)
    norm_constants(nc, m, "K1")
    normed_halves(nc, m, "K2", x)


def convolve(nc, m, weight, bias, out):
    x, source = m.f32(64, NT, D), m.f16(128, NT, 2, D)
    w_sb, bias_sb = m.f32(96, KT, D), m.f32(104, D)
    sums, sums_t, result = m.f32(106, 2, D), m.f32(110, 2, D), m.f32(114, 2, D)
    with ExitStack() as ctx:
        def sem(name):
            return ctx.enter_context(nc.semaphore("L_" + name))

        w_in, b_in, summed, sums_kept, turned, turned_kept = (sem("w_in"), sem("b_in"), sem("summed"), sem("sums_kept"),
                                                              sem("turned"), sem("turned_kept"))
        multiplied, biased, result_done, stored = sem("multiplied"), sem("biased"), sem("result_done"), [sem(f"stored{k}") for k in range(2)]
        block = ctx.enter_context(nc.Block())

        @block.sync
        def _(sp):
            sp.dma_start(w_sb, weight.rearrange("(k p) n -> p k n", p=P)).then_inc(w_in, 16)
            sp.dma_start(bias_sb, on_all(bias)).then_inc(b_in, 16)

            def tile(t, lane, group):
                sp.wait_ge(result_done, t + 1)
                sp.dma_start(out[bass.ts(t, P), :], result[:, lane, :]).then_inc(stored[lane], 16)
            walk(sp, tile, 2)
            for lane in range(2):
                sp.wait_ge(stored[lane], NT // 2 * 16)

        @block.gpsimd
        def _(pool):
            pool.wait_ge(b_in, 16)
            def turn(t):
                pool.tensor_tensor(x[:, t, :], x[:, t, :], bias_sb, ALU.add).then_inc(biased, 1)
            repeat(pool, NT, turn)

        @block.tensor
        def _(pe):
            pe.wait_ge(w_in, 16)

            def gather(t, lane):
                wait(pe, sums_kept, t - 1)
                for j in range(NT):
                    for k in range(2):
                        last = pe.matmul(m.bank(lane), m.adj_t[:, j, bass.ts(t, P)], source[:, j, k, :],
                                         start=j == 0 and k == 0, stop=j == NT - 1 and k == 1)
                last.then_inc(summed, 1)

            def project_sums(t, lane):
                pe.wait_ge(sums_kept, t + 1)
                wait(pe, turned_kept, t - 1)
                for k in range(KT):
                    last = pe.transpose(m.bank(2 + lane)[:, k * P:(k + 1) * P], sums[:, lane, k * P:(k + 1) * P], m.eye[:, :])
                last.then_inc(turned, 1)
                pe.wait_ge(turned_kept, t + 1)
                wait(pe, result_done, t - 1)
                for k in range(KT):
                    last = pe.matmul(m.bank(4 + lane), sums_t[:, lane, k * P:(k + 1) * P], w_sb[:, k, :], start=k == 0, stop=k == KT - 1)
                last.then_inc(multiplied, 1)

            gather(0, 0)
            gather(1, 1)
            project_sums(0, 0)
            with pe.Fori(0, NT // 2 - 1) as i:
                gather(i * 2 + 2, 0)
                project_sums(i * 2 + 1, 1)
                gather(i * 2 + 3, 1)
                project_sums(i * 2 + 2, 0)
            project_sums(NT - 1, 1)

        @block.scalar
        def _(act):
            act.activation(m.scratch[:, 0:1], m.minus_half[:, :], ACT.Copy)

            def tile(t, lane, group):
                act.wait_ge(summed, t + 1)
                wait(act, turned, t - 1)
                act.activation(sums[:, lane, :], m.bank(lane), ACT.Copy).then_inc(sums_kept, 1)
            walk(act, tile, 2)

        @block.vector
        def _(dve):
            def tile(t, lane, group):
                dve.wait_ge(turned, t + 1)
                wait(dve, multiplied, t - 1)
                dve.tensor_scalar(sums_t[:, lane, :], m.bank(2 + lane), 0.0, None, ALU.add).then_inc(turned_kept, 1)
                dve.wait_ge(multiplied, t + 1)
                dve.wait_ge(biased, t + 1)
                wait(dve, stored[lane], group * 16)
                dve.tensor_tensor(result[:, lane, :], m.bank(4 + lane), x[:, t, :], ALU.add).then_inc(result_done, 1)
            walk(dve, tile, 2)


def d_at(columns_of, t, head):
    if isinstance(t, int):
        return columns_of[:, t, head:head + 1]
    return columns_of[:, bass.ds(t, 1), head:head + 1].rearrange("p a h -> p (a h)")


def clear_counts(nc, free):
    with nc.Block() as block:
        @block.gpsimd
        def _(pool):
            pool.sem_clear(range(min(free), max(free) + 1))


def program(nc, x, adj, adj_t, g_w, g_a1, g_a2, g_w1, g_b1, g_w2, g_b2, g_w3, g_b3, g_w4, g_b4,
            t_w1, t_w2, t_w3, u1_0, u1_1, u2_0, u2_1, gamma, beta, c_w, c_b, out):
    with ExitStack() as ctx:
        m = Memory(nc, ctx)
        free = list(nc.free_semaphores)
        constants(nc, m)
        def spill(name, *shape, dt=F32):
            return nc.dram_tensor(name, shape, dt, kind="Internal").ap()

        u_rows, x1_rows, x2_rows = spill("u_rows", H, N), spill("x1_rows", N, D), spill("x2_rows", N, D)
        y1_rows, y2_rows, xa_rows = spill("y1_rows", N, D), spill("y2_rows", N, D), spill("xa_rows", N, D)
        xf_rows = spill("xf_rows", N, 2, D, dt=F16)
        project(nc, m, x, adj_t, g_w, g_a1, g_a2, u_rows)
        attend(nc, m, u_rows)
        dense(nc, m, x, g_w1, g_b1, g_w2, g_b2, g_w3, g_b3, g_w4, g_b4, x1_rows)
        norm_constants(nc, m, "D0")
        queries(nc, m, t_w1, t_w2, t_w3)
        diffuse(nc, m, 0, u1_0, u2_0, xa_rows, xf_rows, None, y1_rows)
        diffuse(nc, m, 1, u1_1, u2_1, xa_rows, xf_rows, y1_rows, y2_rows)
        clear_counts(nc, free)
        close_diffusion(nc, m, y2_rows, x1_rows, x2_rows, gamma, beta)
        symmetrise(nc, m, adj)
        propagate(nc, m, x2_rows)
        convolve(nc, m, c_w, c_b, out)


def kernel(x, adj, L0_gnn_W, L0_gnn_a1, L0_gnn_a2, L0_gnn_W1, L0_gnn_b1, L0_gnn_W2, L0_gnn_b2, L0_gnn_W3, L0_gnn_b3,
           L0_gnn_W4, L0_gnn_b4, L1_gnn_W1, L1_gnn_W2, L1_gnn_W3, L1_gnn_U1_0, L1_gnn_U1_1, L1_gnn_U2_0, L1_gnn_U2_1,
           L1_gnn_gamma, L1_gnn_beta, L3_gnn_weight, L3_gnn_bias):
    import concourse.bacc as bacc
    from concourse.bass_utils import run_bass_kernel_spmd

    laid_out = {
        "x": x, "adj": adj, "adj_t": adj.T, "g_w": L0_gnn_W.transpose(1, 0, 2).reshape(D, D),
        "g_a1": L0_gnn_a1.reshape(-1), "g_a2": L0_gnn_a2.reshape(-1),
        "g_w1": L0_gnn_W1.T, "g_b1": L0_gnn_b1, "g_w2": L0_gnn_W2.T, "g_b2": L0_gnn_b2,
        "g_w3": L0_gnn_W3.T, "g_b3": L0_gnn_b3, "g_w4": L0_gnn_W4.T, "g_b4": L0_gnn_b4,
        "t_w1": L1_gnn_W1.T, "t_w2": L1_gnn_W2, "t_w3": L1_gnn_W3, "u1_0": L1_gnn_U1_0, "u1_1": L1_gnn_U1_1,
        "u2_0": L1_gnn_U2_0, "u2_1": L1_gnn_U2_1, "gamma": L1_gnn_gamma, "beta": L1_gnn_beta,
        "c_w": L3_gnn_weight, "c_b": L3_gnn_bias,
    }
    nc = bacc.Bacc("TRN2", target_bir_lowering=False, num_devices=1)
    arrays, args = {}, []
    for name, a in laid_out.items():
        a = np.ascontiguousarray(a)
        arrays["in_" + name] = a
        args.append(nc.dram_tensor("in_" + name, a.shape, mybir.dt.from_np(a.dtype), kind="ExternalInput").ap())
    out = nc.dram_tensor("out", (N, D), F32, kind="ExternalOutput").ap()
    program(nc, *args, out)
    result = run_bass_kernel_spmd(nc, [arrays], core_ids=[0])
    return result.results[0]["out"]
```

```python
import math
from contextlib import ExitStack

import numpy as np

import concourse.bass as bass
from concourse import mybir

F32 = mybir.dt.float32
F16 = mybir.dt.float16
BF16 = mybir.dt.bfloat16
I8 = mybir.dt.int8
ALU = mybir.AluOpType
ACT = mybir.ActivationFunctionType
AXIS = mybir.AxisListType

P = 128
N = 2048
NT = N // P
D = 512
KT = D // P
H, HD = 8, 64
BANK = 512
HALF = N // 2
SLOPE = 0.2
LN_EPS = 1e-5
EXP_CAP = 80.0
P_TOP = 0.9
SEARCH = math.log(N / (1.0 - P_TOP)) + 0.05
STEPS = 22
HALVINGS = (8, 12)
SCALAR_HALVINGS = (5, 5)
KB = 1024
ARENA = 200 * KB


class Chain:

    def __init__(self, eng, sem, base=0):
        self.eng, self.sem, self.base, self.n = eng, sem, base, 0

    def link(self, ins):
        self.count(ins)
        self.wait()

    def count(self, ins):
        self.n += 1
        ins.then_inc(self.sem, 1)

    def wait(self):
        self.eng.wait_ge(self.sem, self.base + self.n)


class Memory:

    def __init__(self, nc, ctx):
        self.nc, self.ctx = nc, ctx
        self.arena = ctx.enter_context(nc.sbuf_tensor("arena", [P, ARENA // 4], F32))
        self.psum = ctx.enter_context(nc.psum_tensor("banks", [P, 8, BANK], F32))
        self.eye = self.small("eye", [P, P], F32)
        self.eye16 = self.small("eye16", [P, P], F16)
        self.minus_half = self.small("minus_half", [P, 1], F32)
        self.ones = self.small("ones", [P, 32], F32)
        self.ones16 = self.small("ones16", [P, 1], F16)
        self.stats = self.small("stats", [P, NT, 6], F32)
        self.norm = self.small("norm", [P, 6, NT], F32)
        self.inv_degree = self.small("inv_degree", [P, NT], F32)
        self.inv_sqrt_degree = self.small("inv_sqrt_degree", [P, NT], F32)
        self.qk_weight = self.small("qk_weight", [P, KT, P], F32)
        self.scratch = self.small("scratch", [P, 4 * KB // 4], F32)
        self.own_feats = shaped(self.scratch[:, 0:512], (2, 256))
        self.pick = shaped(self.scratch[:, 512:768], (2, P))
        self.dst_part = shaped(self.scratch[:, 768:896], (NT, H))
        self.dst_floor = shaped(self.scratch[:, 896:1024], (NT, H))
        self.adj_t = self.f16(0, NT, N)

    def small(self, name, shape, dt):
        return self.ctx.enter_context(self.nc.sbuf_tensor(name, shape, dt))

    def f32(self, kb, *shape, parts=P):
        start, size = int(kb * KB) // 4, int(np.prod(shape))
        assert kb * KB + size * 4 <= ARENA
        view = self.arena[0:parts, start:start + size]
        return shaped(view, shape)

    def f16(self, kb, *shape, dt=F16):
        start, size = kb * KB // 4, int(np.prod(shape)) // 2
        assert kb * KB + size * 4 <= ARENA
        return shaped(self.arena[:, start:start + size].bitcast(dt), shape)

    def bank(self, b, count=1):
        return self.psum[:, b:b + count, :].rearrange("p b n -> p (b n)")


def shaped(view, shape):
    if len(shape) == 2:
        return view.rearrange("p (a b) -> p a b", a=shape[0])
    if len(shape) == 3:
        return view.rearrange("p (a b c) -> p a b c", a=shape[0], b=shape[1])
    return view


def columns(dram):
    return dram.rearrange("(k p) -> p k", p=P)


def rows(dram):
    return dram.rearrange("(t p) f -> p t f", p=P)


def on_all(dram):
    return dram.partition_broadcast(P)


def wait(eng, sem, value):
    if not isinstance(value, int) or value > 0:
        eng.wait_ge(sem, value)


def halving(k):
    return math.exp(-SEARCH / 2 ** (k + 1))


def tile_rows(t):
    return bass.ts(t, P)


def queries_of(q_rows, t):
    return q_rows[bass.ts(t, P), :][0:64, 0:P]


def column(table, t):
    return table[:, bass.ds(t, 1)]


def repeat(eng, count, body):
    body(0)
    with eng.Fori(1, count) as i:
        body(i)


def walk(eng, body, lanes):
    groups = NT // lanes
    for lane in range(lanes):
        body(lane, lane, 0)
    with eng.Fori(1, groups - 1) as g:
        for lane in range(lanes):
            body(g * lanes + lane, lane, g)
    for lane in range(lanes):
        body(NT - lanes + lane, lane, groups - 1)


def row_constants(dve, chain, stats, norm):
    sq, diff, var, mean2 = (norm[:, k, :] for k in range(4))
    half = [stats[:, :, k] for k in range(6)]
    dve.tensor_tensor(sq, half[2], half[5], ALU.add)
    chain.link(dve.tensor_tensor(diff, half[1], half[4], ALU.subtract))
    chain.link(dve.scalar_tensor_tensor(mean2, diff, 0.25, diff, ALU.mult, ALU.mult))
    chain.link(dve.scalar_tensor_tensor(var, sq, 1.0 / D, mean2, ALU.mult, ALU.add))
    chain.link(dve.tensor_scalar(var, var, LN_EPS, None, ALU.add))
    chain.link(dve.tensor_tensor(mean2, half[1], half[4], ALU.add))


def measure_chunks(dve, x, landed, stats, done):
    for c in range(4):
        dve.wait_ge(landed[c], 16)
        for t in range(4 * c, 4 * c + 4):
            dve.bn_stats(stats[:, t, :], x[:, t, :]).then_inc(done, 1)
    dve.wait_ge(done, NT)


def constants(nc, m):
    with ExitStack() as ctx:
        zeroed = ctx.enter_context(nc.semaphore("zeroed"))
        made = ctx.enter_context(nc.semaphore("made"))
        block = ctx.enter_context(nc.Block())

        @block.gpsimd
        def _(pool):
            for eye in (m.eye, m.eye16):
                pool.memset(eye[:, :], 0.0).then_inc(zeroed, 1)
            pool.wait_ge(zeroed, 2)
            for eye in (m.eye, m.eye16):
                pool.affine_select(out=eye[:, :], in_=eye[:, :], compare_op=ALU.not_equal, fill=1.0, base=0,
                                   pattern=[[-1, P]], channel_multiplier=1).then_inc(made, 1)

        @block.vector
        def _(dve):
            dve.memset(m.minus_half[:, :], -0.5).then_inc(made, 1)
            dve.memset(m.ones[:, :], 1.0).then_inc(made, 1)
            dve.memset(m.ones16[:, :], 1.0).then_inc(made, 1)


def project(nc, m, x, adj_t, weight, a1, a2, u_rows):
    x_sb = m.f32(64, NT, D)
    feats = m.f32(96, NT, D)
    w_sb = m.f32(128, KT, D)
    h = m.f32(136, 2, D)
    h_t = m.f32(140, KT, P)
    a_sb = m.f32(144, 2, D)
    product = m.f32(148, D)
    w_a = m.f32(150, 2, KT * H)
    top_wide = m.f32(151, P, parts=H)
    row_sum = m.f32(152, N, parts=1)
    u_t = m.f32(160, N, parts=H)
    adj_in = m.f32(168, 4, N)
    top = m.f32(151.5, 3, H)
    top_head = m.f32(151.625, 1, parts=H)
    degrees = m.f32(151.65625, 4, NT)
    d_col = m.dst_part
    step = m.norm
    with ExitStack() as ctx:
        def sem(name):
            return ctx.enter_context(nc.semaphore("A_" + name))

        x_in, w_in, a_in = [sem(f"x_in{c}") for c in range(4)], sem("w_in"), sem("a_in")
        adj_landed = [sem(f"adj_landed{k}") for k in range(4)]
        adj_cast, sum_row, sum_cols = sem("adj_cast"), sem("sum_row"), sem("sum_cols")
        stats_done, dve_chain, variance, rstd, shift = (sem("stats_done"), sem("dve_chain"), sem("variance"),
                                                        sem("rstd"), sem("shift"))
        w_a_done, h_done, transposed, h_t_done = sem("w_a_done"), sem("h_done"), sem("transposed"), sem("h_t_done")
        feats_done, feats_kept, parts_done, parts_kept = (sem("feats_done"), sem("feats_kept"), sem("parts_done"),
                                                          sem("parts_kept"))
        top_t, top_row, top_bc, top_all, cols_kept = sem("top_t"), sem("top_row"), sem("top_bc"), sem("top_all"), sem("cols_kept")
        deg_base, deg_pow, base_done, u_done, u_stored = sem("deg_base"), sem("deg_pow"), sem("base_done"), sem("u_done"), sem("u_stored")
        block = ctx.enter_context(nc.Block())
        degree_row = m.bank(0, 4)[0:1, :]
        ps_t, ps_w, ps_s = m.bank(4), m.bank(5), m.bank(6)
        ps_small = m.bank(7)

        @block.sync
        def _(sp):
            sp.dma_start(w_sb, weight.rearrange("(k p) n -> p k n", p=P)).then_inc(w_in, 16)
            for c in range(4):
                sp.dma_start(x_sb[:, 4 * c:4 * c + 4, :], rows(x)[:, 4 * c:4 * c + 4, :]).then_inc(x_in[c], 16)
            def load(t, lane, group):
                wait(sp, adj_cast, t - 3)
                sp.dma_start(adj_in[:, lane, :], adj_t[bass.ts(t, P), :]).then_inc(adj_landed[lane], 16)
            walk(sp, load, 4)
            sp.wait_ge(u_done, 1)
            sp.dma_start(u_rows, u_t).then_inc(u_stored, 16)
            sp.wait_ge(u_stored, 16)

        @block.gpsimd
        def _(pool):
            pool.wait_ge(variance, 1)
            pool.tensor_tensor(step[:, 4, :], step[:, 2, :], m.minus_half[:, :].broadcast_to([P, NT]), ALU.pow).then_inc(rstd, 1)
            pool.wait_ge(deg_base, 1)
            pool.tensor_tensor(m.inv_sqrt_degree[:, :], degrees[:, 2, :], m.minus_half[:, :].broadcast_to([P, NT]), ALU.pow).then_inc(deg_pow, 1)

        @block.vector
        def _(dve):
            chain = Chain(dve, dve_chain)
            dve.wait_ge(w_in, 16)
            dve.wait_ge(a_in, 32)
            for which in range(2):
                for k in range(KT):
                    chain.link(dve.tensor_tensor(product, w_sb[:, k, :], a_sb[:, which, :], ALU.mult))
                    chain.link(dve.tensor_reduce(w_a[:, which, k * H:(k + 1) * H],
                                                 product.rearrange("p (h d) -> p h d", h=H), AXIS.X, ALU.add))
            dve.sem_inc(w_a_done, 1)
            measure_chunks(dve, x_sb, x_in, m.stats, stats_done)
            row_constants(dve, chain, m.stats, step)
            dve.sem_inc(variance, 1)
            dve.wait_ge(rstd, 1)
            dve.scalar_tensor_tensor(step[:, 5, :], step[:, 3, :], -0.5, step[:, 4, :], ALU.mult, ALU.mult).then_inc(shift, 1)
            def turn(t):
                dve.wait_ge(transposed, t + 1)
                wait(dve, parts_done, t)
                dve.tensor_scalar(h_t.rearrange("p k n -> p (k n)"), ps_t, 0.0, None, ALU.add).then_inc(h_t_done, 1)
                dve.wait_ge(parts_done, t + 1)
                dve.tensor_scalar(d_col[:, t, :], ps_s[:, 0:H], 0.0, None, ALU.add).then_inc(parts_kept, 1)
                dve.tensor_scalar(u_t[:, bass.ts(t, P)], ps_s[0:H, 256:256 + P], 0.0, None, ALU.add).then_inc(parts_kept, 1)
            repeat(dve, NT, turn)
            dve.wait_ge(parts_kept, 2 * NT)
            dve.tensor_reduce(top[:, 0, :], d_col.rearrange("p t h -> p h t"), AXIS.X, ALU.max).then_inc(top_t, 1)
            dve.wait_ge(top_row, 1)
            chain.link(dve.tensor_reduce(top_head, ps_small[0:H, 0:P], AXIS.X, ALU.max))
            chain.link(dve.tensor_scalar(top_wide, m.eye[0:H, 0:1].broadcast_to([H, P]), 0.0, top_head,
                                         ALU.mult, ALU.add))
            dve.sem_inc(top_bc, 1)
            chain.link(dve.tensor_scalar(u_t, u_t, top_head, 1.0 - SLOPE, ALU.add, ALU.mult))
            chain.link(dve.tensor_scalar(u_t, u_t, EXP_CAP, None, ALU.min))
            dve.sem_inc(u_done, 1)
            dve.wait_ge(top_all, 1)
            chain.link(dve.tensor_scalar(top[:, 1, :], ps_small[:, P:P + H], 0.0, None, ALU.add))
            dve.tensor_tensor(d_col, d_col, top[:, 1, :].rearrange("p (a h) -> p a h", a=1).broadcast_to([P, NT, H]),
                              ALU.subtract).then_inc(base_done, 1)
            dve.wait_ge(sum_row, NT)
            dve.tensor_scalar(row_sum, degree_row, 0.0, None, ALU.add).then_inc(cols_kept, 1)
            dve.wait_ge(sum_cols, 1)
            deg = degrees
            chain.link(dve.tensor_scalar(deg[:, 0, :], ps_small[:, 256:256 + NT], 0.0, None, ALU.add))
            dve.wait_ge(adj_cast, NT)
            chain.link(dve.tensor_tensor(deg[:, 2, :], deg[:, 0, :], deg[:, 1, :], ALU.add))
            chain.link(dve.tensor_scalar(deg[:, 2, :], deg[:, 2, :], 0.5, 1.0, ALU.mult, ALU.add))
            chain.link(dve.tensor_scalar(deg[:, 3, :], deg[:, 2, :], 0.0, None, ALU.is_gt))
            chain.link(dve.tensor_scalar(deg[:, 2, :], deg[:, 2, :], 1e-37, None, ALU.max))
            dve.sem_inc(deg_base, 1)
            chain.link(dve.tensor_scalar(deg[:, 0, :], deg[:, 0, :], 1.0, 1e-12, ALU.add, ALU.max))
            dve.reciprocal(m.inv_degree[:, :], deg[:, 0, :])
            dve.wait_ge(deg_pow, 1)
            chain.link(dve.tensor_tensor(m.inv_sqrt_degree[:, :], m.inv_sqrt_degree[:, :], deg[:, 3, :], ALU.mult))

        @block.scalar
        def _(act):
            act.dma_start(a_sb[:, 0, :], on_all(a1)).then_inc(a_in, 16)
            act.dma_start(a_sb[:, 1, :], on_all(a2)).then_inc(a_in, 16)
            act.activation(top[:, 2, 0:1], m.minus_half[:, :], ACT.Exp)
            act.wait_ge(shift, 1)

            def tile(t, lane, group):
                wait(act, transposed, t - 1)
                act.activation(h[:, lane % 2, :], x_sb[:, t, :], ACT.Relu, scale=column(step[:, 4, :], t),
                               bias=column(step[:, 5, :], t)).then_inc(h_done, 1)
                act.wait_ge(adj_landed[lane], (group + 1) * 16)
                act.activation(m.adj_t[:, t, :], adj_in[:, lane, :], ACT.Copy,
                               accum_out=column(degrees[:, 1, :], t)).then_inc(adj_cast, 1)
                act.wait_ge(feats_done, t + 1)
                act.activation(feats[:, t, :], ps_w, ACT.Copy).then_inc(feats_kept, 1)
            walk(act, tile, 4)
            act.wait_ge(base_done, 1)
            act.activation(m.dst_floor, d_col, ACT.Exp, scale=SLOPE)

        @block.tensor
        def _(pe):
            pe.wait_ge(w_a_done, 1)

            def tile(t, lane, group):
                pe.wait_ge(h_done, t + 1)
                wait(pe, h_t_done, t)
                for k in range(KT):
                    last = pe.transpose(ps_t[:, k * P:(k + 1) * P], h[:, lane % 2, k * P:(k + 1) * P], m.eye[:, :])
                last.then_inc(transposed, 1)
                if not (isinstance(t, int) and t == 0):
                    sum_columns(t - 1)
                pe.wait_ge(h_t_done, t + 1)
                wait(pe, feats_kept, t)
                wait(pe, parts_kept, t * 2)
                for k in range(KT):
                    last = pe.matmul(ps_w, h_t[:, k, :], w_sb[:, k, :], start=k == 0, stop=k == KT - 1)
                last.then_inc(feats_done, 1)
                for k in range(KT):
                    pe.matmul(ps_s[:, 0:H], h_t[:, k, :], w_a[:, 1, k * H:(k + 1) * H], start=k == 0, stop=k == KT - 1)
                for k in range(KT):
                    last = pe.matmul(ps_s[0:H, 256:256 + P], w_a[:, 0, k * H:(k + 1) * H], h_t[:, k, :],
                                     start=k == 0, stop=k == KT - 1)
                last.then_inc(parts_done, 1)

            def sum_columns(t):
                pe.wait_ge(adj_cast, t + 1)
                first, final = isinstance(t, int) and t == 0, isinstance(t, int) and t == NT - 1
                for c in range(4):
                    last = pe.matmul(degree_row[:, c * BANK:(c + 1) * BANK], m.ones16[:, :],
                                     m.adj_t[:, t, c * BANK:(c + 1) * BANK], start=first, stop=final)
                last.then_inc(sum_row, 1)
            walk(pe, tile, 4)
            sum_columns(NT - 1)
            pe.wait_ge(top_t, 1)
            pe.transpose(ps_small[0:H, 0:P], top[:, 0, :], m.eye[:, :]).then_inc(top_row, 1)
            pe.wait_ge(top_bc, 1)
            pe.matmul(ps_small[:, P:P + H], top_wide, m.eye[0:H, 0:H], start=True, stop=True).then_inc(top_all, 1)
            pe.wait_ge(cols_kept, 1)
            for t in range(NT):
                last = pe.matmul(ps_small[:, 256 + t:257 + t], row_sum[:, t * P:(t + 1) * P], m.ones[0:1, 0:1],
                                 start=True, stop=True)
            last.then_inc(sum_cols, 1)


def attend(nc, m, u_rows):
    feats = m.f32(96, NT, D)
    enc = m.f32(128, KT, N)
    u_all = [m.f32(168, 4, HALF), m.f32(184, 4, HALF)]
    weights = m.f32(64, 8, HALF)
    own = m.own_feats
    pick = m.pick

    def elu_part(r, pair):
        return u_all[r % 2][:, pair, :]

    def inv_den(r):
        return u_all[r % 2][:, 2, :]

    rounds = [(quad, half) for quad in range(2) for half in range(2)]
    with ExitStack() as ctx:
        def sem(name):
            return ctx.enter_context(nc.semaphore("B_" + name))

        pick_zero, pick_done, own_ready = sem("pick_zero"), sem("pick_done"), sem("own_ready")
        u_landed = [sem(f"u_landed{k}") for k in range(2)]
        exp_done, masked, summed, round_done = sem("exp_done"), sem("masked"), sem("summed"), sem("round_done")
        sums_kept, den_kept, den_spread, scaled = sem("sums_kept"), sem("den_kept"), sem("den_spread"), sem("scaled")
        floored, elu_exp, elu_done = sem("floored"), sem("elu_exp"), sem("elu_done")
        block = ctx.enter_context(nc.Block())
        ps_sum = [m.bank(0, 2), m.bank(2, 2)]
        ps_den = m.bank(4, 2)
        ps_misc = m.bank(6, 2)

        @block.sync
        def _(sp):
            for r, (quad, half) in enumerate(rounds):
                if r >= 2:
                    sp.wait_ge(elu_done, 2 * (r - 1))
                sp.dma_start(u_all[r % 2], u_rows[quad * 4:quad * 4 + 4, half * HALF:(half + 1) * HALF]
                             .partition_broadcast(P)).then_inc(u_landed[r % 2], 16)

        @block.gpsimd
        def _(pool):
            pool.memset(pick, 0.0).then_inc(pick_zero, 1)
            pool.wait_ge(pick_zero, 1)
            pool.affine_select(out=pick.rearrange("p a (b c) -> p a b c", b=2), in_=pick.rearrange("p a (b c) -> p a b c", b=2),
                               compare_op=ALU.not_equal, fill=1.0, base=0,
                               pattern=[[-64, 2], [-32, 2], [0, 64]], channel_multiplier=1).then_inc(pick_done, 1)
            for r, (quad, half) in enumerate(rounds):
                def body(t, slot, group):
                    wait(pool, summed, t + (r * NT - 1))
                    pool.tensor_copy(own[:, slot, :], feats[:, t, quad * 256:(quad + 1) * 256]).then_inc(own_ready, 1)
                walk(pool, body, 2)

        @block.scalar
        def _(act):
            act.activation(m.norm[:, 0, 0:1], m.minus_half[:, :], ACT.Exp)

            for r, (quad, half) in enumerate(rounds):
                def body(t, slot, group):
                    wait(act, summed, t + (r * NT - 1))
                    for q in range(4):
                        bias = d_at(m.dst_part, t, quad * 4 + q)
                        act.activation(weights[:, slot * 4 + q, :], u_all[r % 2][:, q, :], ACT.Exp,
                                       bias=bias).then_inc(exp_done, 1)
                act.wait_ge(u_landed[r % 2], 16 * (r // 2 + 1))
                walk(act, body, 2)
                act.wait_ge(round_done, r + 1)
                for pair in range(2):
                    act.activation(enc[:, quad * 2 + pair, half * HALF:(half + 1) * HALF], ps_sum[pair],
                                   ACT.Copy).then_inc(sums_kept, 1)
                for pair in range(2):
                    act.wait_ge(floored, 2 * r + pair + 1)
                    act.activation(elu_part(r, pair), elu_part(r, pair), ACT.Exp).then_inc(elu_exp, 1)

        @block.vector
        def _(dve):
            for r, (quad, half) in enumerate(rounds):
                def body(t, slot, group):
                    for q in range(4):
                        w = weights[:, slot * 4 + q, :]
                        dve.wait_ge(exp_done, (t + r * NT) * 4 + q + 1)
                        dve.scalar_tensor_tensor(w, w, d_at(m.dst_floor, t, quad * 4 + q),
                                                 m.adj_t[:, t, half * HALF:(half + 1) * HALF],
                                                 ALU.max, ALU.mult).then_inc(masked, 1)
                walk(dve, body, 2)
                dve.wait_ge(round_done, r + 1)
                if r:
                    dve.wait_ge(den_spread, 2 * r)
                dve.reciprocal(inv_den(r), ps_den).then_inc(den_kept, 1)
                for pair in range(2):
                    part = enc[:, quad * 2 + pair, half * HALF:(half + 1) * HALF]
                    dve.wait_ge(den_spread, 2 * r + pair + 1)
                    dve.wait_ge(sums_kept, 2 * r + pair + 1)
                    dve.tensor_tensor(part, part, ps_misc, ALU.mult).then_inc(scaled, 1)
                    dve.wait_ge(scaled, 2 * r + pair + 1)
                    dve.tensor_scalar(elu_part(r, pair), part, 0.0, None, ALU.min).then_inc(floored, 1)
                for pair in range(2):
                    part = enc[:, quad * 2 + pair, half * HALF:(half + 1) * HALF]
                    dve.wait_ge(elu_exp, 2 * r + pair + 1)
                    dve.scalar_tensor_tensor(part, elu_part(r, pair), -1.0, part, ALU.add, ALU.max).then_inc(elu_done, 1)

        @block.tensor
        def _(pe):
            pe.wait_ge(pick_done, 1)
            for r, (quad, half) in enumerate(rounds):
                def body(t, slot, group):
                    first, final = isinstance(t, int) and t == 0, isinstance(t, int) and t == NT - 1
                    if first and r:
                        pe.wait_ge(sums_kept, 2 * r)
                        pe.wait_ge(den_kept, r)
                    pe.wait_ge(own_ready, t + (r * NT + 1))
                    for pair in range(2):
                        pe.wait_ge(masked, (t + r * NT) * 4 + 2 * pair + 2)
                        for c in range(2):
                            for q in range(2):
                                pe.matmul(ps_sum[pair][64 * q:64 * q + 64, c * BANK:(c + 1) * BANK],
                                          own[:, slot, (2 * pair + q) * HD:(2 * pair + q + 1) * HD],
                                          weights[:, slot * 4 + 2 * pair + q, c * BANK:(c + 1) * BANK],
                                          start=first, stop=final, tile_position=(0, 64 * q))
                    for c in range(2):
                        for q in range(4):
                            last = pe.matmul(ps_den[32 * q:32 * q + 32, c * BANK:(c + 1) * BANK], m.ones[:, :],
                                             weights[:, slot * 4 + q, c * BANK:(c + 1) * BANK],
                                             start=first, stop=final, tile_position=(0, 32 * q))
                    last.then_inc(summed, 1)
                walk(pe, body, 2)
                pe.wait_ge(summed, (r + 1) * NT)
                pe.sem_inc(round_done, 1)
                pe.wait_ge(den_kept, r + 1)
                for pair in range(2):
                    wait(pe, scaled, 2 * r + pair)
                    for c in range(2):
                        last = pe.matmul(ps_misc[:, c * BANK:(c + 1) * BANK], pick[:, pair, :],
                                         inv_den(r)[:, c * BANK:(c + 1) * BANK], start=True, stop=True)
                    last.then_inc(den_spread, 1)


def dense(nc, m, x, w1, b1, w2, b2, w3, b3, w4, b4, x1_rows):
    x_sb = m.f32(64, NT, D)
    enc = m.f32(128, KT, N)
    w1_sb, w2_sb, w3_sb, w4_sb = m.f32(96, 4, 256), m.f32(100, 2, P), m.f32(101, 1, 256), m.f32(102, 2, D)
    y1, y2, y3 = m.f32(106, 2, BANK), m.f32(110, BANK), m.f32(112, 2, BANK)
    b1_sb, b2_sb, b3_sb, b4_sb = m.f32(116, 2), m.f32(116.125, 1), m.f32(116.25, 2), m.f32(117, D)
    with ExitStack() as ctx:
        def sem(name):
            return ctx.enter_context(nc.semaphore("C_" + name))

        x_in, w_in, b_in, biased = sem("x_in"), sem("w_in"), sem("b_in"), sem("biased")
        l1_done, l2_done, l3_done, l4_done = sem("l1_done"), sem("l2_done"), sem("l3_done"), sem("l4_done")
        y1_kept, y2_kept, y3_kept, x1_done = sem("y1_kept"), sem("y2_kept"), sem("y3_kept"), sem("x1_done")
        stats_done, stored = sem("stats_done"), sem("stored")
        block = ctx.enter_context(nc.Block())

        @block.sync
        def _(sp):
            sp.dma_start(w1_sb, w1.rearrange("(k p) n -> p k n", p=P)).then_inc(w_in, 16)
            sp.dma_start(w2_sb, w2.rearrange("(k p) n -> p k n", p=P)).then_inc(w_in, 16)
            sp.dma_start(w3_sb, w3.rearrange("(k p) n -> p k n", p=P)).then_inc(w_in, 16)
            sp.dma_start(w4_sb, w4.rearrange("(k p) n -> p k n", p=P)).then_inc(w_in, 16)
            sp.dma_start(x_sb, rows(x)).then_inc(x_in, 16)
            def turn(c):
                sp.wait_ge(x1_done, c * 4 + 4)
                sp.dma_start(rows(x1_rows)[:, bass.ts(c, 4), :], x_sb[:, bass.ts(c, 4), :]).then_inc(stored, 16)
            repeat(sp, 4, turn)
            sp.wait_ge(stored, 64)

        @block.gpsimd
        def _(pool):
            with nc.allow_non_contiguous_dma(reason="bias columns"):
                pool.dma_start(b1_sb, columns(b1)).then_inc(b_in, 16)
                pool.dma_start(b2_sb, columns(b2)).then_inc(b_in, 16)
                pool.dma_start(b3_sb, columns(b3)).then_inc(b_in, 16)
            pool.dma_start(b4_sb, on_all(b4)).then_inc(b_in, 16)
            pool.wait_ge(b_in, 64)
            pool.wait_ge(x_in, 16)
            def turn(t):
                pool.tensor_tensor(x_sb[:, t, :], x_sb[:, t, :], b4_sb, ALU.add).then_inc(biased, 1)
            repeat(pool, NT, turn)

        @block.scalar
        def _(act):
            act.wait_ge(b_in, 64)
            act.activation(m.scratch[:, 0:1], m.minus_half[:, :], ACT.Copy)
            def turn(c):
                for half in range(2):
                    wait(act, l2_done, c)
                    act.wait_ge(l1_done, c * 2 + half + 1)
                    act.activation(y1[:, half, :], m.bank(half), ACT.Relu, bias=b1_sb[:, half:half + 1]).then_inc(y1_kept, 1)
                wait(act, l3_done, c * 2)
                act.wait_ge(l2_done, c + 1)
                act.activation(y2, m.bank(2), ACT.Relu, bias=b2_sb).then_inc(y2_kept, 1)
                for half in range(2):
                    wait(act, l4_done, c * 4)
                    act.wait_ge(l3_done, c * 2 + half + 1)
                    act.activation(y3[:, half, :], m.bank(half), ACT.Relu, bias=b3_sb[:, half:half + 1]).then_inc(y3_kept, 1)
            repeat(act, 4, turn)

        @block.vector
        def _(dve):
            dve.wait_ge(biased, NT)
            def turn(c):
                for i in range(4):
                    dve.wait_ge(l4_done, c * 4 + i + 1)
                    dve.tensor_tensor(x_sb[:, c * 4 + i, :], x_sb[:, c * 4 + i, :], m.bank(3 + i), ALU.add).then_inc(x1_done, 1)
                    dve.wait_ge(x1_done, c * 4 + i + 1)
                    dve.bn_stats(m.stats[:, c * 4 + i, :], x_sb[:, c * 4 + i, :]).then_inc(stats_done, 1)
            repeat(dve, 4, turn)

        @block.tensor
        def _(pe):
            pe.wait_ge(w_in, 64)
            def turn(c):
                wait(pe, y3_kept, c * 2)
                for half in range(2):
                    for k in range(KT):
                        last = pe.matmul(m.bank(half), w1_sb[:, k, half * P:(half + 1) * P], enc[:, k, bass.ts(c, BANK)],
                                         start=k == 0, stop=k == KT - 1)
                    last.then_inc(l1_done, 1)
                pe.wait_ge(y1_kept, c * 2 + 2)
                wait(pe, y2_kept, c)
                for k in range(2):
                    last = pe.matmul(m.bank(2), w2_sb[:, k, :], y1[:, k, :], start=k == 0, stop=k == 1)
                last.then_inc(l2_done, 1)
                pe.wait_ge(y2_kept, c + 1)
                for half in range(2):
                    pe.matmul(m.bank(half), w3_sb[:, 0, half * P:(half + 1) * P], y2, start=True, stop=True).then_inc(l3_done, 1)
                pe.wait_ge(y3_kept, c * 2 + 2)
                wait(pe, x1_done, c * 4)
                for i in range(4):
                    for k in range(2):
                        last = pe.matmul(m.bank(3 + i), y3[:, k, i * P:(i + 1) * P], w4_sb[:, k, :], start=k == 0, stop=k == 1)
                    last.then_inc(l4_done, 1)
            repeat(pe, 4, turn)


def norm_constants(nc, m, name, extra_scale=None):
    step = m.norm
    with ExitStack() as ctx:
        variance = ctx.enter_context(nc.semaphore(name + "_variance"))
        power = ctx.enter_context(nc.semaphore(name + "_power"))
        dve_chain = ctx.enter_context(nc.semaphore(name + "_chain"))
        block = ctx.enter_context(nc.Block())

        @block.gpsimd
        def _(pool):
            pool.wait_ge(variance, 1)
            pool.tensor_tensor(step[:, 4, :], step[:, 2, :], m.minus_half[:, :].broadcast_to([P, NT]), ALU.pow).then_inc(power, 1)

        @block.vector
        def _(dve):
            chain = Chain(dve, dve_chain)
            row_constants(dve, chain, m.stats, step)
            dve.sem_inc(variance, 1)
            dve.wait_ge(power, 1)
            if extra_scale is not None:
                chain.link(dve.tensor_tensor(step[:, 4, :], step[:, 4, :], extra_scale, ALU.mult))
            chain.link(dve.scalar_tensor_tensor(step[:, 5, :], step[:, 3, :], -0.5, step[:, 4, :], ALU.mult, ALU.mult))


def queries(nc, m, t_w1, t_w2, t_w3, q_rows):
    h = m.f32(64, NT, D)
    parts = m.f16(96, NT, 2, D)
    keys, query = m.f32(128, N, parts=64), m.f32(136, N, parts=64)
    h_t, w1_t, w2_sb, ring = m.f32(144, 2, KT, P), m.f32(156, D, parts=64), m.f32(148, 64, parts=64), m.f32(150, 2, D)
    step = m.norm
    with ExitStack() as ctx:
        def sem(name):
            return ctx.enter_context(nc.semaphore("D_" + name))

        w_in, merged, merged_kept = sem("w_in"), sem("merged"), sem("merged_kept")
        ring_done, h_done, high_done, low_done = sem("ring_done"), sem("h_done"), sem("high_done"), sem("low_done")
        transposed, h_t_kept, qk_done, qk_kept = sem("transposed"), sem("h_t_kept"), sem("qk_done"), sem("qk_kept")
        q_stored = sem("q_stored")
        block = ctx.enter_context(nc.Block())
        ps_t, ps_qk = [m.bank(0), m.bank(1)], m.bank(2)

        @block.sync
        def _(sp):
            sp.dma_start(w1_t, t_w1).then_inc(w_in, 16)
            sp.dma_start(w2_sb, t_w2).then_inc(w_in, 16)
            sp.dma_start(m.qk_weight[:, :, 64:P], t_w3.rearrange("(k p) n -> p k n", p=P)).then_inc(w_in, 16)
            sp.wait_ge(qk_kept, 2 * NT)
            sp.dma_start(q_rows.rearrange("(t p) f -> p t f", p=P)[0:64, :, 0:P], query.rearrange("p (t n) -> p t n", n=P)).then_inc(q_stored, 16)
            sp.wait_ge(q_stored, 16)

        @block.scalar
        def _(act):
            act.activation(m.scratch[:, 0:1], m.minus_half[:, :], ACT.Copy)

            def tile(t, lane, group):
                wait(act, transposed, t - 1)
                wait(act, h_done, t - 1)
                scale, shift = column(step[:, 4, :], t), column(step[:, 5, :], t)
                act.activation(ring[:, lane, :], h[:, t, :], ACT.Relu, scale=scale, bias=shift).then_inc(ring_done, 1)
                act.activation(parts[:, t, 0, :], h[:, t, :], ACT.Relu, scale=scale, bias=shift).then_inc(high_done, 1)
            walk(act, tile, 2)

        @block.gpsimd
        def _(pool):
            def tile(t, lane, group):
                pool.wait_ge(ring_done, t + 1)
                pool.wait_ge(high_done, t + 1)
                pool.tensor_copy(h[:, t, :], ring[:, lane, :]).then_inc(h_done, 1)
            walk(pool, tile, 2)

        @block.vector
        def _(dve):
            dve.wait_ge(merged, 1)
            dve.tensor_scalar(m.qk_weight[:, :, 0:64], ps_t[0][:, 0:256].rearrange("p (k n) -> p k n", k=KT), 0.0, None,
                              ALU.add).then_inc(merged_kept, 1)

            def tile(t, lane, group):
                dve.wait_ge(transposed, t + 1)
                wait(dve, qk_done, t - 1)
                dve.tensor_scalar(h_t[:, lane, :, :].rearrange("p k n -> p (k n)"), ps_t[lane], 0.0, None, ALU.add).then_inc(h_t_kept, 1)
                dve.wait_ge(h_done, t + 1)
                dve.tensor_tensor(parts[:, t, 1, :], h[:, t, :], parts[:, t, 0, :], ALU.subtract).then_inc(low_done, 1)
                if not (isinstance(t, int) and t == 0):
                    keep(t - 1)

            def keep(t):
                dve.wait_ge(qk_done, t + 1)
                dve.tensor_scalar(query[:, bass.ts(t, P)], ps_qk[0:64, 0:P], 0.0, None, ALU.add).then_inc(qk_kept, 1)
                dve.tensor_scalar(keys[:, bass.ts(t, P)], ps_qk[64:P, 0:P], 0.0, None, ALU.add).then_inc(qk_kept, 1)
            walk(dve, tile, 2)
            keep(NT - 1)

        @block.tensor
        def _(pe):
            pe.wait_ge(w_in, 48)
            for k in range(KT):
                last = pe.matmul(ps_t[0][:, k * 64:(k + 1) * 64], w1_t[:, k * P:(k + 1) * P], w2_sb, start=True, stop=True)
            last.then_inc(merged, 1)
            pe.wait_ge(merged_kept, 1)

            def tile(t, lane, group):
                pe.wait_ge(ring_done, t + 1)
                wait(pe, h_t_kept, t - 1)
                for k in range(KT):
                    last = pe.transpose(ps_t[lane][:, k * P:(k + 1) * P], ring[:, lane, k * P:(k + 1) * P], m.eye[:, :])
                last.then_inc(transposed, 1)
                if not (isinstance(t, int) and t == 0):
                    multiply(t - 1, 1 - lane)

            def multiply(t, lane):
                pe.wait_ge(h_t_kept, t + 1)
                wait(pe, qk_kept, t * 2)
                for k in range(KT):
                    last = pe.matmul(ps_qk[:, 0:P], m.qk_weight[:, k, :], h_t[:, lane, k, :], start=k == 0, stop=k == KT - 1)
                last.then_inc(qk_done, 1)
            walk(pe, tile, 2)
            multiply(NT - 1, 1)


def diffuse(nc, m, s, u1, u2, q_in, q_out, xa_rows, xf_rows, y_in, y_out):
    xa = m.f32(64, NT, D)
    xf = m.f16(96, NT, 2, D)
    lo, hi_part = 64 * s, 64 * s + 64
    keys = m.f32(128, N)[lo:hi_part, :]
    next_keys = m.f32(128, N)[64:P, :]
    probs = [m.f32(136 + 8 * k, N) for k in range(3)]
    spare = m.f32(160, N)
    u1_sb, u2_sb = m.f32(168, KT, D), m.f32(176, KT, D)
    at = m.f32(184, 3, 4 * P)
    x_t, x_t2, xt, zt = m.f32(190, D), at[:, 1, :], m.f32(192, D), m.f32(194, D)
    halves, y_old = m.f16(196, 2, D), m.f32(196, D)
    q_ring = m.f32(198, 3, P)
    state = m.f32(199.5, 3, 16)
    wide = m.f32(199.5 + 0.1875, 8 * 8)
    junk_dve = m.scratch[:, 0:512].bitcast(I8)
    junk_act = m.scratch[:, 512:1024].bitcast(I8)
    table = m.stats[:, :, :].rearrange("p a b -> p (a b)")
    flags, flags_t = table[:, 0:32], table[:, 32:64]
    table_of_factors = m.norm[:, :, :].rearrange("p a b -> p (a b)")
    ratios = table_of_factors[:, 0:STEPS]
    half, nodes, p_top, minus_one = (table_of_factors[:, STEPS + k:STEPS + k + 1] for k in range(4))
    q_stage = q_ring[64:P, 0, :]
    scalar_steps, all_steps = SCALAR_HALVINGS[s], HALVINGS[s]
    pool_links, narrow_links = 11 * scalar_steps + 5, 4 * (STEPS - all_steps) + 7
    top8, sums8, cross8 = wide[:, 0:8], wide[:, 8:16], wide[:, 16:24]
    ones8 = m.ones[:, 0:8]
    below, s_hi, w, above8, s_above, sl, w_inv, count, kept, frac, corr, keep, flag, worst, neg_above, reached = (wide[:, 24 + k:25 + k] for k in range(16))
    quarter = wide[:, 40:44]
    verdict = wide[0:1, 44:45].bitcast(mybir.dt.int32)
    first_step = s == 0

    def of(lane, k):
        return state[:, lane, k:k + 1]
    NEG_MAX, TOTAL, TARGET, HI, CUT, CUT2, NEG_CUT, NEG_HI, RELUS, SIGNS, COUNTED, SUM, LACK, KEEP, LOWER, INV_NORM = range(16)

    with ExitStack() as ctx:
        def sem(name):
            return ctx.enter_context(nc.semaphore(f"E{s}_" + name))

        u_in, xa_in, xf_in, ready = sem("u_in"), sem("xa_in"), sem("xf_in"), sem("ready")
        q_landed = [sem(f"q_landed{k}") for k in range(3)]
        logits, maxed, exp_done, searched = sem("logits"), sem("maxed"), sem("exp_done"), sem("searched")
        half_passed, passed, pool_chain, lacking = sem("half_passed"), sem("passed"), sem("pool_chain"), sem("lacking")
        dve_chain, max_chain, fallback, cut_done, added = (sem("dve_chain"), sem("max_chain"), sem("fallback"), sem("cut_done"),
                                                           sem("added"))
        a_turned, at_kept, product, xa_kept, xa_stored = (sem("a_turned"), sem("at_kept"), sem("product"), sem("xa_kept"),
                                                          sem("xa_stored"))
        xt_turned, xt_kept, u_used, qk_done, qk_kept, q_stored = (sem("xt_turned"), sem("xt_kept"), sem("u_used"), sem("qk_done"),
                                                                  sem("qk_kept"), sem("q_stored"))
        spread, xf_kept, high_done, low_done, xf_stored = (sem("spread"), sem("xf_kept"), sem("high_done"), sem("low_done"),
                                                           sem("xf_stored"))
        z_kept, y_landed, y_done, y_stored = sem("z_kept"), sem("y_landed"), sem("y_done"), sem("y_stored")
        block = ctx.enter_context(nc.Block())
        ps_logits = m.bank(0, 4)
        ps_t, ps_x, ps_z = [m.bank(4), m.bank(5)], m.bank(6), m.bank(7)

        def turns(eng, turn):
            for t in (-1, 0, 1):
                turn(t, t % 3, (t + 2) // 3 + 1)
            with eng.Fori(0, 4) as g:
                for k in range(3):
                    turn(g * 3 + (k + 2), (k + 2) % 3, g + ((k + 4) // 3 + 1))
            for t in range(14, NT + 1):
                turn(t, t % 3, (t + 2) // 3 + 1)

        def exists(t, ahead):
            return not isinstance(t, int) or 0 <= t + ahead < NT

        @block.sync
        def _(sp):
            sp.wait_ge(q_landed[1], 16)
            sp.dma_start(u1_sb, u1.rearrange("(k p) n -> p k n", p=P)).then_inc(u_in, 16)
            sp.dma_start(u2_sb, u2.rearrange("(k p) n -> p k n", p=P)).then_inc(u_in, 16)

            def turn(t, lane, loads):
                if isinstance(t, int) and t == -1:
                    if not first_step:
                        sp.dma_start(xa, rows(xa_rows)).then_inc(xa_in, 16)
                        sp.dma_start(xf, xf_rows.rearrange("(t p) a f -> p t a f", p=P)).then_inc(xf_in, 16)
                    return
                if exists(t, -1):
                    if first_step:
                        sp.wait_ge(low_done, t)
                        sp.dma_start(xf_rows[tile_rows(t - 1), :, :], halves).then_inc(xf_stored, 16)
                        sp.wait_ge(xa_kept, t)
                        sp.dma_start(xa_rows[tile_rows(t - 1), :], xt).then_inc(xa_stored, 16)
                    else:
                        wait(sp, y_done, t - 1)
                        sp.dma_start(y_old, y_in[tile_rows(t - 1), :]).then_inc(y_landed, 16)
                    if first_step:
                        sp.wait_ge(qk_kept, t * 2)
                        sp.dma_start(queries_of(q_out, t - 1), q_stage).then_inc(q_stored, 16)
                    sp.wait_ge(y_done, t)
                    sp.dma_start(y_out[tile_rows(t - 1), :], zt).then_inc(y_stored, 16)
            turns(sp, turn)
            sp.wait_ge(y_stored, 16 * NT)
            if first_step:
                sp.wait_ge(q_stored, 16 * NT)
                sp.wait_ge(xa_stored, 16 * NT)
                sp.wait_ge(xf_stored, 16 * NT)

        @block.gpsimd
        def _(pool):
            per_tile = pool_links

            def turn(t, lane, loads):
                nxt = (lane + 1) % 3
                if exists(t, 1):
                    chain = Chain(pool, pool_chain, (t + 1) * per_tile)
                    pool.wait_ge(exp_done, t + 2)
                    chain.count(pool.tensor_tensor(of(nxt, TARGET), of(nxt, TOTAL), p_top, ALU.mult))
                    chain.count(pool.tensor_scalar(of(nxt, NEG_HI), of(nxt, TOTAL), 0.0, -1.0, ALU.mult, ALU.add))
                    chain.link(pool.tensor_scalar(of(nxt, NEG_CUT), of(nxt, TOTAL), 0.0, -halving(0), ALU.mult, ALU.add))
                    pool.sem_inc(searched, 1)
                if exists(t, -1):
                    pool.wait_ge(cut_done, t)
                    pool.tensor_tensor(probs[(lane - 1) % 3], probs[(lane - 1) % 3], spare, ALU.add).then_inc(added, 1)
                if exists(t, 1):
                    for k in range(scalar_steps):
                        pool.wait_ge(half_passed, (t + 1) * scalar_steps + (k + 1))
                        chain.link(pool.tensor_tensor(of(nxt, COUNTED), of(nxt, SIGNS), nodes, ALU.add))
                        chain.link(pool.tensor_tensor(of(nxt, COUNTED), of(nxt, COUNTED), of(nxt, NEG_CUT), ALU.mult))
                        chain.link(pool.tensor_tensor(of(nxt, COUNTED), of(nxt, COUNTED), half, ALU.mult))
                        chain.link(pool.tensor_tensor(of(nxt, COUNTED), of(nxt, COUNTED), of(nxt, TARGET), ALU.add))
                        pool.wait_ge(passed, (t + 1) * scalar_steps + (k + 1))
                        chain.link(pool.tensor_tensor(of(nxt, LACK), of(nxt, COUNTED), of(nxt, RELUS), ALU.subtract))
                        pool.sem_inc(lacking, 1)
                        chain.count(pool.tensor_scalar(of(nxt, KEEP), of(nxt, LACK), 0.0, None, ALU.is_le))
                        chain.link(pool.tensor_scalar(of(nxt, LOWER), of(nxt, LACK), 0.0, None, ALU.is_gt))
                        chain.count(pool.tensor_tensor(of(nxt, KEEP), of(nxt, KEEP), of(nxt, NEG_HI), ALU.mult))
                        chain.link(pool.tensor_tensor(of(nxt, LOWER), of(nxt, LOWER), of(nxt, NEG_CUT), ALU.mult))
                        chain.link(pool.tensor_tensor(of(nxt, NEG_HI), of(nxt, KEEP), of(nxt, LOWER), ALU.add))
                        chain.link(pool.tensor_tensor(of(nxt, NEG_CUT), of(nxt, NEG_HI), ratios[:, k + 1:k + 2], ALU.mult))
                        if k + 1 < scalar_steps:
                            pool.sem_inc(searched, 1)
                        if k == 1 and first_step and exists(t, -1):
                            pool.wait_ge(high_done, t)
                            pool.tensor_tensor(halves[:, 1, :], xt, halves[:, 0, :], ALU.subtract).then_inc(low_done, 1)
                    chain.count(pool.tensor_tensor(of(nxt, HI), of(nxt, NEG_HI), minus_one, ALU.mult))
                    chain.link(pool.tensor_tensor(of(nxt, CUT), of(nxt, NEG_CUT), minus_one, ALU.mult))
                    pool.sem_inc(searched, 1)
                    assert chain.n == pool_links
                elif first_step and exists(t, -1):
                    pool.wait_ge(high_done, t)
                    pool.tensor_tensor(halves[:, 1, :], xt, halves[:, 0, :], ALU.subtract).then_inc(low_done, 1)
                if exists(t, -1):
                    pool.wait_ge(z_kept, t)
                    if first_step:
                        pool.tensor_tensor(zt, zt, xa[:, t - 1, :], ALU.add).then_inc(y_done, 1)
                    else:
                        pool.wait_ge(y_landed, t * 16)
                        pool.tensor_tensor(zt, zt, y_old, ALU.add).then_inc(y_done, 1)
            pool.wait_ge(ready, 2)
            turns(pool, turn)

        @block.vector
        def _(dve):
            links = [0]

            def row_max(t, lane):
                dve.wait_ge(logits, t + 1)
                dve.tensor_reduce(of(lane, SUM), ps_logits, AXIS.X, ALU.max).then_inc(max_chain, 1)
                dve.wait_ge(max_chain, t + 1)
                dve.tensor_scalar(of(lane, NEG_MAX), of(lane, SUM), -1.0, None, ALU.mult).then_inc(maxed, 1)

            def halve(chain, e, old, new, hi, target, keep, factor):
                chain.link(dve.scalar_tensor_tensor(junk_dve, e, old, e, ALU.is_gt, ALU.mult, accum_out=below))
                chain.link(dve.tensor_scalar(keep, below, target, hi, ALU.is_ge, ALU.mult))
                chain.count(dve.tensor_scalar(new, keep, old, factor, ALU.max, ALU.mult))
                chain.wait()
                chain.count(dve.tensor_scalar(hi, keep, old, None, ALU.max))

            def refine(t, lane):
                e, target, hi = probs[lane], of(lane, TARGET), of(lane, HI)
                base = t * links[0]
                chain = Chain(dve, dve_chain, base)
                dve.wait_ge(searched, (t + 1) * (scalar_steps + 1))
                for k in range(scalar_steps, all_steps):
                    old, new = (CUT, CUT2) if (k - scalar_steps) % 2 == 0 else (CUT2, CUT)
                    halve(chain, e, of(lane, old), of(lane, new), hi, target, keep, halving(k + 1))
                    if k == all_steps - 1 and exists(t, 2):
                        row_max(t + 2, (lane + 2) % 3)
                wait(dve, added, t)
                chain.wait()
                chain.count(dve.scalar_tensor_tensor(spare, e, hi, e, ALU.is_le, ALU.mult, accum_out=below))
                chain.wait()
                chain.count(dve.tensor_tensor(s_hi, of(lane, TOTAL), below, ALU.subtract))
                chain.count(dve.max(top8, spare))
                chain.wait()
                chain.link(dve.tensor_tensor_scan(sums8, ones8, top8, s_hi, ALU.mult, ALU.add))
                chain.link(dve.scalar_tensor_tensor(cross8, sums8, target, top8, ALU.is_ge, ALU.mult))
                chain.link(dve.tensor_reduce(w, cross8, AXIS.X, ALU.max))
                chain.link(dve.tensor_tensor(w, w, top8[:, 7:8], ALU.max))
                chain.link(dve.scalar_tensor_tensor(cross8, top8, w, top8, ALU.is_gt, ALU.mult, accum_out=above8))
                chain.count(dve.tensor_tensor(s_above, s_hi, above8, ALU.add))
                chain.link(dve.scalar_tensor_tensor(spare, e, w, e, ALU.is_ge, ALU.mult, accum_out=sl))
                chain.count(dve.tensor_scalar(flag, target, 1.0 - 2e-6, None, ALU.mult))
                chain.link(dve.tensor_tensor(reached, sl, sums8[:, 7:8], ALU.max))
                chain.link(dve.tensor_tensor(flags[:, 0:1], reached, flag, ALU.is_lt))
                chain.link(dve.transpose(flags_t, flags))
                chain.link(dve.tensor_reduce(worst, flags_t, AXIS.X, ALU.max))
                for k in range(4):
                    chain.count(dve.tensor_scalar(quarter[0:1, k:k + 1], worst[32 * k:32 * k + 1, :], 1.0, None, ALU.mult))
                chain.wait()
                chain.link(dve.tensor_reduce(verdict, quarter[0:1, :], AXIS.X, ALU.max))
                dve.tensor_scalar(quarter[0:1, 0:1], quarter[0:1, 0:1], 1.0, None, ALU.mult)
                missing = dve.value_load(verdict, min_val=0, max_val=1)
                with dve.If(missing > 0):
                    narrow(t, e, target, hi)
                with dve.Else():
                    dve.sem_inc(fallback, narrow_links)
                dve.wait_ge(fallback, t * narrow_links + narrow_links)
                chain.link(dve.reciprocal(w_inv, w))
                chain.link(dve.tensor_tensor(count, sl, s_above, ALU.subtract))
                round_up = 1.5 * 2 ** 23
                chain.link(dve.tensor_scalar(count, count, w_inv, round_up, ALU.mult, ALU.add))
                chain.link(dve.tensor_scalar(count, count, -round_up, 1.0, ALU.add, ALU.max))
                chain.link(dve.tensor_scalar(neg_above, count, w, sl, ALU.mult, ALU.subtract))
                chain.count(dve.reciprocal(frac, count))
                chain.link(dve.tensor_tensor(kept, target, neg_above, ALU.add))
                chain.link(dve.tensor_scalar(kept, kept, w_inv, 0.4999, ALU.mult, ALU.add))
                chain.link(dve.tensor_scalar(kept, kept, round_up, None, ALU.add))
                chain.link(dve.tensor_scalar(kept, kept, -round_up, 1.0, ALU.add, ALU.max))
                chain.link(dve.tensor_tensor(kept, kept, count, ALU.min))
                chain.count(dve.tensor_scalar(of(lane, INV_NORM), kept, w, neg_above, ALU.mult, ALU.subtract))
                chain.link(dve.tensor_tensor(frac, kept, frac, ALU.mult))
                chain.count(dve.reciprocal(of(lane, INV_NORM), of(lane, INV_NORM)))
                chain.link(dve.tensor_scalar(corr, frac, -1.0, w, ALU.add, ALU.mult))
                dve.tensor_scalar(e, spare, w, corr, ALU.is_equal, ALU.mult).then_inc(cut_done, 1)
                if not links[0]:
                    links[0] = chain.n
                assert links[0] == chain.n

            def narrow(t, e, target, hi):
                chain = Chain(dve, fallback, t * narrow_links)
                chain.count(dve.tensor_scalar(w, hi, 0.0, None, ALU.add))
                with dve.Fori(0, STEPS - all_steps) as k:
                    inner = Chain(dve, fallback, t * narrow_links + (k * 4 + 1))
                    inner.wait()
                    inner.link(dve.tensor_scalar(corr, w, column(ratios, k + all_steps), None, ALU.mult))
                    inner.link(dve.scalar_tensor_tensor(junk_dve, e, corr, e, ALU.is_gt, ALU.mult, accum_out=below))
                    inner.link(dve.tensor_scalar(keep, below, target, w, ALU.is_ge, ALU.mult))
                    inner.count(dve.tensor_scalar(w, keep, corr, None, ALU.max))
                    assert inner.n == 4
                chain.n += 4 * (STEPS - all_steps)
                chain.wait()
                chain.link(dve.tensor_scalar(corr, w, math.exp(-SEARCH / 2 ** STEPS - 6e-7), None, ALU.mult))
                chain.link(dve.tensor_scalar(spare, e, corr, None, ALU.is_gt))
                chain.link(dve.scalar_tensor_tensor(spare, e, w, spare, ALU.is_le, ALU.mult))
                chain.link(dve.scalar_tensor_tensor(e, spare, w, e, ALU.mult, ALU.max))
                chain.link(dve.scalar_tensor_tensor(junk_dve, e, w, e, ALU.is_gt, ALU.mult, accum_out=s_above))
                chain.count(dve.scalar_tensor_tensor(spare, e, w, e, ALU.is_ge, ALU.mult, accum_out=sl))
                assert chain.n == narrow_links

            def turn(t, lane, loads):
                if isinstance(t, int) and t == -1:
                    for k in range(STEPS):
                        dve.memset(ratios[:, k:k + 1], halving(k))
                    dve.memset(half, 0.5)
                    dve.memset(nodes, float(N))
                    dve.memset(p_top, P_TOP)
                    last = dve.memset(minus_one, -1.0)
                    last.then_inc(ready, 1)
                    dve.memset(flags, 0.0).then_inc(ready, 1)
                    dve.wait_ge(ready, 2)
                    row_max(0, 0)
                    row_max(1, 1)
                elif exists(t, 0):
                    refine(t, lane)
            turns(dve, turn)

        @block.scalar
        def _(act):
            act.activation(xt[:, 0:1], m.minus_half[:, :], ACT.Exp)

            def load_q(t, lane):
                act.dma_start(q_ring[lo:hi_part, lane, :], queries_of(q_in, t)).then_inc(q_landed[lane], 16)
            load_q(0, 0)
            load_q(1, 1)

            def turn(t, lane, loads):
                nxt = (lane + 1) % 3
                if exists(t, 2) and exists(t, 0):
                    wait(act, logits, t)
                    load_q(t + 2, (lane + 2) % 3)

                def halve(k, which=(0, 1)):
                    if not exists(t, 1) or k >= scalar_steps:
                        return
                    if 0 in which:
                        act.wait_ge(searched, (t + 1) * (scalar_steps + 1) + (k + 1))
                        act.activation(junk_act, probs[nxt], ACT.Sign, bias=of(nxt, NEG_CUT), accum_out=of(nxt, SIGNS)).then_inc(half_passed, 1)
                    if 1 in which:
                        act.wait_ge(half_passed, (t + 1) * scalar_steps + (k + 1))
                        act.activation(junk_act, probs[nxt], ACT.Relu, bias=of(nxt, NEG_CUT), accum_out=of(nxt, RELUS)).then_inc(passed, 1)

                if exists(t, 1):
                    act.wait_ge(maxed, t + 2)
                    wait(act, a_turned, (t - 1) * 4)
                    act.activation(probs[nxt], ps_logits, ACT.Exp, bias=of(nxt, NEG_MAX), accum_out=of(nxt, TOTAL)).then_inc(exp_done, 1)
                halve(0)
                if not exists(t, -1):
                    for k in range(1, scalar_steps):
                        halve(k)
                    return
                before = (lane - 1) % 3

                def keep_at(g):
                    act.wait_ge(a_turned, (t - 1) * 4 + (g + 1))
                    if g == 3:
                        act.wait_ge(product, (t - 1) * 4 + 1)
                    act.activation(at[:, g % 3, :], ps_t[g % 2], ACT.Copy).then_inc(at_kept, 1)
                act.wait_ge(spread, t)
                if first_step:
                    wait(act, xa_stored, (t - 1) * 16)
                act.activation(xt, ps_x, ACT.Copy, scale=column(m.inv_degree[:, :], t - 1)).then_inc(xf_kept, 1)
                if first_step:
                    act.wait_ge(xf_kept, t)
                    wait(act, xf_stored, (t - 1) * 16)
                    act.activation(halves[:, 0, :], xt, ACT.Copy).then_inc(high_done, 1)
                keep_at(0)
                keep_at(1)
                halve(1, (0,))
                keep_at(2)
                halve(1, (1,))
                keep_at(3)
                halve(2)
                act.wait_ge(xt_turned, t * 2 - 1)
                act.activation(x_t, ps_t[0], ACT.Copy).then_inc(xt_kept, 1)
                for k in range(3, scalar_steps - 1):
                    halve(k)
                act.wait_ge(product, (t - 1) * 4 + 4)
                if first_step:
                    act.wait_ge(low_done, t)
                act.activation(xt, ps_x, ACT.Copy, scale=of(before, INV_NORM)).then_inc(xa_kept, 1)
                act.wait_ge(xt_turned, t * 2)
                act.activation(x_t2, ps_t[1], ACT.Copy).then_inc(xt_kept, 1)
                halve(scalar_steps - 1, (0,))
                if first_step:
                    act.wait_ge(qk_done, t)
                    act.activation(next_keys[:, tile_rows(t - 1)], ps_t[0][64:P, 0:P], ACT.Copy).then_inc(qk_kept, 1)
                    wait(act, q_stored, (t - 1) * 16)
                    act.activation(q_stage, ps_t[0][0:64, 0:P], ACT.Copy).then_inc(qk_kept, 1)
                act.wait_ge(u_used, t * 2)
                wait(act, y_stored, (t - 1) * 16)
                act.activation(zt, ps_z, ACT.Copy).then_inc(z_kept, 1)
                halve(scalar_steps - 1, (1,))
            turns(act, turn)

        @block.tensor
        def _(pe):
            def make_logits(t, lane, loads):
                pe.wait_ge(q_landed[lane], loads * 16)
                wait(pe, exp_done, t)
                for c in range(4):
                    last = pe.matmul(ps_logits[:, c * BANK:(c + 1) * BANK], q_ring[lo:hi_part, lane, :],
                                     keys[:, c * BANK:(c + 1) * BANK], start=True, stop=True)
                last.then_inc(logits, 1)

            def turn(t, lane, loads):
                if isinstance(t, int) and t == -1:
                    make_logits(0, 0, 1)
                    make_logits(1, 1, 1)
                    return
                if isinstance(t, int) and t == 0:
                    if not first_step:
                        pe.wait_ge(xa_in, 16)
                        pe.wait_ge(xf_in, 16)
                    make_logits(2, 2, 1)
                    pe.wait_ge(u_in, 32)
                    return
                weights = probs[(lane - 1) % 3]

                def turn_a(g):
                    if g >= 2:
                        pe.wait_ge(at_kept, (t - 1) * 4 + (g - 1))
                    for j in range(4):
                        block_of = slice((4 * g + j) * P, (4 * g + j + 1) * P)
                        last = pe.transpose(ps_t[g % 2][:, j * P:(j + 1) * P], weights[:, block_of], m.eye[:, :])
                    last.then_inc(a_turned, 1)

                def multiply(g):
                    pe.wait_ge(at_kept, (t - 1) * 4 + (g + 1))
                    for j in range(4):
                        last = pe.matmul(ps_x, at[:, g % 3, j * P:(j + 1) * P], xa[:, 4 * g + j, :],
                                         start=g == 0 and j == 0, stop=g == 3 and j == 3)
                    last.then_inc(product, 1)

                wait(pe, xa_kept, t - 1)
                for k in range(2):
                    pe.matmul(ps_x, m.eye16[:, :], xf[:, t - 1, k, :], start=k == 0, stop=False)
                for j in range(NT):
                    for k in range(2):
                        last = pe.matmul(ps_x, m.adj_t[:, j, tile_rows(t - 1)], xf[:, j, k, :], start=False,
                                         stop=j == NT - 1 and k == 1)
                last.then_inc(spread, 1)
                if exists(t, 2):
                    make_logits(t + 2, (lane + 2) % 3, loads)
                pe.wait_ge(added, t)
                wait(pe, xt_kept, (t - 1) * 2)
                if first_step:
                    wait(pe, qk_kept, (t - 1) * 2)
                turn_a(0)
                turn_a(1)
                turn_a(2)
                pe.wait_ge(xf_kept, t)
                multiply(0)
                turn_a(3)
                multiply(1)
                pe.wait_ge(at_kept, (t - 1) * 4 + 3)
                for k in range(KT):
                    last = pe.transpose(ps_t[0][:, k * P:(k + 1) * P], xt[:, k * P:(k + 1) * P], m.eye[:, :])
                last.then_inc(xt_turned, 1)
                multiply(2)
                multiply(3)
                pe.wait_ge(xt_kept, t * 2 - 1)
                wait(pe, z_kept, t - 1)
                for k in range(KT):
                    last = pe.matmul(ps_z, x_t[:, k * P:(k + 1) * P], u1_sb[:, k, :], start=k == 0, stop=False)
                last.then_inc(u_used, 1)
                pe.wait_ge(xa_kept, t)
                for k in range(KT):
                    last = pe.transpose(ps_t[1][:, k * P:(k + 1) * P], xt[:, k * P:(k + 1) * P], m.eye[:, :])
                last.then_inc(xt_turned, 1)
                pe.wait_ge(xt_kept, t * 2)
                if first_step:
                    for k in range(KT):
                        last = pe.matmul(ps_t[0][:, 0:P], m.qk_weight[:, k, :], x_t2[:, k * P:(k + 1) * P], start=k == 0, stop=k == KT - 1)
                    last.then_inc(qk_done, 1)
                for k in range(KT):
                    last = pe.matmul(ps_z, x_t2[:, k * P:(k + 1) * P], u2_sb[:, k, :], start=False, stop=k == KT - 1)
                last.then_inc(u_used, 1)
            turns(pe, turn)


def close_diffusion(nc, m, y_rows, x1_rows, x2_rows, gamma, beta):
    y, x = m.f32(64, NT, D), m.f32(96, NT, D)
    gamma_sb, beta_sb = m.f32(192, D), m.f32(194, D)
    step = m.norm
    with ExitStack() as ctx:
        def sem(name):
            return ctx.enter_context(nc.semaphore("F_" + name))

        y_in, x_in, g_in, stats_done = [sem(f"y_in{c}") for c in range(4)], sem("x_in"), sem("g_in"), sem("stats_done")
        block = ctx.enter_context(nc.Block())

        @block.sync
        def _(sp):
            for c in range(4):
                sp.dma_start(y[:, 4 * c:4 * c + 4, :], rows(y_rows)[:, 4 * c:4 * c + 4, :]).then_inc(y_in[c], 16)
            sp.dma_start(x, rows(x1_rows)).then_inc(x_in, 16)
            sp.dma_start(gamma_sb, on_all(gamma)).then_inc(g_in, 16)
            sp.dma_start(beta_sb, on_all(beta)).then_inc(g_in, 16)
            sp.wait_ge(x_in, 16)
            sp.wait_ge(g_in, 32)

        @block.vector
        def _(dve):
            measure_chunks(dve, y, y_in, m.stats, stats_done)
    norm_constants(nc, m, "F1")
    with ExitStack() as ctx:
        def sem(name):
            return ctx.enter_context(nc.semaphore("G_" + name))

        centred, scaled, shifted, x_done, stats_done, x_stored = (sem("centred"), sem("scaled"), sem("shifted"), sem("x_done"),
                                                                  sem("stats_done"), sem("x_stored"))
        block = ctx.enter_context(nc.Block())

        @block.scalar
        def _(act):
            act.activation(m.scratch[:, 0:1], m.minus_half[:, :], ACT.Identity)
            def turn(t):
                act.activation(y[:, t, :], y[:, t, :], ACT.Identity, scale=column(step[:, 4, :], t),
                               bias=column(step[:, 5, :], t)).then_inc(centred, 1)
            repeat(act, NT, turn)

        @block.gpsimd
        def _(pool):
            def turn(t):
                pool.tensor_tensor(x[:, t, :], x[:, t, :], beta_sb, ALU.add).then_inc(shifted, 1)
            repeat(pool, NT, turn)

        @block.vector
        def _(dve):
            def scale(t):
                dve.wait_ge(centred, t + 1)
                dve.tensor_tensor(y[:, t, :], y[:, t, :], gamma_sb, ALU.mult).then_inc(scaled, 1)

            def add(t):
                dve.wait_ge(scaled, t + 1)
                dve.wait_ge(shifted, t + 1)
                dve.tensor_tensor(x[:, t, :], x[:, t, :], y[:, t, :], ALU.add).then_inc(x_done, 1)

            def measure(t):
                dve.wait_ge(x_done, t + 1)
                dve.bn_stats(m.stats[:, t, :], x[:, t, :]).then_inc(stats_done, 1)
            scale(0)
            scale(1)
            add(0)
            with dve.Fori(2, NT) as t:
                scale(t)
                add(t - 1)
                measure(t - 2)
            add(NT - 1)
            measure(NT - 2)
            measure(NT - 1)

        @block.sync
        def _(sp):
            def turn(c):
                sp.wait_ge(x_done, c * 4 + 4)
                sp.dma_start(rows(x2_rows)[:, bass.ts(c, 4), :], x[:, bass.ts(c, 4), :]).then_inc(x_stored, 16)
            repeat(sp, 4, turn)
            sp.wait_ge(x_stored, 64)
    norm_constants(nc, m, "F2", m.inv_sqrt_degree[:, :])
    normed_halves(nc, m, "F3", x)


def normed_halves(nc, m, name, x):
    halves, ring = m.f16(128, NT, 2, D), m.f32(192, 2, D)
    step = m.norm
    with ExitStack() as ctx:
        full, high, low = (ctx.enter_context(nc.semaphore(name + s)) for s in ("_full", "_high", "_low"))
        block = ctx.enter_context(nc.Block())

        @block.scalar
        def _(act):
            act.activation(m.scratch[:, 0:1], m.minus_half[:, :], ACT.Relu)

            def tile(t, lane, group):
                scale, shift = column(step[:, 4, :], t), column(step[:, 5, :], t)
                wait(act, low, t - 1)
                act.activation(ring[:, lane, :], x[:, t, :], ACT.Relu, scale=scale, bias=shift).then_inc(full, 1)
                act.activation(halves[:, t, 0, :], x[:, t, :], ACT.Relu, scale=scale, bias=shift).then_inc(high, 1)
            walk(act, tile, 2)

        @block.vector
        def _(dve):
            def tile(t, lane, group):
                dve.wait_ge(full, t + 1)
                dve.wait_ge(high, t + 1)
                dve.tensor_tensor(halves[:, t, 1, :], ring[:, lane, :], halves[:, t, 0, :], ALU.subtract).then_inc(low, 1)
            walk(dve, tile, 2)


def symmetrise_and_spread(nc, m, adj):
    mean, source = m.f16(64, NT, N), m.f16(128, NT, 2, D)
    adj_in, spread = m.f32(160, 4, N), m.f16(160, NT, 2, D)
    ring = m.f32(192, 2, D)
    banks = 8
    with ExitStack() as ctx:
        def sem(name):
            return ctx.enter_context(nc.semaphore("H_" + name))

        landed = [sem(f"landed{k}") for k in range(4)]
        added, halved, summed, kept, high, low = (sem("added"), sem("halved"), sem("summed"), sem("kept"), sem("high"), sem("low"))
        block = ctx.enter_context(nc.Block())

        @block.sync
        def _(sp):
            def tile(t, lane, group):
                wait(sp, added, t - 3)
                sp.dma_start(adj_in[:, lane, :], adj[bass.ts(t, P), :]).then_inc(landed[lane], 16)
            walk(sp, tile, 4)

        @block.tensor
        def _(pe):
            def start(t, bank):
                for k in range(2):
                    pe.matmul(m.bank(bank), m.eye16[:, :], source[:, t, k, :], start=k == 0, stop=False)

            for t in range(banks):
                start(t, t)

            def take(j):
                pe.wait_ge(halved, j + 1)
                for t in range(banks):
                    for k in range(2):
                        last = pe.matmul(m.bank(t), mean[:, j, t * P:(t + 1) * P], source[:, j, k, :], start=False,
                                         stop=isinstance(j, int) and j == NT - 1 and k == 1)
                    if isinstance(j, int) and j == NT - 1:
                        last.then_inc(summed, 1)
            with pe.Fori(0, NT - 1) as j:
                take(j)
            take(NT - 1)

            def whole(t, bank, kept_before):
                pe.wait_ge(kept, kept_before)
                start(t, bank)
                for j in range(NT):
                    for k in range(2):
                        last = pe.matmul(m.bank(bank), mean[:, j, bass.ts(t, P)], source[:, j, k, :], start=False,
                                         stop=j == NT - 1 and k == 1)
                last.then_inc(summed, 1)
            for lane in range(2):
                whole(banks + lane, lane, lane + 1)
            with pe.Fori(banks // 2 + 1, NT // 2) as i:
                for lane in range(2):
                    whole(i * 2 + lane, lane, i * 2 + (lane - 1))

        @block.scalar
        def _(act):
            act.activation(m.scratch[:, 0:1], m.minus_half[:, :], ACT.Copy)

            def halve(t):
                act.wait_ge(added, t + 1)
                act.activation(mean[:, t, :], mean[:, t, :], ACT.Copy, scale=0.5).then_inc(halved, 1)
            repeat(act, NT, halve)

            def keep(t, lane, bank):
                wait(act, low, t - 1)
                act.wait_ge(summed, t + 1)
                act.activation(ring[:, lane, :], m.bank(bank), ACT.Copy, scale=column(m.inv_sqrt_degree[:, :], t)).then_inc(kept, 1)
                act.wait_ge(kept, t + 1)
                act.activation(spread[:, t, 0, :], ring[:, lane, :], ACT.Copy).then_inc(high, 1)
            for t in range(banks):
                keep(t, t % 2, t)
            with act.Fori(banks // 2, NT // 2) as i:
                for lane in range(2):
                    keep(i * 2 + lane, lane, lane)

        @block.vector
        def _(dve):
            def add(t, lane, group):
                dve.wait_ge(landed[lane], (group + 1) * 16)
                dve.tensor_tensor(mean[:, t, :], adj_in[:, lane, :], m.adj_t[:, t, :], ALU.add).then_inc(added, 1)
            walk(dve, add, 4)

            def low_half(t, lane, group):
                dve.wait_ge(high, t + 1)
                dve.tensor_tensor(spread[:, t, 1, :], ring[:, lane, :], spread[:, t, 0, :], ALU.subtract).then_inc(low, 1)
            walk(dve, low_half, 2)


def propagate(nc, m, x2_rows, c_weight, c_bias):
    spread = m.f16(160, NT, 2, D)
    x = m.f32(64, NT, D)
    with ExitStack() as ctx:
        x_in, w_in, summed, x_done, stats_done = (ctx.enter_context(nc.semaphore("J_" + s))
                                                  for s in ("x_in", "w_in", "summed", "x_done", "stats_done"))
        block = ctx.enter_context(nc.Block())

        @block.sync
        def _(sp):
            sp.dma_start(x, rows(x2_rows)).then_inc(x_in, 16)
            sp.wait_ge(x_in, 16)
            w_sb, bias_sb = convolve_constants(m)
            sp.dma_start(w_sb, c_weight.rearrange("(k p) n -> p k n", p=P)).then_inc(w_in, 16)
            sp.dma_start(bias_sb, on_all(c_bias)).then_inc(w_in, 16)
            sp.wait_ge(w_in, 32)

        @block.tensor
        def _(pe):
            def tile(t, lane, group):
                wait(pe, x_done, t - 1)
                for j in range(NT):
                    for k in range(2):
                        last = pe.matmul(m.bank(lane), m.adj_t[:, j, bass.ts(t, P)], spread[:, j, k, :],
                                         start=j == 0 and k == 0, stop=j == NT - 1 and k == 1)
                last.then_inc(summed, 1)
            walk(pe, tile, 2)

        @block.vector
        def _(dve):
            dve.wait_ge(x_in, 16)

            def tile(t, lane, group):
                dve.wait_ge(summed, t + 1)
                dve.tensor_tensor(x[:, t, :], x[:, t, :], m.bank(lane), ALU.add).then_inc(x_done, 1)
                dve.wait_ge(x_done, t + 1)
                dve.bn_stats(m.stats[:, t, :], x[:, t, :]).then_inc(stats_done, 1)
            walk(dve, tile, 2)
    norm_constants(nc, m, "K1")
    normed_halves(nc, m, "K2", x)


def convolve_constants(m):
    return m.f32(96, KT, D), m.f32(104, D)


def convolve(nc, m, out):
    x, source = m.f32(64, NT, D), m.f16(128, NT, 2, D)
    w_sb, bias_sb = convolve_constants(m)
    sums, sums_t, result = m.f32(106, 2, D), m.f32(110, 2, D), m.f32(114, 2, D)
    with ExitStack() as ctx:
        def sem(name):
            return ctx.enter_context(nc.semaphore("L_" + name))

        summed, sums_kept, turned, turned_kept = sem("summed"), sem("sums_kept"), sem("turned"), sem("turned_kept")
        multiplied, biased, result_done, stored = sem("multiplied"), sem("biased"), sem("result_done"), [sem(f"stored{k}") for k in range(2)]
        block = ctx.enter_context(nc.Block())

        @block.sync
        def _(sp):
            def tile(t, lane, group):
                sp.wait_ge(result_done, t + 1)
                sp.dma_start(out[bass.ts(t, P), :], result[:, lane, :]).then_inc(stored[lane], 16)
            walk(sp, tile, 2)
            for lane in range(2):
                sp.wait_ge(stored[lane], NT // 2 * 16)

        @block.gpsimd
        def _(pool):
            def turn(t):
                pool.tensor_tensor(x[:, t, :], x[:, t, :], bias_sb, ALU.add).then_inc(biased, 1)
            repeat(pool, NT, turn)

        @block.tensor
        def _(pe):
            def gather(t, lane):
                wait(pe, sums_kept, t - 1)
                for j in range(NT):
                    for k in range(2):
                        last = pe.matmul(m.bank(lane), m.adj_t[:, j, bass.ts(t, P)], source[:, j, k, :],
                                         start=j == 0 and k == 0, stop=j == NT - 1 and k == 1)
                last.then_inc(summed, 1)

            def project_sums(t, lane):
                pe.wait_ge(sums_kept, t + 1)
                wait(pe, turned_kept, t - 1)
                for k in range(KT):
                    last = pe.transpose(m.bank(2 + lane)[:, k * P:(k + 1) * P], sums[:, lane, k * P:(k + 1) * P], m.eye[:, :])
                last.then_inc(turned, 1)
                pe.wait_ge(turned_kept, t + 1)
                wait(pe, result_done, t - 1)
                for k in range(KT):
                    last = pe.matmul(m.bank(4 + lane), sums_t[:, lane, k * P:(k + 1) * P], w_sb[:, k, :], start=k == 0, stop=k == KT - 1)
                last.then_inc(multiplied, 1)

            gather(0, 0)
            gather(1, 1)
            project_sums(0, 0)
            with pe.Fori(0, NT // 2 - 1) as i:
                gather(i * 2 + 2, 0)
                project_sums(i * 2 + 1, 1)
                gather(i * 2 + 3, 1)
                project_sums(i * 2 + 2, 0)
            project_sums(NT - 1, 1)

        @block.scalar
        def _(act):
            act.activation(m.scratch[:, 0:1], m.minus_half[:, :], ACT.Copy)

            def tile(t, lane, group):
                act.wait_ge(summed, t + 1)
                wait(act, turned, t - 1)
                act.activation(sums[:, lane, :], m.bank(lane), ACT.Copy).then_inc(sums_kept, 1)
            walk(act, tile, 2)

        @block.vector
        def _(dve):
            def tile(t, lane, group):
                dve.wait_ge(turned, t + 1)
                wait(dve, multiplied, t - 1)
                dve.tensor_scalar(sums_t[:, lane, :], m.bank(2 + lane), 0.0, None, ALU.add).then_inc(turned_kept, 1)
                dve.wait_ge(multiplied, t + 1)
                dve.wait_ge(biased, t + 1)
                wait(dve, stored[lane], group * 16)
                dve.tensor_tensor(result[:, lane, :], m.bank(4 + lane), x[:, t, :], ALU.add).then_inc(result_done, 1)
            walk(dve, tile, 2)


def d_at(columns_of, t, head):
    if isinstance(t, int):
        return columns_of[:, t, head:head + 1]
    return columns_of[:, bass.ds(t, 1), head:head + 1].rearrange("p a h -> p (a h)")


def clear_counts(nc, free):
    with nc.Block() as block:
        @block.gpsimd
        def _(pool):
            pool.sem_clear(range(min(free), max(free) + 1))


def program(nc, x, adj, adj_t, g_w, g_a1, g_a2, g_w1, g_b1, g_w2, g_b2, g_w3, g_b3, g_w4, g_b4,
            t_w1, t_w2, t_w3, u1_0, u1_1, u2_0, u2_1, gamma, beta, c_w, c_b, out):
    with ExitStack() as ctx:
        m = Memory(nc, ctx)
        free = list(nc.free_semaphores)
        constants(nc, m)
        def spill(name, *shape, dt=F32):
            return nc.dram_tensor(name, shape, dt, kind="Internal").ap()

        u_rows, x1_rows, x2_rows = spill("u_rows", H, N), spill("x1_rows", N, D), spill("x2_rows", N, D)
        y1_rows, y2_rows, xa_rows = spill("y1_rows", N, D), spill("y2_rows", N, D), spill("xa_rows", N, D)
        xf_rows = spill("xf_rows", N, 2, D, dt=F16)
        q0_rows, q1_rows = spill("q0_rows", N, D), spill("q1_rows", N, D)
        project(nc, m, x, adj_t, g_w, g_a1, g_a2, u_rows)
        attend(nc, m, u_rows)
        dense(nc, m, x, g_w1, g_b1, g_w2, g_b2, g_w3, g_b3, g_w4, g_b4, x1_rows)
        norm_constants(nc, m, "D0")
        queries(nc, m, t_w1, t_w2, t_w3, q0_rows)
        clear_counts(nc, free)
        diffuse(nc, m, 0, u1_0, u2_0, q0_rows, q1_rows, xa_rows, xf_rows, None, y1_rows)
        diffuse(nc, m, 1, u1_1, u2_1, q1_rows, None, xa_rows, xf_rows, y1_rows, y2_rows)
        close_diffusion(nc, m, y2_rows, x1_rows, x2_rows, gamma, beta)
        symmetrise_and_spread(nc, m, adj)
        propagate(nc, m, x2_rows, c_w, c_b)
        convolve(nc, m, out)


def kernel(x, adj, L0_gnn_W, L0_gnn_a1, L0_gnn_a2, L0_gnn_W1, L0_gnn_b1, L0_gnn_W2, L0_gnn_b2, L0_gnn_W3, L0_gnn_b3,
           L0_gnn_W4, L0_gnn_b4, L1_gnn_W1, L1_gnn_W2, L1_gnn_W3, L1_gnn_U1_0, L1_gnn_U1_1, L1_gnn_U2_0, L1_gnn_U2_1,
           L1_gnn_gamma, L1_gnn_beta, L3_gnn_weight, L3_gnn_bias):
    import concourse.bacc as bacc
    from concourse.bass_utils import run_bass_kernel_spmd

    laid_out = {
        "x": x, "adj": adj, "adj_t": adj.T, "g_w": L0_gnn_W.transpose(1, 0, 2).reshape(D, D),
        "g_a1": L0_gnn_a1.reshape(-1), "g_a2": L0_gnn_a2.reshape(-1),
        "g_w1": L0_gnn_W1.T, "g_b1": L0_gnn_b1, "g_w2": L0_gnn_W2.T, "g_b2": L0_gnn_b2,
        "g_w3": L0_gnn_W3.T, "g_b3": L0_gnn_b3, "g_w4": L0_gnn_W4.T, "g_b4": L0_gnn_b4,
        "t_w1": L1_gnn_W1.T, "t_w2": L1_gnn_W2, "t_w3": L1_gnn_W3, "u1_0": L1_gnn_U1_0, "u1_1": L1_gnn_U1_1,
        "u2_0": L1_gnn_U2_0, "u2_1": L1_gnn_U2_1, "gamma": L1_gnn_gamma, "beta": L1_gnn_beta,
        "c_w": L3_gnn_weight, "c_b": L3_gnn_bias,
    }
    nc = bacc.Bacc("TRN2", target_bir_lowering=False, num_devices=1)
    arrays, args = {}, []
    for name, a in laid_out.items():
        a = np.ascontiguousarray(a)
        arrays["in_" + name] = a
        args.append(nc.dram_tensor("in_" + name, a.shape, mybir.dt.from_np(a.dtype), kind="ExternalInput").ap())
    out = nc.dram_tensor("out", (N, D), F32, kind="ExternalOutput").ap()
    program(nc, *args, out)
    result = run_bass_kernel_spmd(nc, [arrays], core_ids=[0])
    return result.results[0]["out"]
```

```python
import math
from contextlib import ExitStack

import numpy as np

import concourse.bass as bass
from concourse import mybir

F32 = mybir.dt.float32
F16 = mybir.dt.float16
I8 = mybir.dt.int8
ALU = mybir.AluOpType
ACT = mybir.ActivationFunctionType
AXIS = mybir.AxisListType

P = 128
N = 2048
NT = N // P
D = 512
KT = D // P
H, HD = 8, 64
BANK = 512
HALF = N // 2
SLOPE = 0.2
LN_EPS = 1e-5
EXP_CAP = 80.0
P_TOP = 0.9
SEARCH = math.log(N / (1.0 - P_TOP)) + 0.05
STEPS = 22
HALVINGS = (8, 12)
SCALAR_HALVINGS = (4, 5)
KB = 1024
ARENA = 200 * KB


class Chain:

    def __init__(self, eng, sem, base=0):
        self.eng, self.sem, self.base, self.n = eng, sem, base, 0

    def link(self, ins):
        self.count(ins)
        self.wait()

    def count(self, ins):
        self.n += 1
        ins.then_inc(self.sem, 1)

    def wait(self):
        self.eng.wait_ge(self.sem, self.base + self.n)


class Memory:

    def __init__(self, nc, ctx):
        self.nc, self.ctx = nc, ctx
        self.arena = ctx.enter_context(nc.sbuf_tensor("arena", [P, ARENA // 4], F32))
        self.psum = ctx.enter_context(nc.psum_tensor("banks", [P, 8, BANK], F32))
        self.eye = self.small("eye", [P, P], F32)
        self.eye16 = self.small("eye16", [P, P], F16)
        self.minus_half = self.small("minus_half", [P, 1], F32)
        self.ones = self.small("ones", [P, 32], F32)
        self.ones16 = self.small("ones16", [P, 1], F16)
        self.stats = self.small("stats", [P, NT, 6], F32)
        self.norm = self.small("norm", [P, 6, NT], F32)
        self.inv_degree = self.small("inv_degree", [P, NT], F32)
        self.inv_sqrt_degree = self.small("inv_sqrt_degree", [P, NT], F32)
        self.qk_weight = self.small("qk_weight", [P, KT, P], F32)
        self.scratch = self.small("scratch", [P, 4 * KB // 4], F32)
        self.own_feats = shaped(self.scratch[:, 0:512], (2, 256))
        self.pick = shaped(self.scratch[:, 512:768], (2, P))
        self.dst_part = shaped(self.scratch[:, 768:896], (NT, H))
        self.dst_floor = shaped(self.scratch[:, 896:1024], (NT, H))
        self.adj_t = self.f16(0, NT, N)

    def small(self, name, shape, dt):
        return self.ctx.enter_context(self.nc.sbuf_tensor(name, shape, dt))

    def f32(self, kb, *shape, parts=P):
        start, size = int(kb * KB) // 4, int(np.prod(shape))
        assert kb * KB + size * 4 <= ARENA
        view = self.arena[0:parts, start:start + size]
        return shaped(view, shape)

    def f16(self, kb, *shape, dt=F16):
        start, size = kb * KB // 4, int(np.prod(shape)) // 2
        assert kb * KB + size * 4 <= ARENA
        return shaped(self.arena[:, start:start + size].bitcast(dt), shape)

    def bank(self, b, count=1):
        return self.psum[:, b:b + count, :].rearrange("p b n -> p (b n)")


def shaped(view, shape):
    if len(shape) == 2:
        return view.rearrange("p (a b) -> p a b", a=shape[0])
    if len(shape) == 3:
        return view.rearrange("p (a b c) -> p a b c", a=shape[0], b=shape[1])
    return view


def columns(dram):
    return dram.rearrange("(k p) -> p k", p=P)


def rows(dram):
    return dram.rearrange("(t p) f -> p t f", p=P)


def on_all(dram):
    return dram.partition_broadcast(P)


def wait(eng, sem, value):
    if not isinstance(value, int) or value > 0:
        eng.wait_ge(sem, value)


AT_SCALE = 1024.0
SHARE_STEPS = 11


def halving(k):
    return math.exp(-SEARCH / 2 ** (k + 1))


def tile_rows(t):
    return bass.ts(t, P)


def queries_of(q_rows, t):
    return q_rows[bass.ts(t, P), :][0:64, 0:P]


def column(table, t):
    return table[:, bass.ds(t, 1)]


def repeat(eng, count, body):
    body(0)
    with eng.Fori(1, count) as i:
        body(i)


def walk(eng, body, lanes):
    groups = NT // lanes
    for lane in range(lanes):
        body(lane, lane, 0)
    with eng.Fori(1, groups - 1) as g:
        for lane in range(lanes):
            body(g * lanes + lane, lane, g)
    for lane in range(lanes):
        body(NT - lanes + lane, lane, groups - 1)


def row_constants(dve, chain, stats, norm):
    sq, diff, var, mean2 = (norm[:, k, :] for k in range(4))
    half = [stats[:, :, k] for k in range(6)]
    dve.tensor_tensor(sq, half[2], half[5], ALU.add)
    chain.link(dve.tensor_tensor(diff, half[1], half[4], ALU.subtract))
    chain.link(dve.scalar_tensor_tensor(mean2, diff, 0.25, diff, ALU.mult, ALU.mult))
    chain.link(dve.scalar_tensor_tensor(var, sq, 1.0 / D, mean2, ALU.mult, ALU.add))
    chain.link(dve.tensor_scalar(var, var, LN_EPS, None, ALU.add))
    chain.link(dve.tensor_tensor(mean2, half[1], half[4], ALU.add))


def measure_chunks(dve, x, landed, stats, done):
    for c in range(4):
        dve.wait_ge(landed[c], 16)
        for t in range(4 * c, 4 * c + 4):
            dve.bn_stats(stats[:, t, :], x[:, t, :]).then_inc(done, 1)
    dve.wait_ge(done, NT)


def constants(nc, m):
    with ExitStack() as ctx:
        zeroed = ctx.enter_context(nc.semaphore("zeroed"))
        made = ctx.enter_context(nc.semaphore("made"))
        block = ctx.enter_context(nc.Block())

        @block.gpsimd
        def _(pool):
            for eye in (m.eye, m.eye16):
                pool.memset(eye[:, :], 0.0).then_inc(zeroed, 1)
            pool.wait_ge(zeroed, 2)
            for eye in (m.eye, m.eye16):
                pool.affine_select(out=eye[:, :], in_=eye[:, :], compare_op=ALU.not_equal, fill=1.0, base=0,
                                   pattern=[[-1, P]], channel_multiplier=1).then_inc(made, 1)

        @block.vector
        def _(dve):
            dve.memset(m.minus_half[:, :], -0.5).then_inc(made, 1)
            dve.memset(m.ones[:, :], 1.0).then_inc(made, 1)
            dve.memset(m.ones16[:, :], 1.0).then_inc(made, 1)


def project(nc, m, x, adj_t, weight, a1, a2, u_rows):
    x_sb = m.f32(64, NT, D)
    feats = m.f32(96, NT, D)
    w_sb = m.f32(128, KT, D)
    h = m.f32(136, 2, D)
    h_t = m.f32(140, KT, P)
    a_sb = m.f32(144, 2, D)
    product = m.f32(148, D)
    w_a = m.f32(150, 2, KT * H)
    top_wide = m.f32(151, P, parts=H)
    row_sum = m.f32(152, N, parts=1)
    u_t = m.f32(160, N, parts=H)
    adj_in = m.f32(168, 4, N)
    top = m.f32(151.5, 3, H)
    top_head = m.f32(151.625, 1, parts=H)
    degrees = m.f32(151.65625, 4, NT)
    d_col = m.dst_part
    step = m.norm
    with ExitStack() as ctx:
        def sem(name):
            return ctx.enter_context(nc.semaphore("A_" + name))

        x_in, w_in, a_in = [sem(f"x_in{c}") for c in range(4)], sem("w_in"), sem("a_in")
        adj_landed = [sem(f"adj_landed{k}") for k in range(4)]
        adj_cast, sum_row, sum_cols = sem("adj_cast"), sem("sum_row"), sem("sum_cols")
        stats_done, dve_chain, variance, rstd, shift = (sem("stats_done"), sem("dve_chain"), sem("variance"),
                                                        sem("rstd"), sem("shift"))
        w_a_done, h_done, transposed, h_t_done = sem("w_a_done"), sem("h_done"), sem("transposed"), sem("h_t_done")
        feats_done, feats_kept, parts_done, parts_kept = (sem("feats_done"), sem("feats_kept"), sem("parts_done"),
                                                          sem("parts_kept"))
        top_t, top_row, top_bc, top_all, cols_kept = sem("top_t"), sem("top_row"), sem("top_bc"), sem("top_all"), sem("cols_kept")
        deg_base, deg_pow, base_done, u_done, u_stored = sem("deg_base"), sem("deg_pow"), sem("base_done"), sem("u_done"), sem("u_stored")
        block = ctx.enter_context(nc.Block())
        degree_row = m.bank(0, 4)[0:1, :]
        ps_t, ps_w, ps_s = m.bank(4), m.bank(5), m.bank(6)
        ps_small = m.bank(7)

        @block.sync
        def _(sp):
            sp.dma_start(w_sb, weight.rearrange("(k p) n -> p k n", p=P)).then_inc(w_in, 16)
            for c in range(4):
                sp.dma_start(x_sb[:, 4 * c:4 * c + 4, :], rows(x)[:, 4 * c:4 * c + 4, :]).then_inc(x_in[c], 16)
            def load(t, lane, group):
                wait(sp, adj_cast, t - 3)
                sp.dma_start(adj_in[:, lane, :], adj_t[bass.ts(t, P), :]).then_inc(adj_landed[lane], 16)
            walk(sp, load, 4)
            sp.wait_ge(u_done, 1)
            sp.dma_start(u_rows, u_t).then_inc(u_stored, 16)
            sp.wait_ge(u_stored, 16)

        @block.gpsimd
        def _(pool):
            pool.wait_ge(variance, 1)
            pool.tensor_tensor(step[:, 4, :], step[:, 2, :], m.minus_half[:, :].broadcast_to([P, NT]), ALU.pow).then_inc(rstd, 1)
            pool.wait_ge(deg_base, 1)
            pool.tensor_tensor(m.inv_sqrt_degree[:, :], degrees[:, 2, :], m.minus_half[:, :].broadcast_to([P, NT]), ALU.pow).then_inc(deg_pow, 1)

        @block.vector
        def _(dve):
            chain = Chain(dve, dve_chain)
            dve.wait_ge(w_in, 16)
            dve.wait_ge(a_in, 32)
            for which in range(2):
                for k in range(KT):
                    chain.link(dve.tensor_tensor(product, w_sb[:, k, :], a_sb[:, which, :], ALU.mult))
                    chain.link(dve.tensor_reduce(w_a[:, which, k * H:(k + 1) * H],
                                                 product.rearrange("p (h d) -> p h d", h=H), AXIS.X, ALU.add))
            dve.sem_inc(w_a_done, 1)
            measure_chunks(dve, x_sb, x_in, m.stats, stats_done)
            row_constants(dve, chain, m.stats, step)
            dve.sem_inc(variance, 1)
            dve.wait_ge(rstd, 1)
            dve.scalar_tensor_tensor(step[:, 5, :], step[:, 3, :], -0.5, step[:, 4, :], ALU.mult, ALU.mult).then_inc(shift, 1)
            def turn(t):
                dve.wait_ge(transposed, t + 1)
                wait(dve, parts_done, t)
                dve.tensor_scalar(h_t.rearrange("p k n -> p (k n)"), ps_t, 0.0, None, ALU.add).then_inc(h_t_done, 1)
                dve.wait_ge(parts_done, t + 1)
                dve.tensor_scalar(d_col[:, t, :], ps_s[:, 0:H], 0.0, None, ALU.add).then_inc(parts_kept, 1)
                dve.tensor_scalar(u_t[:, bass.ts(t, P)], ps_s[0:H, 256:256 + P], 0.0, None, ALU.add).then_inc(parts_kept, 1)
            repeat(dve, NT, turn)
            dve.wait_ge(parts_kept, 2 * NT)
            dve.tensor_reduce(top[:, 0, :], d_col.rearrange("p t h -> p h t"), AXIS.X, ALU.max).then_inc(top_t, 1)
            dve.wait_ge(top_row, 1)
            chain.link(dve.tensor_reduce(top_head, ps_small[0:H, 0:P], AXIS.X, ALU.max))
            chain.link(dve.tensor_scalar(top_wide, m.eye[0:H, 0:1].broadcast_to([H, P]), 0.0, top_head,
                                         ALU.mult, ALU.add))
            dve.sem_inc(top_bc, 1)
            chain.link(dve.tensor_scalar(u_t, u_t, top_head, 1.0 - SLOPE, ALU.add, ALU.mult))
            chain.link(dve.tensor_scalar(u_t, u_t, EXP_CAP, None, ALU.min))
            dve.sem_inc(u_done, 1)
            dve.wait_ge(top_all, 1)
            chain.link(dve.tensor_scalar(top[:, 1, :], ps_small[:, P:P + H], 0.0, None, ALU.add))
            dve.tensor_tensor(d_col, d_col, top[:, 1, :].rearrange("p (a h) -> p a h", a=1).broadcast_to([P, NT, H]),
                              ALU.subtract).then_inc(base_done, 1)
            dve.wait_ge(sum_row, NT)
            dve.tensor_scalar(row_sum, degree_row, 0.0, None, ALU.add).then_inc(cols_kept, 1)
            dve.wait_ge(sum_cols, 1)
            deg = degrees
            chain.link(dve.tensor_scalar(deg[:, 0, :], ps_small[:, 256:256 + NT], 0.0, None, ALU.add))
            dve.wait_ge(adj_cast, NT)
            chain.link(dve.tensor_tensor(deg[:, 2, :], deg[:, 0, :], deg[:, 1, :], ALU.add))
            chain.link(dve.tensor_scalar(deg[:, 2, :], deg[:, 2, :], 0.5, 1.0, ALU.mult, ALU.add))
            chain.link(dve.tensor_scalar(deg[:, 3, :], deg[:, 2, :], 0.0, None, ALU.is_gt))
            chain.link(dve.tensor_scalar(deg[:, 2, :], deg[:, 2, :], 1e-37, None, ALU.max))
            dve.sem_inc(deg_base, 1)
            chain.link(dve.tensor_scalar(deg[:, 0, :], deg[:, 0, :], 1.0, 1e-12, ALU.add, ALU.max))
            dve.reciprocal(m.inv_degree[:, :], deg[:, 0, :])
            dve.wait_ge(deg_pow, 1)
            chain.link(dve.tensor_tensor(m.inv_sqrt_degree[:, :], m.inv_sqrt_degree[:, :], deg[:, 3, :], ALU.mult))

        @block.scalar
        def _(act):
            act.dma_start(a_sb[:, 0, :], on_all(a1)).then_inc(a_in, 16)
            act.dma_start(a_sb[:, 1, :], on_all(a2)).then_inc(a_in, 16)
            act.activation(top[:, 2, 0:1], m.minus_half[:, :], ACT.Exp)
            act.wait_ge(shift, 1)

            def tile(t, lane, group):
                wait(act, transposed, t - 1)
                act.activation(h[:, lane % 2, :], x_sb[:, t, :], ACT.Relu, scale=column(step[:, 4, :], t),
                               bias=column(step[:, 5, :], t)).then_inc(h_done, 1)
                act.wait_ge(adj_landed[lane], (group + 1) * 16)
                act.activation(m.adj_t[:, t, :], adj_in[:, lane, :], ACT.Copy,
                               accum_out=column(degrees[:, 1, :], t)).then_inc(adj_cast, 1)
                act.wait_ge(feats_done, t + 1)
                act.activation(feats[:, t, :], ps_w, ACT.Copy).then_inc(feats_kept, 1)
            walk(act, tile, 4)
            act.wait_ge(base_done, 1)
            act.activation(m.dst_floor, d_col, ACT.Exp, scale=SLOPE)

        @block.tensor
        def _(pe):
            pe.wait_ge(w_a_done, 1)

            def tile(t, lane, group):
                pe.wait_ge(h_done, t + 1)
                wait(pe, h_t_done, t)
                for k in range(KT):
                    last = pe.transpose(ps_t[:, k * P:(k + 1) * P], h[:, lane % 2, k * P:(k + 1) * P], m.eye[:, :])
                last.then_inc(transposed, 1)
                if not (isinstance(t, int) and t == 0):
                    sum_columns(t - 1)
                pe.wait_ge(h_t_done, t + 1)
                wait(pe, feats_kept, t)
                wait(pe, parts_kept, t * 2)
                for k in range(KT):
                    last = pe.matmul(ps_w, h_t[:, k, :], w_sb[:, k, :], start=k == 0, stop=k == KT - 1)
                last.then_inc(feats_done, 1)
                for k in range(KT):
                    pe.matmul(ps_s[:, 0:H], h_t[:, k, :], w_a[:, 1, k * H:(k + 1) * H], start=k == 0, stop=k == KT - 1)
                for k in range(KT):
                    last = pe.matmul(ps_s[0:H, 256:256 + P], w_a[:, 0, k * H:(k + 1) * H], h_t[:, k, :],
                                     start=k == 0, stop=k == KT - 1)
                last.then_inc(parts_done, 1)

            def sum_columns(t):
                pe.wait_ge(adj_cast, t + 1)
                first, final = isinstance(t, int) and t == 0, isinstance(t, int) and t == NT - 1
                for c in range(4):
                    last = pe.matmul(degree_row[:, c * BANK:(c + 1) * BANK], m.ones16[:, :],
                                     m.adj_t[:, t, c * BANK:(c + 1) * BANK], start=first, stop=final)
                last.then_inc(sum_row, 1)
            walk(pe, tile, 4)
            sum_columns(NT - 1)
            pe.wait_ge(top_t, 1)
            pe.transpose(ps_small[0:H, 0:P], top[:, 0, :], m.eye[:, :]).then_inc(top_row, 1)
            pe.wait_ge(top_bc, 1)
            pe.matmul(ps_small[:, P:P + H], top_wide, m.eye[0:H, 0:H], start=True, stop=True).then_inc(top_all, 1)
            pe.wait_ge(cols_kept, 1)
            for t in range(NT):
                last = pe.matmul(ps_small[:, 256 + t:257 + t], row_sum[:, t * P:(t + 1) * P], m.ones[0:1, 0:1],
                                 start=True, stop=True)
            last.then_inc(sum_cols, 1)


def dense_weights(m):
    return m.f32(160, 4, 256), m.f32(164, 2, P), m.f32(165, 1, 256)


def attend(nc, m, u_rows, w1, w2, w3):
    feats = m.f32(96, NT, D)
    enc = m.f32(128, KT, N)
    u_all = [m.f32(168, 4, HALF), m.f32(184, 4, HALF)]
    weights = m.f32(64, 8, HALF)
    own = m.own_feats
    pick = m.pick

    def elu_part(r, pair):
        return u_all[r % 2][:, pair, :]

    def inv_den(r):
        return u_all[r % 2][:, 2, :]

    rounds = [(quad, half) for quad in range(2) for half in range(2)]

    def enc_part(r, pair):
        quad, half = rounds[r]
        return enc[:, quad * 2 + pair, half * HALF:(half + 1) * HALF]

    steps_to_close = 5

    def walk_round(eng, r, body, keep, close, at_end=None):
        for t in range(6):
            body(t, t % 2, t // 2)
            if r and t == 0 and keep:
                keep(r - 1)
            if r and t < steps_to_close:
                close(r - 1, t)
        with eng.Fori(3, NT // 2 - 1) as g:
            for slot in range(2):
                body(g * 2 + slot, slot, g)
        for slot in range(2):
            body(NT - 2 + slot, slot, NT // 2 - 1)
        if at_end:
            at_end(r)
        if r == len(rounds) - 1:
            if keep:
                keep(r)
            for k in range(steps_to_close):
                close(r, k)
    with ExitStack() as ctx:
        def sem(name):
            return ctx.enter_context(nc.semaphore("B_" + name))

        pick_zero, pick_done, own_ready = sem("pick_zero"), sem("pick_done"), sem("own_ready")
        u_landed = [sem(f"u_landed{k}") for k in range(2)]
        exp_done, masked, summed, round_done = sem("exp_done"), sem("masked"), sem("summed"), sem("round_done")
        den_inverted, w_in = sem("den_inverted"), sem("w_in")
        sums_kept, den_kept, den_spread, scaled = sem("sums_kept"), sem("den_kept"), sem("den_spread"), sem("scaled")
        floored, elu_exp, elu_done = sem("floored"), sem("elu_exp"), sem("elu_done")
        block = ctx.enter_context(nc.Block())
        ps_sum = [m.bank(0, 2), m.bank(2, 2)]
        ps_den = m.bank(4, 2)
        ps_misc = m.bank(6, 2)

        @block.sync
        def _(sp):
            for r, (quad, half) in enumerate(rounds):
                if r >= 2:
                    sp.wait_ge(elu_done, 2 * (r - 1))
                sp.dma_start(u_all[r % 2], u_rows[quad * 4:quad * 4 + 4, half * HALF:(half + 1) * HALF]
                             .partition_broadcast(P)).then_inc(u_landed[r % 2], 16)
                if r == 1:
                    for weights_sb, source in zip(dense_weights(m), (w1, w2, w3)):
                        sp.dma_start(weights_sb, source.rearrange("(k p) n -> p k n", p=P)).then_inc(w_in, 16)
            sp.wait_ge(w_in, 48)

        @block.gpsimd
        def _(pool):
            pool.memset(pick, 0.0).then_inc(pick_zero, 1)
            pool.wait_ge(pick_zero, 1)
            pool.affine_select(out=pick.rearrange("p a (b c) -> p a b c", b=2), in_=pick.rearrange("p a (b c) -> p a b c", b=2),
                               compare_op=ALU.not_equal, fill=1.0, base=0,
                               pattern=[[-64, 2], [-32, 2], [0, 64]], channel_multiplier=1).then_inc(pick_done, 1)
            for r, (quad, half) in enumerate(rounds):
                def body(t, slot, group):
                    wait(pool, summed, t + (r * NT - 1))
                    pool.tensor_copy(own[:, slot, :], feats[:, t, quad * 256:(quad + 1) * 256]).then_inc(own_ready, 1)
                walk(pool, body, 2)

        @block.scalar
        def _(act):
            act.activation(m.norm[:, 0, 0:1], m.minus_half[:, :], ACT.Exp)

            for r, (quad, half) in enumerate(rounds):
                def body(t, slot, group):
                    wait(act, summed, t + (r * NT - 1))
                    for q in range(4):
                        bias = d_at(m.dst_part, t, quad * 4 + q)
                        act.activation(weights[:, slot * 4 + q, :], u_all[r % 2][:, q, :], ACT.Exp,
                                       bias=bias).then_inc(exp_done, 1)

                def keep(r):
                    act.wait_ge(round_done, r + 1)
                    for pair in range(2):
                        act.activation(enc_part(r, pair), ps_sum[pair], ACT.Copy).then_inc(sums_kept, 1)

                def close(r, k):
                    if k >= 3:
                        pair = k - 3
                        act.wait_ge(floored, 2 * r + pair + 1)
                        act.activation(elu_part(r, pair), elu_part(r, pair), ACT.Exp).then_inc(elu_exp, 1)
                act.wait_ge(u_landed[r % 2], 16 * (r // 2 + 1))
                walk_round(act, r, body, keep, close)

        @block.vector
        def _(dve):
            for r, (quad, half) in enumerate(rounds):
                def body(t, slot, group):
                    for q in range(4):
                        w = weights[:, slot * 4 + q, :]
                        dve.wait_ge(exp_done, (t + r * NT) * 4 + q + 1)
                        dve.scalar_tensor_tensor(w, w, d_at(m.dst_floor, t, quad * 4 + q),
                                                 m.adj_t[:, t, half * HALF:(half + 1) * HALF],
                                                 ALU.max, ALU.mult).then_inc(masked, 1)

                def keep(r):
                    dve.wait_ge(round_done, r + 1)
                    dve.tensor_scalar(inv_den(r), ps_den, 0.0, None, ALU.add).then_inc(den_kept, 1)

                def close(r, k):
                    if k < 2:
                        dve.wait_ge(den_kept, r + 1)
                        part = inv_den(r)[:, k * BANK:(k + 1) * BANK]
                        dve.reciprocal(part, part).then_inc(den_inverted, 1)
                    if k in (2, 3):
                        pair = k - 2
                        value = enc_part(r, pair)
                        dve.wait_ge(den_spread, 2 * r + pair + 1)
                        dve.wait_ge(sums_kept, 2 * r + pair + 1)
                        dve.tensor_tensor(value, value, ps_misc, ALU.mult).then_inc(scaled, 1)
                        dve.wait_ge(scaled, 2 * r + pair + 1)
                        dve.tensor_scalar(elu_part(r, pair), value, 0.0, None, ALU.min).then_inc(floored, 1)
                    if k >= 3:
                        pair = k - 3
                        value = enc_part(r, pair)
                        dve.wait_ge(elu_exp, 2 * r + pair + 1)
                        dve.scalar_tensor_tensor(value, elu_part(r, pair), -1.0, value, ALU.add, ALU.max).then_inc(elu_done, 1)
                walk_round(dve, r, body, keep, close)

        @block.tensor
        def _(pe):
            pe.wait_ge(pick_done, 1)
            for r, (quad, half) in enumerate(rounds):
                def body(t, slot, group):
                    first, final = isinstance(t, int) and t == 0, isinstance(t, int) and t == NT - 1
                    if first and r:
                        pe.wait_ge(sums_kept, 2 * r)
                        pe.wait_ge(den_kept, r)
                    pe.wait_ge(own_ready, t + (r * NT + 1))
                    for pair in range(2):
                        pe.wait_ge(masked, (t + r * NT) * 4 + 2 * pair + 2)
                        for c in range(2):
                            for q in range(2):
                                pe.matmul(ps_sum[pair][64 * q:64 * q + 64, c * BANK:(c + 1) * BANK],
                                          own[:, slot, (2 * pair + q) * HD:(2 * pair + q + 1) * HD],
                                          weights[:, slot * 4 + 2 * pair + q, c * BANK:(c + 1) * BANK],
                                          start=first, stop=final, tile_position=(0, 64 * q))
                    for c in range(2):
                        for q in range(4):
                            last = pe.matmul(ps_den[32 * q:32 * q + 32, c * BANK:(c + 1) * BANK], m.ones[:, :],
                                             weights[:, slot * 4 + q, c * BANK:(c + 1) * BANK],
                                             start=first, stop=final, tile_position=(0, 32 * q))
                    last.then_inc(summed, 1)

                def close(r, k):
                    if k not in (1, 2):
                        return
                    pair = k - 1
                    pe.wait_ge(den_inverted, 2 * r + 2)
                    wait(pe, scaled, 2 * r + pair)
                    for c in range(2):
                        last = pe.matmul(ps_misc[:, c * BANK:(c + 1) * BANK], pick[:, pair, :],
                                         inv_den(r)[:, c * BANK:(c + 1) * BANK], start=True, stop=True)
                    last.then_inc(den_spread, 1)

                def signal_end(r):
                    pe.wait_ge(summed, (r + 1) * NT)
                    pe.sem_inc(round_done, 1)
                walk_round(pe, r, body, None, close, signal_end)


def dense(nc, m, x, b1, b2, b3, w4, b4, x1_rows):
    x_sb = m.f32(64, NT, D)
    enc = m.f32(128, KT, N)
    w1_sb, w2_sb, w3_sb = dense_weights(m)
    w4_sb = m.f32(102, 2, D)
    y1, y2, y3 = m.f32(106, 2, BANK), m.f32(110, BANK), m.f32(112, 2, BANK)
    b1_sb, b2_sb, b3_sb, b4_sb = m.f32(116, 2), m.f32(116.125, 1), m.f32(116.25, 2), m.f32(117, D)
    with ExitStack() as ctx:
        def sem(name):
            return ctx.enter_context(nc.semaphore("C_" + name))

        x_in, w_in, b_in, biased = sem("x_in"), sem("w_in"), sem("b_in"), sem("biased")
        l1_done, l2_done, l3_done, l4_done = sem("l1_done"), sem("l2_done"), sem("l3_done"), sem("l4_done")
        y1_kept, y2_kept, y3_kept, x1_done = sem("y1_kept"), sem("y2_kept"), sem("y3_kept"), sem("x1_done")
        stats_done, stored = sem("stats_done"), sem("stored")
        block = ctx.enter_context(nc.Block())

        @block.sync
        def _(sp):
            with nc.allow_non_contiguous_dma(reason="bias columns"):
                sp.dma_start(b1_sb, columns(b1)).then_inc(b_in, 16)
                sp.dma_start(b2_sb, columns(b2)).then_inc(b_in, 16)
                sp.dma_start(b3_sb, columns(b3)).then_inc(b_in, 16)
            sp.dma_start(b4_sb, on_all(b4)).then_inc(b_in, 16)
            sp.dma_start(w4_sb, w4.rearrange("(k p) n -> p k n", p=P)).then_inc(w_in, 16)
            sp.dma_start(x_sb, rows(x)).then_inc(x_in, 16)
            def turn(c):
                sp.wait_ge(x1_done, c * 4 + 4)
                sp.dma_start(rows(x1_rows)[:, bass.ts(c, 4), :], x_sb[:, bass.ts(c, 4), :]).then_inc(stored, 16)
            repeat(sp, 4, turn)
            sp.wait_ge(stored, 64)

        @block.gpsimd
        def _(pool):
            pool.wait_ge(b_in, 64)
            pool.wait_ge(x_in, 16)
            def turn(t):
                pool.tensor_tensor(x_sb[:, t, :], x_sb[:, t, :], b4_sb, ALU.add).then_inc(biased, 1)
            repeat(pool, NT, turn)

        @block.scalar
        def _(act):
            act.wait_ge(b_in, 64)
            act.activation(m.scratch[:, 0:1], m.minus_half[:, :], ACT.Copy)
            def turn(c):
                for half in range(2):
                    wait(act, l2_done, c)
                    act.wait_ge(l1_done, c * 2 + half + 1)
                    act.activation(y1[:, half, :], m.bank(half), ACT.Relu, bias=b1_sb[:, half:half + 1]).then_inc(y1_kept, 1)
                wait(act, l3_done, c * 2)
                act.wait_ge(l2_done, c + 1)
                act.activation(y2, m.bank(2), ACT.Relu, bias=b2_sb).then_inc(y2_kept, 1)
                for half in range(2):
                    wait(act, l4_done, c * 4)
                    act.wait_ge(l3_done, c * 2 + half + 1)
                    act.activation(y3[:, half, :], m.bank(half), ACT.Relu, bias=b3_sb[:, half:half + 1]).then_inc(y3_kept, 1)
            repeat(act, 4, turn)

        @block.vector
        def _(dve):
            dve.wait_ge(biased, NT)
            def turn(c):
                for i in range(4):
                    dve.wait_ge(l4_done, c * 4 + i + 1)
                    dve.tensor_tensor(x_sb[:, c * 4 + i, :], x_sb[:, c * 4 + i, :], m.bank(3 + i), ALU.add).then_inc(x1_done, 1)
                    dve.wait_ge(x1_done, c * 4 + i + 1)
                    dve.bn_stats(m.stats[:, c * 4 + i, :], x_sb[:, c * 4 + i, :]).then_inc(stats_done, 1)
            repeat(dve, 4, turn)

        @block.tensor
        def _(pe):
            def turn(c):
                wait(pe, y3_kept, c * 2)
                for half in range(2):
                    for k in range(KT):
                        last = pe.matmul(m.bank(half), w1_sb[:, k, half * P:(half + 1) * P], enc[:, k, bass.ts(c, BANK)],
                                         start=k == 0, stop=k == KT - 1)
                    last.then_inc(l1_done, 1)
                pe.wait_ge(y1_kept, c * 2 + 2)
                wait(pe, y2_kept, c)
                for k in range(2):
                    last = pe.matmul(m.bank(2), w2_sb[:, k, :], y1[:, k, :], start=k == 0, stop=k == 1)
                last.then_inc(l2_done, 1)
                pe.wait_ge(y2_kept, c + 1)
                for half in range(2):
                    pe.matmul(m.bank(half), w3_sb[:, 0, half * P:(half + 1) * P], y2, start=True, stop=True).then_inc(l3_done, 1)
                pe.wait_ge(y3_kept, c * 2 + 2)
                wait(pe, x1_done, c * 4)
                if isinstance(c, int):
                    pe.wait_ge(w_in, 16)
                for i in range(4):
                    for k in range(2):
                        last = pe.matmul(m.bank(3 + i), y3[:, k, i * P:(i + 1) * P], w4_sb[:, k, :], start=k == 0, stop=k == 1)
                    last.then_inc(l4_done, 1)
            repeat(pe, 4, turn)


def norm_constants(nc, m, name, extra_scale=None):
    step = m.norm
    with ExitStack() as ctx:
        variance = ctx.enter_context(nc.semaphore(name + "_variance"))
        power = ctx.enter_context(nc.semaphore(name + "_power"))
        dve_chain = ctx.enter_context(nc.semaphore(name + "_chain"))
        block = ctx.enter_context(nc.Block())

        @block.gpsimd
        def _(pool):
            pool.wait_ge(variance, 1)
            pool.tensor_tensor(step[:, 4, :], step[:, 2, :], m.minus_half[:, :].broadcast_to([P, NT]), ALU.pow).then_inc(power, 1)

        @block.vector
        def _(dve):
            chain = Chain(dve, dve_chain)
            row_constants(dve, chain, m.stats, step)
            dve.sem_inc(variance, 1)
            dve.wait_ge(power, 1)
            if extra_scale is not None:
                chain.link(dve.tensor_tensor(step[:, 4, :], step[:, 4, :], extra_scale, ALU.mult))
            chain.link(dve.scalar_tensor_tensor(step[:, 5, :], step[:, 3, :], -0.5, step[:, 4, :], ALU.mult, ALU.mult))


def queries(nc, m, t_w1, t_w2, t_w3, q_rows):
    h = m.f32(64, NT, D)
    parts = m.f16(96, NT, 2, D)
    keys, query = m.f32(128, N, parts=64), m.f32(136, N, parts=64)
    h_t, w1_t, w2_sb, ring = m.f32(144, 2, KT, P), m.f32(156, D, parts=64), m.f32(148, 64, parts=64), m.f32(150, 2, D)
    step = m.norm
    with ExitStack() as ctx:
        def sem(name):
            return ctx.enter_context(nc.semaphore("D_" + name))

        w_in, merged, merged_kept = sem("w_in"), sem("merged"), sem("merged_kept")
        ring_done, h_done, high_done, low_done = sem("ring_done"), sem("h_done"), sem("high_done"), sem("low_done")
        transposed, h_t_kept, qk_done, qk_kept = sem("transposed"), sem("h_t_kept"), sem("qk_done"), sem("qk_kept")
        q_stored = sem("q_stored")
        block = ctx.enter_context(nc.Block())
        ps_t, ps_qk = [m.bank(0), m.bank(1)], m.bank(2)

        @block.sync
        def _(sp):
            sp.dma_start(w1_t, t_w1).then_inc(w_in, 16)
            sp.dma_start(w2_sb, t_w2).then_inc(w_in, 16)
            sp.dma_start(m.qk_weight[:, :, 64:P], t_w3.rearrange("(k p) n -> p k n", p=P)).then_inc(w_in, 16)
            sp.wait_ge(qk_kept, 2 * NT)
            sp.dma_start(q_rows.rearrange("(t p) f -> p t f", p=P)[0:64, :, 0:P], query.rearrange("p (t n) -> p t n", n=P)).then_inc(q_stored, 16)
            sp.wait_ge(q_stored, 16)

        @block.scalar
        def _(act):
            act.activation(m.scratch[:, 0:1], m.minus_half[:, :], ACT.Copy)

            def tile(t, lane, group):
                wait(act, transposed, t - 1)
                wait(act, h_done, t - 1)
                scale, shift = column(step[:, 4, :], t), column(step[:, 5, :], t)
                act.activation(ring[:, lane, :], h[:, t, :], ACT.Relu, scale=scale, bias=shift).then_inc(ring_done, 1)
                act.activation(parts[:, t, 0, :], h[:, t, :], ACT.Relu, scale=scale, bias=shift).then_inc(high_done, 1)
            walk(act, tile, 2)

        @block.gpsimd
        def _(pool):
            def tile(t, lane, group):
                pool.wait_ge(ring_done, t + 1)
                pool.wait_ge(high_done, t + 1)
                pool.tensor_copy(h[:, t, :], ring[:, lane, :]).then_inc(h_done, 1)
            walk(pool, tile, 2)

        @block.vector
        def _(dve):
            dve.wait_ge(merged, 1)
            dve.tensor_scalar(m.qk_weight[:, :, 0:64], ps_t[0][:, 0:256].rearrange("p (k n) -> p k n", k=KT), 0.0, None,
                              ALU.add).then_inc(merged_kept, 1)

            def tile(t, lane, group):
                dve.wait_ge(transposed, t + 1)
                wait(dve, qk_done, t - 1)
                dve.tensor_scalar(h_t[:, lane, :, :].rearrange("p k n -> p (k n)"), ps_t[lane], 0.0, None, ALU.add).then_inc(h_t_kept, 1)
                dve.wait_ge(h_done, t + 1)
                dve.tensor_tensor(parts[:, t, 1, :], h[:, t, :], parts[:, t, 0, :], ALU.subtract).then_inc(low_done, 1)
                if not (isinstance(t, int) and t == 0):
                    keep(t - 1)

            def keep(t):
                dve.wait_ge(qk_done, t + 1)
                dve.tensor_scalar(query[:, bass.ts(t, P)], ps_qk[0:64, 0:P], 0.0, None, ALU.add).then_inc(qk_kept, 1)
                dve.tensor_scalar(keys[:, bass.ts(t, P)], ps_qk[64:P, 0:P], 0.0, None, ALU.add).then_inc(qk_kept, 1)
            walk(dve, tile, 2)
            keep(NT - 1)

        @block.tensor
        def _(pe):
            pe.wait_ge(w_in, 48)
            for k in range(KT):
                last = pe.matmul(ps_t[0][:, k * 64:(k + 1) * 64], w1_t[:, k * P:(k + 1) * P], w2_sb, start=True, stop=True)
            last.then_inc(merged, 1)
            pe.wait_ge(merged_kept, 1)

            def tile(t, lane, group):
                pe.wait_ge(ring_done, t + 1)
                wait(pe, h_t_kept, t - 1)
                for k in range(KT):
                    last = pe.transpose(ps_t[lane][:, k * P:(k + 1) * P], ring[:, lane, k * P:(k + 1) * P], m.eye[:, :])
                last.then_inc(transposed, 1)
                if not (isinstance(t, int) and t == 0):
                    multiply(t - 1, 1 - lane)

            def multiply(t, lane):
                pe.wait_ge(h_t_kept, t + 1)
                wait(pe, qk_kept, t * 2)
                for k in range(KT):
                    last = pe.matmul(ps_qk[:, 0:P], m.qk_weight[:, k, :], h_t[:, lane, k, :], start=k == 0, stop=k == KT - 1)
                last.then_inc(qk_done, 1)
            walk(pe, tile, 2)
            multiply(NT - 1, 1)


def diffuse(nc, m, s, u1, u2, q_in, q_out, xa_rows, xf_rows, y_in, y_out):
    xa = m.f32(64, NT, D)
    xf = m.f16(96, NT, 2, D)
    lo, hi_part = 64 * s, 64 * s + 64
    keys = m.f32(128, N)[lo:hi_part, :]
    next_keys = m.f32(128, N)[64:P, :]
    probs = [m.f32(136 + 8 * k, N) for k in range(3)]
    spare = m.f32(160, N)
    u1_sb, u2_sb = m.f32(168, KT, D), m.f32(176, KT, D)
    at = m.f32(184, 3, 4 * P)
    at_halves = m.f16(184, 3, 2, 4 * P)
    x_t, x_t2, xt, zt = m.f32(190, D), at[:, 1, :], m.f32(192, D), m.f32(194, D)
    halves, y_old = m.f16(196, 2, D), m.f32(196, D)
    q_ring = m.f32(198, 3, P)
    state = m.f32(199.5, 3, 16)
    wide = m.f32(199.5 + 0.1875, 8 * 8)
    junk_dve = m.scratch[:, 0:512].bitcast(I8)
    junk_act = m.scratch[:, 512:1024].bitcast(I8)
    flag_table = m.stats[:, :, :].rearrange("p a b -> p (a b)")
    flags, flags_t = flag_table[:, 0:32], flag_table[:, 32:64]
    factors = m.norm[:, :, :].rearrange("p a b -> p (a b)")
    ratios = factors[:, 0:STEPS]
    half, nodes, p_top, minus_one = (factors[:, STEPS + k:STEPS + k + 1] for k in range(4))
    q_stage = q_ring[64:P, 0, :]
    first_step = s == 0
    scalar_steps, all_steps = SCALAR_HALVINGS[s], HALVINGS[s]
    pool_links, narrow_links = 11 * scalar_steps + 5, 4 * (STEPS - all_steps) + 22 + first_step
    top8, sums8, cross8 = wide[:, 0:8], wide[:, 8:16], wide[:, 16:24]
    ones8 = m.ones[:, 0:8]
    (below, s_hi, w, above8, s_above, sl, w_inv, count, kept, frac, corr, keep, flag, worst, neg_above,
     reached) = (wide[:, 24 + k:25 + k] for k in range(16))
    norm = wide[:, 45:46]
    quarter = wide[:, 40:44]
    verdict = wide[0:1, 44:45].bitcast(mybir.dt.int32)

    def of(lane, k):
        return state[:, lane, k:k + 1]
    (NEG_MAX, TOTAL, TARGET, HI, CUT, CUT2, NEG_CUT, NEG_HI, RELUS, SIGNS, COUNTED, SUM, LACK, KEEP, LOWER,
     INV_NORM) = range(16)

    with ExitStack() as ctx:
        def sem(name):
            return ctx.enter_context(nc.semaphore(f"E{s}_" + name))

        u_in, xa_in, xf_in, ready = sem("u_in"), sem("xa_in"), sem("xf_in"), sem("ready")
        q_landed = [sem(f"q_landed{k}") for k in range(3)]
        logits, maxed, exp_done, searched = sem("logits"), sem("maxed"), sem("exp_done"), sem("searched")
        half_passed, passed, pool_chain, lacking = sem("half_passed"), sem("passed"), sem("pool_chain"), sem("lacking")
        dve_chain, max_chain, fallback, cut_done, added = (sem("dve_chain"), sem("max_chain"), sem("fallback"), sem("cut_done"),
                                                           sem("added"))
        a_turned, at_kept, product, xa_kept, xa_stored = (sem("a_turned"), sem("at_kept"), sem("product"), sem("xa_kept"),
                                                          sem("xa_stored"))
        xt_turned, xt_kept, u_used, qk_done, qk_kept, q_stored = (sem("xt_turned"), sem("xt_kept"), sem("u_used"), sem("qk_done"),
                                                                  sem("qk_kept"), sem("q_stored"))
        spread, xf_kept, high_done, low_done, xf_stored = (sem("spread"), sem("xf_kept"), sem("high_done"), sem("low_done"),
                                                           sem("xf_stored"))
        z_kept, y_landed, y_done, y_stored = sem("z_kept"), sem("y_landed"), sem("y_done"), sem("y_stored")
        at_low = sem("at_low")
        at_ready = at_low if first_step else at_kept
        block = ctx.enter_context(nc.Block())
        ps_logits = m.bank(0, 4)
        ps_t, ps_x, ps_z = [m.bank(4), m.bank(5)], m.bank(6), m.bank(7)

        def turns(eng, turn):
            for t in (-1, 0, 1):
                turn(t, t % 3, (t + 2) // 3 + 1)
            with eng.Fori(0, 4) as g:
                for k in range(3):
                    turn(g * 3 + (k + 2), (k + 2) % 3, g + ((k + 4) // 3 + 1))
            for t in range(14, NT + 1):
                turn(t, t % 3, (t + 2) // 3 + 1)

        def passes(tile, k):
            return (tile - 1) * scalar_steps + k

        def searches(tile, k):
            return 1 + (tile - 1) * (scalar_steps + 1) + k

        def exists(t, ahead):
            return not isinstance(t, int) or 0 <= t + ahead < NT

        @block.sync
        def _(sp):
            sp.wait_ge(q_landed[1], 16)
            sp.dma_start(u1_sb, u1.rearrange("(k p) n -> p k n", p=P)).then_inc(u_in, 16)
            sp.dma_start(u2_sb, u2.rearrange("(k p) n -> p k n", p=P)).then_inc(u_in, 16)

            def turn(t, lane, loads):
                if isinstance(t, int) and t == -1:
                    if not first_step:
                        sp.dma_start(xa, rows(xa_rows)).then_inc(xa_in, 16)
                        sp.dma_start(xf, xf_rows.rearrange("(t p) a f -> p t a f", p=P)).then_inc(xf_in, 16)
                    return
                if exists(t, -1):
                    if first_step:
                        sp.wait_ge(low_done, t)
                        sp.dma_start(xf_rows[tile_rows(t - 1), :, :], halves).then_inc(xf_stored, 16)
                        sp.wait_ge(xa_kept, t)
                        sp.dma_start(xa_rows[tile_rows(t - 1), :], xt).then_inc(xa_stored, 16)
                    else:
                        wait(sp, y_done, t - 1)
                        sp.dma_start(y_old, y_in[tile_rows(t - 1), :]).then_inc(y_landed, 16)
                    if first_step:
                        sp.wait_ge(qk_kept, t * 2)
                        sp.dma_start(queries_of(q_out, t - 1), q_stage).then_inc(q_stored, 16)
                    sp.wait_ge(y_done, t)
                    sp.dma_start(y_out[tile_rows(t - 1), :], zt).then_inc(y_stored, 16)
            turns(sp, turn)
            sp.wait_ge(y_stored, 16 * NT)
            if first_step:
                sp.wait_ge(q_stored, 16 * NT)
                sp.wait_ge(xa_stored, 16 * NT)
                sp.wait_ge(xf_stored, 16 * NT)

        @block.gpsimd
        def _(pool):
            def turn(t, lane, loads):
                nxt = (lane + 1) % 3
                if exists(t, 1):
                    tile0 = isinstance(t, int) and t == -1
                    chain = Chain(pool, pool_chain, 0 if tile0 else t * pool_links + 5)
                    pool.wait_ge(exp_done, t + 2)
                    chain.count(pool.tensor_tensor(of(nxt, TARGET), of(nxt, TOTAL), p_top, ALU.mult))
                    chain.count(pool.tensor_scalar(of(nxt, NEG_HI), of(nxt, TOTAL), 0.0, -1.0, ALU.mult, ALU.add))
                    chain.link(pool.tensor_scalar(of(nxt, NEG_CUT), of(nxt, TOTAL), 0.0, -halving(0), ALU.mult, ALU.add))
                    if not tile0:
                        pool.sem_inc(searched, 1)
                if exists(t, -1):
                    pool.wait_ge(cut_done, t)
                    pool.tensor_tensor(probs[(lane - 1) % 3], probs[(lane - 1) % 3], spare, ALU.add).then_inc(added, 1)
                if exists(t, 1):
                    for k in range(0 if tile0 else scalar_steps):
                        pool.wait_ge(half_passed, passes(t + 1, k + 1))
                        chain.link(pool.tensor_tensor(of(nxt, COUNTED), of(nxt, SIGNS), nodes, ALU.add))
                        chain.link(pool.tensor_tensor(of(nxt, COUNTED), of(nxt, COUNTED), of(nxt, NEG_CUT), ALU.mult))
                        chain.link(pool.tensor_tensor(of(nxt, COUNTED), of(nxt, COUNTED), half, ALU.mult))
                        chain.link(pool.tensor_tensor(of(nxt, COUNTED), of(nxt, COUNTED), of(nxt, TARGET), ALU.add))
                        pool.wait_ge(passed, passes(t + 1, k + 1))
                        chain.link(pool.tensor_tensor(of(nxt, LACK), of(nxt, COUNTED), of(nxt, RELUS), ALU.subtract))
                        pool.sem_inc(lacking, 1)
                        chain.count(pool.tensor_scalar(of(nxt, KEEP), of(nxt, LACK), 0.0, None, ALU.is_le))
                        chain.link(pool.tensor_scalar(of(nxt, LOWER), of(nxt, LACK), 0.0, None, ALU.is_gt))
                        chain.count(pool.tensor_tensor(of(nxt, KEEP), of(nxt, KEEP), of(nxt, NEG_HI), ALU.mult))
                        chain.link(pool.tensor_tensor(of(nxt, LOWER), of(nxt, LOWER), of(nxt, NEG_CUT), ALU.mult))
                        chain.link(pool.tensor_tensor(of(nxt, NEG_HI), of(nxt, KEEP), of(nxt, LOWER), ALU.add))
                        chain.link(pool.tensor_tensor(of(nxt, NEG_CUT), of(nxt, NEG_HI), ratios[:, k + 1:k + 2], ALU.mult))
                        if k + 1 < scalar_steps:
                            pool.sem_inc(searched, 1)
                        if k == 1 and first_step and exists(t, -1):
                            pool.wait_ge(high_done, t)
                            pool.tensor_tensor(halves[:, 1, :], xt, halves[:, 0, :], ALU.subtract).then_inc(low_done, 1)
                    chain.count(pool.tensor_tensor(of(nxt, HI), of(nxt, NEG_HI), minus_one, ALU.mult))
                    chain.link(pool.tensor_tensor(of(nxt, CUT), of(nxt, NEG_CUT), minus_one, ALU.mult))
                    pool.sem_inc(searched, 1)
                    assert chain.n == (5 if tile0 else pool_links)
                elif first_step and exists(t, -1):
                    pool.wait_ge(high_done, t)
                    pool.tensor_tensor(halves[:, 1, :], xt, halves[:, 0, :], ALU.subtract).then_inc(low_done, 1)
                if exists(t, -1):
                    pool.wait_ge(z_kept, t)
                    if first_step:
                        pool.tensor_tensor(zt, zt, xa[:, t - 1, :], ALU.add).then_inc(y_done, 1)
                    else:
                        pool.wait_ge(y_landed, t * 16)
                        pool.tensor_tensor(zt, zt, y_old, ALU.add).then_inc(y_done, 1)
            pool.wait_ge(ready, 2)
            turns(pool, turn)

        @block.vector
        def _(dve):
            links = [0, 0]

            def row_max(t, lane):
                dve.wait_ge(logits, t + 1)
                dve.tensor_reduce(of(lane, SUM), ps_logits, AXIS.X, ALU.max).then_inc(max_chain, 1)
                dve.wait_ge(max_chain, t + 1)
                dve.tensor_scalar(of(lane, NEG_MAX), of(lane, SUM), -1.0, None, ALU.mult).then_inc(maxed, 1)

            def split_low(t, g):
                if first_step and exists(t, -1):
                    dve.wait_ge(at_kept, (t - 1) * 4 + (g + 1))
                    dve.scalar_tensor_tensor(at_halves[:, g % 3, 1, :], ps_t[g % 2], AT_SCALE, at_halves[:, g % 3, 0, :],
                                             ALU.mult, ALU.subtract).then_inc(at_low, 1)

            def halve(chain, e, old, new, hi, target, keep, factor):
                chain.link(dve.scalar_tensor_tensor(junk_dve, e, old, e, ALU.is_gt, ALU.mult, accum_out=below))
                chain.link(dve.tensor_scalar(keep, below, target, hi, ALU.is_ge, ALU.mult))
                chain.count(dve.tensor_scalar(new, keep, old, factor, ALU.max, ALU.mult))
                chain.wait()
                chain.count(dve.tensor_scalar(hi, keep, old, None, ALU.max))

            def refine(t, lane):
                e, target, hi = probs[lane], of(lane, TARGET), of(lane, HI)
                tile0 = isinstance(t, int) and t == 0
                before = 0 if tile0 else scalar_steps
                chain = Chain(dve, dve_chain, 0 if tile0 else (t - 1) * links[1] + links[0])
                dve.wait_ge(searched, searches(t, scalar_steps + 1))
                for k in range(before, all_steps):
                    old, new = (CUT, CUT2) if (k - before) % 2 == 0 else (CUT2, CUT)
                    if k == all_steps - 2:
                        split_low(t, 0)
                        split_low(t, 1)
                    halve(chain, e, of(lane, old), of(lane, new), hi, target, keep, halving(k + 1))
                split_low(t, 2)
                if exists(t, 2):
                    row_max(t + 2, (lane + 2) % 3)
                split_low(t, 3)
                wait(dve, added, t)
                chain.wait()
                chain.count(dve.scalar_tensor_tensor(spare, e, hi, e, ALU.is_le, ALU.mult, accum_out=below))
                chain.wait()
                chain.count(dve.tensor_tensor(s_hi, of(lane, TOTAL), below, ALU.subtract))
                chain.count(dve.max(top8, spare))
                chain.wait()
                chain.link(dve.tensor_tensor_scan(sums8, ones8, top8, s_hi, ALU.mult, ALU.add))
                chain.link(dve.scalar_tensor_tensor(cross8, sums8, target, top8, ALU.is_ge, ALU.mult))
                chain.link(dve.tensor_reduce(w, cross8, AXIS.X, ALU.max))
                chain.link(dve.tensor_tensor(w, w, top8[:, 7:8], ALU.max))
                chain.link(dve.scalar_tensor_tensor(cross8, top8, w, top8, ALU.is_gt, ALU.mult, accum_out=above8))
                chain.count(dve.tensor_tensor(s_above, s_hi, above8, ALU.add))
                chain.link(dve.scalar_tensor_tensor(spare, e, w, e, ALU.is_ge, ALU.mult, accum_out=sl))
                chain.count(dve.tensor_scalar(flag, target, 1.0 - 2e-6, None, ALU.mult))
                chain.count(dve.tensor_tensor(reached, sl, sums8[:, 7:8], ALU.max))
                share(chain, lane, 0)
                chain.wait()
                chain.count(dve.tensor_tensor(flags[:, 0:1], reached, flag, ALU.is_lt))
                share(chain, lane, 1)
                chain.wait()
                chain.count(dve.transpose(flags_t, flags))
                share(chain, lane, 2)
                chain.wait()
                chain.count(dve.tensor_reduce(worst, flags_t, AXIS.X, ALU.max))
                share(chain, lane, 3)
                chain.wait()
                for k in range(4):
                    chain.count(dve.tensor_scalar(quarter[0:1, k:k + 1], worst[32 * k:32 * k + 1, :], 1.0, None, ALU.mult))
                share(chain, lane, 4)
                chain.wait()
                chain.count(dve.tensor_reduce(verdict, quarter[0:1, :], AXIS.X, ALU.max))
                share(chain, lane, 5)
                chain.wait()
                share(chain, lane, 6)
                missing = dve.value_load(verdict, min_val=0, max_val=1)
                for step in range(7, SHARE_STEPS):
                    chain.wait()
                    share(chain, lane, step)
                with dve.If(missing > 0):
                    chain.wait()
                    narrow(t, lane, e, target, hi)
                with dve.Else():
                    dve.sem_inc(fallback, narrow_links)
                chain.wait()
                dve.wait_ge(fallback, t * narrow_links + narrow_links)
                dve.tensor_scalar(e, spare, w, corr, ALU.is_equal, ALU.mult).then_inc(cut_done, 1)
                if not links[not tile0]:
                    links[not tile0] = chain.n
                assert links[not tile0] == chain.n

            def share(chain, lane, step):
                target, round_up = of(lane, TARGET), 1.5 * 2 ** 23
                if step == 0:
                    chain.count(dve.reciprocal(w_inv, w))
                    chain.count(dve.tensor_tensor(count, sl, s_above, ALU.subtract))
                elif step == 1:
                    chain.count(dve.tensor_scalar(count, count, w_inv, round_up, ALU.mult, ALU.add))
                elif step == 2:
                    chain.count(dve.tensor_scalar(count, count, -round_up, 1.0, ALU.add, ALU.max))
                elif step == 3:
                    chain.count(dve.tensor_scalar(neg_above, count, w, sl, ALU.mult, ALU.subtract))
                    chain.count(dve.reciprocal(frac, count))
                elif step == 4:
                    chain.count(dve.tensor_tensor(kept, target, neg_above, ALU.add))
                elif step == 5:
                    chain.count(dve.tensor_scalar(kept, kept, w_inv, 0.4999, ALU.mult, ALU.add))
                elif step == 6:
                    chain.count(dve.tensor_scalar(kept, kept, round_up, None, ALU.add))
                elif step == 7:
                    chain.count(dve.tensor_scalar(kept, kept, -round_up, 1.0, ALU.add, ALU.max))
                elif step == 8:
                    chain.count(dve.tensor_tensor(kept, kept, count, ALU.min))
                elif step == 9:
                    chain.count(dve.tensor_scalar(norm, kept, w, neg_above, ALU.mult, ALU.subtract))
                    if first_step:
                        chain.wait()
                        chain.count(dve.tensor_scalar(norm, norm, AT_SCALE, None, ALU.mult))
                    chain.count(dve.tensor_tensor(frac, kept, frac, ALU.mult))
                elif step == 10:
                    chain.count(dve.reciprocal(of(lane, INV_NORM), norm))
                    chain.count(dve.tensor_scalar(corr, frac, -1.0, w, ALU.add, ALU.mult))

            def narrow(t, lane, e, target, hi):
                chain = Chain(dve, fallback, t * narrow_links)
                chain.count(dve.tensor_scalar(w, hi, 0.0, None, ALU.add))
                with dve.Fori(0, STEPS - all_steps) as k:
                    inner = Chain(dve, fallback, t * narrow_links + (k * 4 + 1))
                    inner.wait()
                    inner.link(dve.tensor_scalar(corr, w, column(ratios, k + all_steps), None, ALU.mult))
                    inner.link(dve.scalar_tensor_tensor(junk_dve, e, corr, e, ALU.is_gt, ALU.mult, accum_out=below))
                    inner.link(dve.tensor_scalar(keep, below, target, w, ALU.is_ge, ALU.mult))
                    inner.count(dve.tensor_scalar(w, keep, corr, None, ALU.max))
                    assert inner.n == 4
                chain.n += 4 * (STEPS - all_steps)
                chain.wait()
                chain.link(dve.tensor_scalar(corr, w, math.exp(-SEARCH / 2 ** STEPS - 6e-7), None, ALU.mult))
                chain.link(dve.tensor_scalar(spare, e, corr, None, ALU.is_gt))
                chain.link(dve.scalar_tensor_tensor(spare, e, w, spare, ALU.is_le, ALU.mult))
                chain.link(dve.scalar_tensor_tensor(e, spare, w, e, ALU.mult, ALU.max))
                chain.link(dve.scalar_tensor_tensor(junk_dve, e, w, e, ALU.is_gt, ALU.mult, accum_out=s_above))
                chain.link(dve.scalar_tensor_tensor(spare, e, w, e, ALU.is_ge, ALU.mult, accum_out=sl))
                for step in range(SHARE_STEPS):
                    share(chain, lane, step)
                    if step + 1 < SHARE_STEPS:
                        chain.wait()
                assert chain.n == narrow_links

            def turn(t, lane, loads):
                if isinstance(t, int) and t == -1:
                    for k in range(STEPS):
                        dve.memset(ratios[:, k:k + 1], halving(k))
                    dve.memset(half, 0.5)
                    dve.memset(nodes, float(N))
                    dve.memset(p_top, P_TOP)
                    last = dve.memset(minus_one, -1.0)
                    last.then_inc(ready, 1)
                    dve.memset(flags, 0.0).then_inc(ready, 1)
                    dve.wait_ge(ready, 2)
                    row_max(0, 0)
                    row_max(1, 1)
                elif exists(t, 0):
                    refine(t, lane)
                else:
                    for g in range(4):
                        split_low(t, g)
            turns(dve, turn)

        @block.scalar
        def _(act):
            act.activation(xt[:, 0:1], m.minus_half[:, :], ACT.Exp)

            def load_q(t, lane):
                act.dma_start(q_ring[lo:hi_part, lane, :], queries_of(q_in, t)).then_inc(q_landed[lane], 16)
            load_q(0, 0)
            load_q(1, 1)

            def turn(t, lane, loads):
                nxt = (lane + 1) % 3
                if exists(t, 2) and exists(t, 0):
                    wait(act, logits, t)
                    load_q(t + 2, (lane + 2) % 3)

                def halve(k, which=(0, 1)):
                    if not exists(t, 1) or k >= scalar_steps or isinstance(t, int) and t == -1:
                        return
                    if 0 in which:
                        act.wait_ge(searched, searches(t + 1, k + 1))
                        act.activation(junk_act, probs[nxt], ACT.Sign, bias=of(nxt, NEG_CUT), accum_out=of(nxt, SIGNS)).then_inc(half_passed, 1)
                    if 1 in which:
                        act.wait_ge(half_passed, passes(t + 1, k + 1))
                        act.activation(junk_act, probs[nxt], ACT.Relu, bias=of(nxt, NEG_CUT), accum_out=of(nxt, RELUS)).then_inc(passed, 1)

                if exists(t, 1):
                    act.wait_ge(maxed, t + 2)
                    wait(act, a_turned, (t - 1) * 4)
                    act.activation(probs[nxt], ps_logits, ACT.Exp, bias=of(nxt, NEG_MAX), accum_out=of(nxt, TOTAL)).then_inc(exp_done, 1)
                halve(0)
                if not exists(t, -1):
                    for k in range(1, scalar_steps):
                        halve(k)
                    return
                before = (lane - 1) % 3

                def keep_at(g):
                    act.wait_ge(a_turned, (t - 1) * 4 + (g + 1))
                    if g == 3:
                        act.wait_ge(product, (t - 1) * 4 + 1)
                    if first_step:
                        act.activation(at_halves[:, g % 3, 0, :], ps_t[g % 2], ACT.Copy, scale=AT_SCALE).then_inc(at_kept, 1)
                    else:
                        act.activation(at[:, g % 3, :], ps_t[g % 2], ACT.Copy).then_inc(at_kept, 1)
                keep_at(0)
                keep_at(1)
                act.wait_ge(spread, t)
                if first_step:
                    wait(act, xa_stored, (t - 1) * 16)
                act.activation(xt, ps_x, ACT.Copy, scale=column(m.inv_degree[:, :], t - 1)).then_inc(xf_kept, 1)
                if first_step:
                    act.wait_ge(xf_kept, t)
                    wait(act, xf_stored, (t - 1) * 16)
                    act.activation(halves[:, 0, :], xt, ACT.Copy).then_inc(high_done, 1)
                halve(1, (0,))
                keep_at(2)
                halve(1, (1,))
                keep_at(3)
                halve(2)
                act.wait_ge(xt_turned, t * 2 - 1)
                act.activation(x_t, ps_t[0], ACT.Copy).then_inc(xt_kept, 1)
                for k in range(3, scalar_steps - 1):
                    halve(k)
                act.wait_ge(product, (t - 1) * 4 + 4)
                if first_step:
                    act.wait_ge(low_done, t)
                act.activation(xt, ps_x, ACT.Copy, scale=of(before, INV_NORM)).then_inc(xa_kept, 1)
                act.wait_ge(xt_turned, t * 2)
                act.activation(x_t2, ps_t[1], ACT.Copy).then_inc(xt_kept, 1)
                halve(scalar_steps - 1, (0,))
                if first_step:
                    act.wait_ge(qk_done, t)
                    act.activation(next_keys[:, tile_rows(t - 1)], ps_t[0][64:P, 0:P], ACT.Copy).then_inc(qk_kept, 1)
                    wait(act, q_stored, (t - 1) * 16)
                    act.activation(q_stage, ps_t[0][0:64, 0:P], ACT.Copy).then_inc(qk_kept, 1)
                act.wait_ge(u_used, t * 2)
                wait(act, y_stored, (t - 1) * 16)
                act.activation(zt, ps_z, ACT.Copy).then_inc(z_kept, 1)
                halve(scalar_steps - 1, (1,))
            turns(act, turn)

        @block.tensor
        def _(pe):
            def make_logits(t, lane, loads):
                pe.wait_ge(q_landed[lane], loads * 16)
                wait(pe, exp_done, t)
                for c in range(4):
                    last = pe.matmul(ps_logits[:, c * BANK:(c + 1) * BANK], q_ring[lo:hi_part, lane, :],
                                     keys[:, c * BANK:(c + 1) * BANK], start=True, stop=True)
                last.then_inc(logits, 1)

            def turn(t, lane, loads):
                if isinstance(t, int) and t == -1:
                    make_logits(0, 0, 1)
                    make_logits(1, 1, 1)
                    return
                if isinstance(t, int) and t == 0:
                    if not first_step:
                        pe.wait_ge(xa_in, 16)
                        pe.wait_ge(xf_in, 16)
                    make_logits(2, 2, 1)
                    pe.wait_ge(u_in, 32)
                    return
                weights = probs[(lane - 1) % 3]

                def turn_a(g):
                    if g >= 2:
                        pe.wait_ge(at_ready, (t - 1) * 4 + (g - 1))
                    for j in range(4):
                        block_of = slice((4 * g + j) * P, (4 * g + j + 1) * P)
                        last = pe.transpose(ps_t[g % 2][:, j * P:(j + 1) * P], weights[:, block_of], m.eye[:, :])
                    last.then_inc(a_turned, 1)

                def multiply(g):
                    pe.wait_ge(at_ready, (t - 1) * 4 + (g + 1))
                    for j in range(4):
                        first, final = g == 0 and j == 0, g == 3 and j == 3
                        if first_step:
                            for a, b in ((0, 0), (0, 1), (1, 0)):
                                last = pe.matmul(ps_x, at_halves[:, g % 3, a, j * P:(j + 1) * P], xf[:, 4 * g + j, b, :],
                                                 start=first and a == b, stop=final and a == 1)
                        else:
                            last = pe.matmul(ps_x, at[:, g % 3, j * P:(j + 1) * P], xa[:, 4 * g + j, :],
                                             start=first, stop=final)
                    last.then_inc(product, 1)

                wait(pe, xa_kept, t - 1)
                for j in range(NT):
                    for k in range(2):
                        pe.matmul(ps_x, m.adj_t[:, j, tile_rows(t - 1)], xf[:, j, k, :], start=j == 0 and k == 0, stop=False)
                pe.matmul(ps_x, m.eye16[:, :], xf[:, t - 1, 0, :], start=False, stop=False)
                if exists(t, 2):
                    make_logits(t + 2, (lane + 2) % 3, loads)
                pe.wait_ge(added, t)
                wait(pe, xt_kept, (t - 1) * 2)
                if first_step:
                    wait(pe, qk_kept, (t - 1) * 2)
                turn_a(0)
                turn_a(1)
                pe.matmul(ps_x, m.eye16[:, :], xf[:, t - 1, 1, :], start=False, stop=True).then_inc(spread, 1)
                turn_a(2)
                pe.wait_ge(xf_kept, t)
                multiply(0)
                turn_a(3)
                multiply(1)
                pe.wait_ge(at_ready, (t - 1) * 4 + 3)
                for k in range(KT):
                    last = pe.transpose(ps_t[0][:, k * P:(k + 1) * P], xt[:, k * P:(k + 1) * P], m.eye[:, :])
                last.then_inc(xt_turned, 1)
                multiply(2)
                multiply(3)
                pe.wait_ge(xt_kept, t * 2 - 1)
                wait(pe, z_kept, t - 1)
                for k in range(KT):
                    last = pe.matmul(ps_z, x_t[:, k * P:(k + 1) * P], u1_sb[:, k, :], start=k == 0, stop=False)
                last.then_inc(u_used, 1)
                pe.wait_ge(xa_kept, t)
                for k in range(KT):
                    last = pe.transpose(ps_t[1][:, k * P:(k + 1) * P], xt[:, k * P:(k + 1) * P], m.eye[:, :])
                last.then_inc(xt_turned, 1)
                pe.wait_ge(xt_kept, t * 2)
                if first_step:
                    for k in range(KT):
                        last = pe.matmul(ps_t[0][:, 0:P], m.qk_weight[:, k, :], x_t2[:, k * P:(k + 1) * P], start=k == 0, stop=k == KT - 1)
                    last.then_inc(qk_done, 1)
                for k in range(KT):
                    last = pe.matmul(ps_z, x_t2[:, k * P:(k + 1) * P], u2_sb[:, k, :], start=False, stop=k == KT - 1)
                last.then_inc(u_used, 1)
            turns(pe, turn)


def close_diffusion(nc, m, y_rows, x1_rows, x2_rows, gamma, beta):
    y, x = m.f32(64, NT, D), m.f32(96, NT, D)
    gamma_sb, beta_sb = m.f32(192, D), m.f32(194, D)
    step = m.norm
    with ExitStack() as ctx:
        def sem(name):
            return ctx.enter_context(nc.semaphore("F_" + name))

        y_in, x_in, g_in, stats_done = [sem(f"y_in{c}") for c in range(4)], sem("x_in"), sem("g_in"), sem("stats_done")
        block = ctx.enter_context(nc.Block())

        @block.sync
        def _(sp):
            for c in range(4):
                sp.dma_start(y[:, 4 * c:4 * c + 4, :], rows(y_rows)[:, 4 * c:4 * c + 4, :]).then_inc(y_in[c], 16)
            sp.dma_start(x, rows(x1_rows)).then_inc(x_in, 16)
            sp.dma_start(gamma_sb, on_all(gamma)).then_inc(g_in, 16)
            sp.dma_start(beta_sb, on_all(beta)).then_inc(g_in, 16)
            sp.wait_ge(x_in, 16)
            sp.wait_ge(g_in, 32)

        @block.vector
        def _(dve):
            measure_chunks(dve, y, y_in, m.stats, stats_done)
    norm_constants(nc, m, "F1")
    with ExitStack() as ctx:
        def sem(name):
            return ctx.enter_context(nc.semaphore("G_" + name))

        centred, scaled, shifted, x_done, stats_done, x_stored = (sem("centred"), sem("scaled"), sem("shifted"), sem("x_done"),
                                                                  sem("stats_done"), sem("x_stored"))
        block = ctx.enter_context(nc.Block())

        @block.scalar
        def _(act):
            act.activation(m.scratch[:, 0:1], m.minus_half[:, :], ACT.Identity)
            def turn(t):
                act.activation(y[:, t, :], y[:, t, :], ACT.Identity, scale=column(step[:, 4, :], t),
                               bias=column(step[:, 5, :], t)).then_inc(centred, 1)
            repeat(act, NT, turn)

        @block.gpsimd
        def _(pool):
            def turn(t):
                pool.tensor_tensor(x[:, t, :], x[:, t, :], beta_sb, ALU.add).then_inc(shifted, 1)
            repeat(pool, NT, turn)

        @block.vector
        def _(dve):
            def scale(t):
                dve.wait_ge(centred, t + 1)
                dve.tensor_tensor(y[:, t, :], y[:, t, :], gamma_sb, ALU.mult).then_inc(scaled, 1)

            def add(t):
                dve.wait_ge(scaled, t + 1)
                dve.wait_ge(shifted, t + 1)
                dve.tensor_tensor(x[:, t, :], x[:, t, :], y[:, t, :], ALU.add).then_inc(x_done, 1)

            def measure(t):
                dve.wait_ge(x_done, t + 1)
                dve.bn_stats(m.stats[:, t, :], x[:, t, :]).then_inc(stats_done, 1)
            scale(0)
            scale(1)
            add(0)
            with dve.Fori(2, NT) as t:
                scale(t)
                add(t - 1)
                measure(t - 2)
            add(NT - 1)
            measure(NT - 2)
            measure(NT - 1)

        @block.sync
        def _(sp):
            def turn(c):
                sp.wait_ge(x_done, c * 4 + 4)
                sp.dma_start(rows(x2_rows)[:, bass.ts(c, 4), :], x[:, bass.ts(c, 4), :]).then_inc(x_stored, 16)
            repeat(sp, 4, turn)
            sp.wait_ge(x_stored, 64)
    norm_constants(nc, m, "F2", m.inv_sqrt_degree[:, :])
    normed_halves(nc, m, "F3", x)


def normed_halves(nc, m, name, x):
    halves, ring = m.f16(128, NT, 2, D), m.f32(192, 2, D)
    step = m.norm
    with ExitStack() as ctx:
        full, high, low = (ctx.enter_context(nc.semaphore(name + s)) for s in ("_full", "_high", "_low"))
        block = ctx.enter_context(nc.Block())

        @block.scalar
        def _(act):
            act.activation(m.scratch[:, 0:1], m.minus_half[:, :], ACT.Relu)

            def tile(t, lane, group):
                scale, shift = column(step[:, 4, :], t), column(step[:, 5, :], t)
                wait(act, low, t - 1)
                act.activation(ring[:, lane, :], x[:, t, :], ACT.Relu, scale=scale, bias=shift).then_inc(full, 1)
                act.activation(halves[:, t, 0, :], x[:, t, :], ACT.Relu, scale=scale, bias=shift).then_inc(high, 1)
            walk(act, tile, 2)

        @block.vector
        def _(dve):
            def tile(t, lane, group):
                dve.wait_ge(full, t + 1)
                dve.wait_ge(high, t + 1)
                dve.tensor_tensor(halves[:, t, 1, :], ring[:, lane, :], halves[:, t, 0, :], ALU.subtract).then_inc(low, 1)
            walk(dve, tile, 2)


def symmetrise_and_spread(nc, m, adj):
    mean, source = m.f16(64, NT, N), m.f16(128, NT, 2, D)
    adj_in, spread = m.f32(160, 4, N), m.f16(160, NT, 2, D)
    ring = m.f32(192, 2, D)
    banks = 8
    with ExitStack() as ctx:
        def sem(name):
            return ctx.enter_context(nc.semaphore("H_" + name))

        landed = [sem(f"landed{k}") for k in range(4)]
        added, halved, summed, kept, high, low = (sem("added"), sem("halved"), sem("summed"), sem("kept"), sem("high"), sem("low"))
        block = ctx.enter_context(nc.Block())

        @block.sync
        def _(sp):
            def tile(t, lane, group):
                wait(sp, added, t - 3)
                sp.dma_start(adj_in[:, lane, :], adj[bass.ts(t, P), :]).then_inc(landed[lane], 16)
            walk(sp, tile, 4)

        @block.tensor
        def _(pe):
            def start(t, bank):
                for k in range(2):
                    pe.matmul(m.bank(bank), m.eye16[:, :], source[:, t, k, :], start=k == 0, stop=False)

            for t in range(banks):
                start(t, t)

            def take(j):
                pe.wait_ge(halved, j + 1)
                for t in range(banks):
                    for k in range(2):
                        last = pe.matmul(m.bank(t), mean[:, j, t * P:(t + 1) * P], source[:, j, k, :], start=False,
                                         stop=isinstance(j, int) and j == NT - 1 and k == 1)
                    if isinstance(j, int) and j == NT - 1:
                        last.then_inc(summed, 1)
            with pe.Fori(0, NT - 1) as j:
                take(j)
            take(NT - 1)

            def whole(t, bank, kept_before):
                pe.wait_ge(kept, kept_before)
                start(t, bank)
                for j in range(NT):
                    for k in range(2):
                        last = pe.matmul(m.bank(bank), mean[:, j, bass.ts(t, P)], source[:, j, k, :], start=False,
                                         stop=j == NT - 1 and k == 1)
                last.then_inc(summed, 1)
            for lane in range(2):
                whole(banks + lane, lane, lane + 1)
            with pe.Fori(banks // 2 + 1, NT // 2) as i:
                for lane in range(2):
                    whole(i * 2 + lane, lane, i * 2 + (lane - 1))

        @block.scalar
        def _(act):
            act.activation(m.scratch[:, 0:1], m.minus_half[:, :], ACT.Copy)

            def halve(t):
                act.wait_ge(added, t + 1)
                act.activation(mean[:, t, :], mean[:, t, :], ACT.Copy, scale=0.5).then_inc(halved, 1)
            repeat(act, NT, halve)

            def keep(t, lane, bank):
                wait(act, low, t - 1)
                act.wait_ge(summed, t + 1)
                act.activation(ring[:, lane, :], m.bank(bank), ACT.Copy, scale=column(m.inv_sqrt_degree[:, :], t)).then_inc(kept, 1)
                act.wait_ge(kept, t + 1)
                act.activation(spread[:, t, 0, :], ring[:, lane, :], ACT.Copy).then_inc(high, 1)
            for t in range(banks):
                keep(t, t % 2, t)
            with act.Fori(banks // 2, NT // 2) as i:
                for lane in range(2):
                    keep(i * 2 + lane, lane, lane)

        @block.vector
        def _(dve):
            def add(t, lane, group):
                dve.wait_ge(landed[lane], (group + 1) * 16)
                dve.tensor_tensor(mean[:, t, :], adj_in[:, lane, :], m.adj_t[:, t, :], ALU.add).then_inc(added, 1)
            walk(dve, add, 4)

            def low_half(t, lane, group):
                dve.wait_ge(high, t + 1)
                dve.tensor_tensor(spread[:, t, 1, :], ring[:, lane, :], spread[:, t, 0, :], ALU.subtract).then_inc(low, 1)
            walk(dve, low_half, 2)


def propagate(nc, m, x2_rows, c_weight, c_bias):
    spread = m.f16(160, NT, 2, D)
    x = m.f32(64, NT, D)
    with ExitStack() as ctx:
        x_in, w_in, summed, x_done, stats_done = (ctx.enter_context(nc.semaphore("J_" + s))
                                                  for s in ("x_in", "w_in", "summed", "x_done", "stats_done"))
        block = ctx.enter_context(nc.Block())

        @block.sync
        def _(sp):
            sp.dma_start(x, rows(x2_rows)).then_inc(x_in, 16)
            sp.wait_ge(x_in, 16)
            w_sb, bias_sb = convolve_constants(m)
            sp.dma_start(w_sb, c_weight.rearrange("(k p) n -> p k n", p=P)).then_inc(w_in, 16)
            sp.dma_start(bias_sb, on_all(c_bias)).then_inc(w_in, 16)
            sp.wait_ge(w_in, 32)

        @block.tensor
        def _(pe):
            def tile(t, lane, group):
                wait(pe, x_done, t - 1)
                for j in range(NT):
                    for k in range(2):
                        last = pe.matmul(m.bank(lane), m.adj_t[:, j, bass.ts(t, P)], spread[:, j, k, :],
                                         start=j == 0 and k == 0, stop=j == NT - 1 and k == 1)
                last.then_inc(summed, 1)
            walk(pe, tile, 2)

        @block.vector
        def _(dve):
            dve.wait_ge(x_in, 16)

            def tile(t, lane, group):
                dve.wait_ge(summed, t + 1)
                dve.tensor_tensor(x[:, t, :], x[:, t, :], m.bank(lane), ALU.add).then_inc(x_done, 1)
                dve.wait_ge(x_done, t + 1)
                dve.bn_stats(m.stats[:, t, :], x[:, t, :]).then_inc(stats_done, 1)
            walk(dve, tile, 2)
    norm_constants(nc, m, "K1")
    normed_halves(nc, m, "K2", x)


def convolve_constants(m):
    return m.f32(96, KT, D), m.f32(104, D)


def convolve(nc, m, out):
    x, source = m.f32(64, NT, D), m.f16(128, NT, 2, D)
    w_sb, bias_sb = convolve_constants(m)
    sums, sums_t, result = m.f32(106, 2, D), m.f32(110, 2, D), m.f32(114, 2, D)
    with ExitStack() as ctx:
        def sem(name):
            return ctx.enter_context(nc.semaphore("L_" + name))

        summed, sums_kept, turned, turned_kept = sem("summed"), sem("sums_kept"), sem("turned"), sem("turned_kept")
        multiplied, biased, result_done, stored = sem("multiplied"), sem("biased"), sem("result_done"), [sem(f"stored{k}") for k in range(2)]
        block = ctx.enter_context(nc.Block())

        @block.sync
        def _(sp):
            def tile(t, lane, group):
                sp.wait_ge(result_done, t + 1)
                sp.dma_start(out[bass.ts(t, P), :], result[:, lane, :]).then_inc(stored[lane], 16)
            walk(sp, tile, 2)
            for lane in range(2):
                sp.wait_ge(stored[lane], NT // 2 * 16)

        @block.gpsimd
        def _(pool):
            def turn(t):
                pool.tensor_tensor(x[:, t, :], x[:, t, :], bias_sb, ALU.add).then_inc(biased, 1)
            repeat(pool, NT, turn)

        @block.tensor
        def _(pe):
            def gather(t, lane):
                wait(pe, sums_kept, t - 1)
                for j in range(NT):
                    for k in range(2):
                        last = pe.matmul(m.bank(lane), m.adj_t[:, j, bass.ts(t, P)], source[:, j, k, :],
                                         start=j == 0 and k == 0, stop=j == NT - 1 and k == 1)
                last.then_inc(summed, 1)

            def turn(t, lane):
                pe.wait_ge(sums_kept, t + 1)
                wait(pe, turned_kept, t - 1)
                for k in range(KT):
                    last = pe.transpose(m.bank(2 + lane)[:, k * P:(k + 1) * P], sums[:, lane, k * P:(k + 1) * P], m.eye[:, :])
                last.then_inc(turned, 1)

            def project_sums(t, lane):
                pe.wait_ge(turned_kept, t + 1)
                wait(pe, result_done, t - 1)
                for k in range(KT):
                    last = pe.matmul(m.bank(4 + lane), sums_t[:, lane, k * P:(k + 1) * P], w_sb[:, k, :], start=k == 0, stop=k == KT - 1)
                last.then_inc(multiplied, 1)

            gather(0, 0)
            gather(1, 1)
            turn(0, 0)
            gather(2, 0)
            turn(1, 1)
            project_sums(0, 0)
            gather(3, 1)
            turn(2, 0)
            project_sums(1, 1)
            with pe.Fori(2, NT // 2) as i:
                for lane in range(2):
                    gather(i * 2 + lane, lane)
                    turn(i * 2 + (lane - 1), 1 - lane)
                    project_sums(i * 2 + (lane - 2), lane)
            turn(NT - 1, 1)
            project_sums(NT - 2, 0)
            project_sums(NT - 1, 1)

        @block.scalar
        def _(act):
            act.activation(m.scratch[:, 0:1], m.minus_half[:, :], ACT.Copy)

            def tile(t, lane, group):
                act.wait_ge(summed, t + 1)
                wait(act, turned, t - 1)
                act.activation(sums[:, lane, :], m.bank(lane), ACT.Copy).then_inc(sums_kept, 1)
            walk(act, tile, 2)

        @block.vector
        def _(dve):
            def tile(t, lane, group):
                dve.wait_ge(turned, t + 1)
                wait(dve, multiplied, t - 1)
                dve.tensor_scalar(sums_t[:, lane, :], m.bank(2 + lane), 0.0, None, ALU.add).then_inc(turned_kept, 1)
                dve.wait_ge(multiplied, t + 1)
                dve.wait_ge(biased, t + 1)
                wait(dve, stored[lane], group * 16)
                dve.tensor_tensor(result[:, lane, :], m.bank(4 + lane), x[:, t, :], ALU.add).then_inc(result_done, 1)
            walk(dve, tile, 2)


def d_at(columns_of, t, head):
    if isinstance(t, int):
        return columns_of[:, t, head:head + 1]
    return columns_of[:, bass.ds(t, 1), head:head + 1].rearrange("p a h -> p (a h)")


def clear_counts(nc, free):
    with nc.Block() as block:
        @block.gpsimd
        def _(pool):
            pool.sem_clear(range(min(free), max(free) + 1))


def program(nc, x, adj, adj_t, g_w, g_a1, g_a2, g_w1, g_b1, g_w2, g_b2, g_w3, g_b3, g_w4, g_b4,
            t_w1, t_w2, t_w3, u1_0, u1_1, u2_0, u2_1, gamma, beta, c_w, c_b, out):
    with ExitStack() as ctx:
        m = Memory(nc, ctx)
        free = list(nc.free_semaphores)
        constants(nc, m)
        def spill(name, *shape, dt=F32):
            return nc.dram_tensor(name, shape, dt, kind="Internal").ap()

        u_rows, x1_rows, x2_rows = spill("u_rows", H, N), spill("x1_rows", N, D), spill("x2_rows", N, D)
        y1_rows, y2_rows, xa_rows = spill("y1_rows", N, D), spill("y2_rows", N, D), spill("xa_rows", N, D)
        xf_rows = spill("xf_rows", N, 2, D, dt=F16)
        q0_rows, q1_rows = spill("q0_rows", N, D), spill("q1_rows", N, D)
        project(nc, m, x, adj_t, g_w, g_a1, g_a2, u_rows)
        attend(nc, m, u_rows, g_w1, g_w2, g_w3)
        dense(nc, m, x, g_b1, g_b2, g_b3, g_w4, g_b4, x1_rows)
        norm_constants(nc, m, "D0")
        queries(nc, m, t_w1, t_w2, t_w3, q0_rows)
        clear_counts(nc, free)
        diffuse(nc, m, 0, u1_0, u2_0, q0_rows, q1_rows, xa_rows, xf_rows, None, y1_rows)
        diffuse(nc, m, 1, u1_1, u2_1, q1_rows, None, xa_rows, xf_rows, y1_rows, y2_rows)
        close_diffusion(nc, m, y2_rows, x1_rows, x2_rows, gamma, beta)
        symmetrise_and_spread(nc, m, adj)
        propagate(nc, m, x2_rows, c_w, c_b)
        convolve(nc, m, out)


def kernel(x, adj, L0_gnn_W, L0_gnn_a1, L0_gnn_a2, L0_gnn_W1, L0_gnn_b1, L0_gnn_W2, L0_gnn_b2, L0_gnn_W3, L0_gnn_b3,
           L0_gnn_W4, L0_gnn_b4, L1_gnn_W1, L1_gnn_W2, L1_gnn_W3, L1_gnn_U1_0, L1_gnn_U1_1, L1_gnn_U2_0, L1_gnn_U2_1,
           L1_gnn_gamma, L1_gnn_beta, L3_gnn_weight, L3_gnn_bias):
    import concourse.bacc as bacc
    from concourse.bass_utils import run_bass_kernel_spmd

    laid_out = {
        "x": x, "adj": adj, "adj_t": adj.T, "g_w": L0_gnn_W.transpose(1, 0, 2).reshape(D, D),
        "g_a1": L0_gnn_a1.reshape(-1), "g_a2": L0_gnn_a2.reshape(-1),
        "g_w1": L0_gnn_W1.T, "g_b1": L0_gnn_b1, "g_w2": L0_gnn_W2.T, "g_b2": L0_gnn_b2,
        "g_w3": L0_gnn_W3.T, "g_b3": L0_gnn_b3, "g_w4": L0_gnn_W4.T, "g_b4": L0_gnn_b4,
        "t_w1": L1_gnn_W1.T, "t_w2": L1_gnn_W2, "t_w3": L1_gnn_W3, "u1_0": L1_gnn_U1_0, "u1_1": L1_gnn_U1_1,
        "u2_0": L1_gnn_U2_0, "u2_1": L1_gnn_U2_1, "gamma": L1_gnn_gamma, "beta": L1_gnn_beta,
        "c_w": L3_gnn_weight, "c_b": L3_gnn_bias,
    }
    nc = bacc.Bacc("TRN2", target_bir_lowering=False, num_devices=1)
    arrays, args = {}, []
    for name, a in laid_out.items():
        a = np.ascontiguousarray(a)
        arrays["in_" + name] = a
        args.append(nc.dram_tensor("in_" + name, a.shape, mybir.dt.from_np(a.dtype), kind="ExternalInput").ap())
    out = nc.dram_tensor("out", (N, D), F32, kind="ExternalOutput").ap()
    program(nc, *args, out)
    result = run_bass_kernel_spmd(nc, [arrays], core_ids=[0])
    return result.results[0]["out"]
```
